# Optimizing a Trainium2 kernel written in Bass

```python
import numpy as np
import jax
import jax.numpy as jnp

def _softmax(x, axis=-1):
    return jax.nn.softmax(x, axis=axis)

def _gelu(x):
    return jax.nn.gelu(x, approximate=True)

def _silu(x):
    return jax.nn.silu(x)

def _sigmoid(x):
    return jax.nn.sigmoid(x)

def _layernorm(x, axis=-1, eps=1e-05):
    m = jnp.mean(x, axis=axis, keepdims=True)
    v = jnp.var(x, axis=axis, keepdims=True)
    return (x - m) / jnp.sqrt(v + eps)

def _scatter_add(tgt, idx, src, axis=0):
    return tgt.at[idx].add(src)

def _segment_sum(src, seg, n):
    return jax.ops.segment_sum(src, seg, n)
kernel_name = 'mk_flamingo_gated_d2_seqx_r4_0fda9f'

def setup_inputs(seed: int=0):
    np.random.seed(seed)
    _w = jnp.asarray

    def _rec_inputs():
        import jax
        import jax.numpy as jnp
        _rk = jax.random.key(seed)
        x = 7.22e-05 + 1 * jax.random.normal(jax.random.fold_in(_rk, 1), (16, 256, 256), jnp.float32)
        _lenS = 256 - jax.random.randint(jax.random.fold_in(_rk, 7), (16,), 0, max(1, 256 // 4) + 1, jnp.int32)
        _lenS2 = 77 - jax.random.randint(jax.random.fold_in(_rk, 8), (16,), 0, max(1, 77 // 4) + 1, jnp.int32)
        _ctx_1024P = jax.random.normal(jax.random.fold_in(_rk, 11), (16, 16, 256), jnp.float32)
        _ctx_1024c = jax.random.dirichlet(jax.random.fold_in(_rk, 511), 0.3 * jnp.ones((16,), jnp.float32), (16, 77))
        _ctx_1024t = jnp.einsum('bsk,bkd->bsd', _ctx_1024c, _ctx_1024P)
        _ctx_1024t = _ctx_1024t * jax.lax.rsqrt(jnp.mean(jnp.square(_ctx_1024t)) + 1e-12) * 0.953939
        ctx_1024 = 4.13588e-05 + 0.999923 * (_ctx_1024t + 0.3 * jax.random.normal(jax.random.fold_in(_rk, 611), (16, 77, 256), jnp.float32))
        _validS = jnp.arange(256)[None, :] < _lenS[:, None]
        _validS2 = jnp.arange(77)[None, :] < _lenS2[:, None]
        _causal = jnp.tril(jnp.ones((256, 256), dtype=bool))
        mask_BxS2_bf0 = jnp.logical_not(jnp.ones((16, 77), dtype=bool))
        _g = jax.random.normal(jax.random.fold_in(_rk, 9001), (2, 2), jnp.float32)
        _g = jnp.sign(_g) * jnp.maximum(jnp.abs(_g), 1.0) + (_g == 0) * 1.0
        g_xattn = _g[0]
        g_ffn = _g[1]
        return (x, ctx_1024, mask_BxS2_bf0, g_xattn, g_ffn)
    x, ctx_1024, mask_BxS2_bf0, g_xattn, g_ffn = _rec_inputs()

    def _L0_xattn_setup():
        import jax, jax.numpy as jnp
        import numpy as np
        N_HEADS = 16
        DIM = 256
        HEAD_DIM = DIM // N_HEADS

        def _split_heads(t):
            B, S, _ = t.shape
            return t.reshape(B, S, N_HEADS, HEAD_DIM).transpose(0, 2, 1, 3)
        key = jax.random.key(seed)
        ks = jax.random.split(key, 12)
        B, S = (4, 512)
        scale = 1.0 / np.sqrt(DIM)
        inp = {'x': jax.random.normal(ks[0], (B, S, DIM), jnp.float32), 'memory': jax.random.normal(ks[1], (B, S, DIM), jnp.float32), 'mask': jnp.zeros((B, S), jnp.bool_), 'wq': jax.random.normal(ks[2], (DIM, DIM), jnp.float32) * scale, 'bq': jnp.zeros((DIM,), jnp.float32), 'wk': jax.random.normal(ks[3], (DIM, DIM), jnp.float32) * scale, 'bk': jnp.zeros((DIM,), jnp.float32), 'wv': jax.random.normal(ks[4], (DIM, DIM), jnp.float32) * scale, 'bv': jnp.zeros((DIM,), jnp.float32), 'wo': jax.random.normal(ks[5], (DIM, DIM), jnp.float32) * scale, 'bo': jnp.zeros((DIM,), jnp.float32)}
        return inp
    _L0_xattn_all = _L0_xattn_setup()
    _L0_xattn_in = {k: v for k, v in _L0_xattn_all.items() if k in ('wq', 'bq', 'wk', 'bk', 'wv', 'bv', 'wo', 'bo')}
    del _L0_xattn_all

    def _L0_ffn_setup():
        import jax, jax.numpy as jnp
        import numpy as np
        D = 256
        H = 256
        E = 8
        K = 2
        I = 2 * 256
        ROUTE_SCALE = 1.0
        key = jax.random.key(seed)
        ks = jax.random.split(key, 12)
        s = lambda *sh: 1.0 / np.sqrt(sh[-1])
        return {'x': jax.random.normal(ks[0], (1, 512, D), jnp.float32), 'gate_w': jax.random.normal(ks[1], (E, D), jnp.float32) * s(E, D), 'w1': jax.random.normal(ks[2], (E, H, D), jnp.float32) * s(H, D), 'b1': jax.random.normal(ks[3], (E, H), jnp.float32) * 0.01, 'w2': jax.random.normal(ks[4], (E, D, H), jnp.float32) * s(D, H), 'b2': jax.random.normal(ks[5], (E, D), jnp.float32) * 0.01, 'w3': jax.random.normal(ks[6], (E, H, D), jnp.float32) * s(H, D), 'b3': jax.random.normal(ks[7], (E, H), jnp.float32) * 0.01, 'sw1': jax.random.normal(ks[8], (I, D), jnp.float32) * s(I, D), 'sw2': jax.random.normal(ks[9], (I, D), jnp.float32) * s(I, D), 'sw3': jax.random.normal(ks[10], (D, I), jnp.float32) * s(D, I)}
    _L0_ffn_all = _L0_ffn_setup()
    _L0_ffn_in = {k: v for k, v in _L0_ffn_all.items() if k in ('gate_w', 'w1', 'b1', 'w2', 'b2', 'w3', 'b3', 'sw1', 'sw2', 'sw3')}
    del _L0_ffn_all

    def _L1_xattn_setup():
        import jax, jax.numpy as jnp
        import numpy as np
        EMBED = 256
        HEADS = 16
        HEAD_DIM = EMBED // HEADS
        key = jax.random.key(seed)
        ks = jax.random.split(key, 8)
        B, S = (2, 512)
        return {'values': jax.random.normal(ks[0], (B, S, EMBED), jnp.float32), 'keys': jax.random.normal(ks[1], (B, S, EMBED), jnp.float32), 'query': jax.random.normal(ks[2], (B, S, EMBED), jnp.float32), 'Wv': jax.random.normal(ks[3], (EMBED, EMBED), jnp.float32) * EMBED ** (-0.5), 'Wk': jax.random.normal(ks[4], (EMBED, EMBED), jnp.float32) * EMBED ** (-0.5), 'Wq': jax.random.normal(ks[5], (EMBED, EMBED), jnp.float32) * EMBED ** (-0.5), 'Wo': jax.random.normal(ks[6], (EMBED, EMBED), jnp.float32) * EMBED ** (-0.5), 'bo': jnp.zeros((EMBED,), jnp.float32)}
    _L1_xattn_all = _L1_xattn_setup()
    _L1_xattn_in = {k: v for k, v in _L1_xattn_all.items() if k in ('Wv', 'Wk', 'Wq', 'Wo', 'bo')}
    del _L1_xattn_all

    def _L1_ffn_setup():
        import jax, jax.numpy as jnp
        import numpy as np
        N_EXPERTS = 16
        TOPK = 2
        CAPACITY_FACTOR = 1.0
        EPS_GATE = 1e-06
        LN_EPS = 1e-05
        key = jax.random.key(seed)
        ks = jax.random.split(key, 8)
        B, S, D, F, E = (4, 512, 256, 1024, N_EXPERTS)
        Fp = F // E
        s = 0.02
        return {'x': jax.random.normal(ks[0], (B, S, D), dtype=jnp.float32), 'wg': s * jax.random.normal(ks[1], (D, E), dtype=jnp.float32), 'bg': jnp.zeros((E,), dtype=jnp.float32), 'w1': s * jax.random.normal(ks[2], (E, D, Fp), dtype=jnp.float32), 'b1': jnp.zeros((E, Fp), dtype=jnp.float32), 'w2': s * jax.random.normal(ks[3], (E, Fp, D), dtype=jnp.float32), 'b2': jnp.zeros((E, D), dtype=jnp.float32), 'gamma': jnp.ones((D,), dtype=jnp.float32), 'beta': jnp.zeros((D,), dtype=jnp.float32)}
    _L1_ffn_all = _L1_ffn_setup()
    _L1_ffn_in = {k: v for k, v in _L1_ffn_all.items() if k in ('wg', 'bg', 'w1', 'b1', 'w2', 'b2', 'gamma', 'beta')}
    del _L1_ffn_all
    return {'x': x, 'ctx_1024': ctx_1024, 'mask_BxS2_bf0': mask_BxS2_bf0, 'g_xattn': g_xattn, 'g_ffn': g_ffn, 'L0_xattn_wq': _L0_xattn_in['wq'], 'L0_xattn_bq': _L0_xattn_in['bq'], 'L0_xattn_wk': _L0_xattn_in['wk'], 'L0_xattn_bk': _L0_xattn_in['bk'], 'L0_xattn_wv': _L0_xattn_in['wv'], 'L0_xattn_bv': _L0_xattn_in['bv'], 'L0_xattn_wo': _L0_xattn_in['wo'], 'L0_xattn_bo': _L0_xattn_in['bo'], 'L0_ffn_gate_w': _L0_ffn_in['gate_w'], 'L0_ffn_w1': _L0_ffn_in['w1'], 'L0_ffn_b1': _L0_ffn_in['b1'], 'L0_ffn_w2': _L0_ffn_in['w2'], 'L0_ffn_b2': _L0_ffn_in['b2'], 'L0_ffn_w3': _L0_ffn_in['w3'], 'L0_ffn_b3': _L0_ffn_in['b3'], 'L0_ffn_sw1': _L0_ffn_in['sw1'], 'L0_ffn_sw2': _L0_ffn_in['sw2'], 'L0_ffn_sw3': _L0_ffn_in['sw3'], 'L1_xattn_Wv': _L1_xattn_in['Wv'], 'L1_xattn_Wk': _L1_xattn_in['Wk'], 'L1_xattn_Wq': _L1_xattn_in['Wq'], 'L1_xattn_Wo': _L1_xattn_in['Wo'], 'L1_xattn_bo': _L1_xattn_in['bo'], 'L1_ffn_wg': _L1_ffn_in['wg'], 'L1_ffn_bg': _L1_ffn_in['bg'], 'L1_ffn_w1': _L1_ffn_in['w1'], 'L1_ffn_b1': _L1_ffn_in['b1'], 'L1_ffn_w2': _L1_ffn_in['w2'], 'L1_ffn_b2': _L1_ffn_in['b2'], 'L1_ffn_gamma': _L1_ffn_in['gamma'], 'L1_ffn_beta': _L1_ffn_in['beta']}

def reference(x, ctx_1024, mask_BxS2_bf0, g_xattn, g_ffn, L0_xattn_wq, L0_xattn_bq, L0_xattn_wk, L0_xattn_bk, L0_xattn_wv, L0_xattn_bv, L0_xattn_wo, L0_xattn_bo, L0_ffn_gate_w, L0_ffn_w1, L0_ffn_b1, L0_ffn_w2, L0_ffn_b2, L0_ffn_w3, L0_ffn_b3, L0_ffn_sw1, L0_ffn_sw2, L0_ffn_sw3, L1_xattn_Wv, L1_xattn_Wk, L1_xattn_Wq, L1_xattn_Wo, L1_xattn_bo, L1_ffn_wg, L1_ffn_bg, L1_ffn_w1, L1_ffn_b1, L1_ffn_w2, L1_ffn_b2, L1_ffn_gamma, L1_ffn_beta):
    import jax
    import jax.numpy as jnp

    def _L0_xattn_ref(x, memory, mask, wq, bq, wk, bk, wv, bv, wo, bo):
        import jax, jax.numpy as jnp
        import numpy as np
        N_HEADS = 16
        DIM = 256
        HEAD_DIM = DIM // N_HEADS

        def _split_heads(t):
            B, S, _ = t.shape
            return t.reshape(B, S, N_HEADS, HEAD_DIM).transpose(0, 2, 1, 3)
        B, Sq, _ = x.shape
        q = _split_heads(x @ wq.T + bq) / np.sqrt(HEAD_DIM)
        k = _split_heads(memory @ wk.T + bk)
        v = _split_heads(memory @ wv.T + bv)
        logit = jnp.einsum('bhqd,bhkd->bhqk', q, k)
        m = mask[:, None, None, :]
        logit = jnp.where(m, -jnp.inf, logit)
        weights = jax.nn.softmax(logit, axis=-1)
        out = jnp.einsum('bhqk,bhkd->bhqd', weights, v)
        out = out.transpose(0, 2, 1, 3).reshape(B, Sq, DIM)
        return out @ wo.T + bo

    def _L0_ffn_ref(x, gate_w, w1, b1, w2, b2, w3, b3, sw1, sw2, sw3):
        import jax, jax.numpy as jnp
        import numpy as np
        D = 256
        H = 256
        E = 8
        K = 2
        I = 2 * 256
        ROUTE_SCALE = 1.0
        B, S, _ = x.shape
        xt = x.reshape(-1, D)
        logits = xt @ gate_w.T
        scores = jax.nn.softmax(logits.astype(jnp.float32), axis=-1)
        top_vals, idx = jax.lax.top_k(scores, K)
        weights = jnp.take_along_axis(scores, idx, axis=1).astype(x.dtype) * ROUTE_SCALE
        xs = xt[:, None, :] * weights[:, :, None]
        y = jnp.zeros_like(xt)
        for e in range(E):
            mask = (idx == e).astype(x.dtype)
            h = jax.nn.silu(jnp.einsum('tkd,hd->tkh', xs, w1[e]) + b1[e])
            x2 = jnp.einsum('tkh,dh->tkd', h, w2[e]) + b2[e]
            x3 = jnp.einsum('tkd,hd->tkh', xs, w3[e]) + b3[e]
            y = y + jnp.sum(x2 * x3 * mask[:, :, None], axis=1)
        z = jax.nn.silu(xt @ sw1.T) * (xt @ sw2.T) @ sw3.T
        return (y + z).reshape(B, S, D)

    def _L1_xattn_ref(values, keys, query, Wv, Wk, Wq, Wo, bo):
        import jax, jax.numpy as jnp
        import numpy as np
        EMBED = 256
        HEADS = 16
        HEAD_DIM = EMBED // HEADS
        N, Q, _ = query.shape
        v = (values @ Wv.T).reshape(N, -1, HEADS, HEAD_DIM)
        k = (keys @ Wk.T).reshape(N, -1, HEADS, HEAD_DIM)
        q = (query @ Wq.T).reshape(N, -1, HEADS, HEAD_DIM)
        energy = jnp.einsum('nqhd,nkhd->nhqk', q, k)
        attn = jax.nn.softmax(energy / HEAD_DIM ** 0.5, axis=-1)
        out = jnp.einsum('nhqk,nkhd->nqhd', attn, v).reshape(N, Q, EMBED)
        return out @ Wo.T + bo

    def _L1_ffn_ref(x, wg, bg, w1, b1, w2, b2, gamma, beta):
        import jax, jax.numpy as jnp
        import numpy as np
        N_EXPERTS = 16
        TOPK = 2
        CAPACITY_FACTOR = 1.0
        EPS_GATE = 1e-06
        LN_EPS = 1e-05
        B, S, D = x.shape
        E = wg.shape[1]
        capacity = int(CAPACITY_FACTOR * B)
        scores = jax.nn.softmax(x @ wg + bg, axis=-1)
        _, top_i = jax.lax.top_k(scores, TOPK)
        mask = jax.nn.one_hot(top_i, E, dtype=scores.dtype).sum(-2)
        masked = scores * mask
        denom = masked.sum(0, keepdims=True) + EPS_GATE
        route = masked / denom * capacity
        route_e = jnp.transpose(route, (2, 0, 1))
        max_len = S // 2
        _, seq_ids = jax.lax.top_k(route_e, max_len)
        seq_ids = jnp.sort(seq_ids, axis=-1)
        b_idx = jnp.arange(B)[None, :, None]
        xg = x[b_idx, seq_ids]
        h = jnp.einsum('ebld,edf->eblf', xg, w1) + b1[:, None, None, :]
        h = jax.nn.gelu(h, approximate=False)
        out = jnp.einsum('eblf,efd->ebld', h, w2) + b2[:, None, None, :]
        outs = jnp.zeros_like(x).at[b_idx, seq_ids].add(out)
        z = x + outs
        mu = z.mean(-1, keepdims=True)
        var = ((z - mu) ** 2).mean(-1, keepdims=True)
        return (z - mu) / jnp.sqrt(var + LN_EPS) * gamma + beta
    x = x + jnp.tanh(g_xattn[0]) * _L0_xattn_ref(_layernorm(x, axis=-1), ctx_1024, mask_BxS2_bf0, L0_xattn_wq, L0_xattn_bq, L0_xattn_wk, L0_xattn_bk, L0_xattn_wv, L0_xattn_bv, L0_xattn_wo, L0_xattn_bo)
    x = x + jnp.tanh(g_ffn[0]) * _L0_ffn_ref(_layernorm(x, axis=-1), L0_ffn_gate_w, L0_ffn_w1, L0_ffn_b1, L0_ffn_w2, L0_ffn_b2, L0_ffn_w3, L0_ffn_b3, L0_ffn_sw1, L0_ffn_sw2, L0_ffn_sw3)
    x = x + jnp.tanh(g_xattn[1]) * _L1_xattn_ref(ctx_1024, ctx_1024, _layernorm(x, axis=-1), L1_xattn_Wv, L1_xattn_Wk, L1_xattn_Wq, L1_xattn_Wo, L1_xattn_bo)
    x = x + jnp.tanh(g_ffn[1]) * _L1_ffn_ref(_layernorm(x, axis=-1), L1_ffn_wg, L1_ffn_bg, L1_ffn_w1, L1_ffn_b1, L1_ffn_w2, L1_ffn_b2, L1_ffn_gamma, L1_ffn_beta)
    return x

_drawn_inputs = setup_inputs


def setup_inputs(seed=0):
    import zlib

    import numpy as np

    out = dict(_drawn_inputs(seed))
    spreads = {'g_ffn': (-1.0, 0.2),
     'L0_xattn_bq': (0.0, 0.1),
     'L0_xattn_bk': (0.0, 0.8),
     'L0_xattn_bv': (0.0, 0.1),
     'L0_xattn_bo': (0.0, 0.1),
     'L1_xattn_bo': (0.0, 0.1),
     'L1_ffn_bg': (0.0, 0.1),
     'L1_ffn_b1': (0.0, 0.1),
     'L1_ffn_b2': (0.0, 0.1),
     'L1_ffn_gamma': (1.0, 0.2),
     'L1_ffn_beta': (0.0, 0.1)}
    factors = {'L0_ffn_b1': 6.655, 'L0_ffn_b2': 4.316, 'L0_ffn_b3': 5.388}
    for name, (base, spread) in spreads.items():
        noise = np.random.default_rng([zlib.crc32(name.encode()), seed]).standard_normal(out[name].shape)
        drawn = base * np.exp(spread * noise) if base else spread * noise
        out[name] = jnp.asarray(drawn.astype(out[name].dtype))
    for name, factor in factors.items():
        out[name] = (out[name] * factor).astype(out[name].dtype)
    return out
```

```python
from contextlib import ExitStack

import concourse.bass as bass
from concourse import mybir

ALU = mybir.AluOpType
ACT = mybir.ActivationFunctionType
F32 = mybir.dt.float32
BF16 = mybir.dt.bfloat16
U8 = mybir.dt.uint8
AX = mybir.AxisListType

P = 128
B, S, D = 16, 256, 256
SK = 77
H, HD = 16, 16
KC = D // P
NT = B * S // P
TB = S // P
GT = 4
NG = NT // GT
GN = GT * P
HG = 4
V1 = HD + 1
E0, E1 = 8, 16
I0 = 512
F1 = 64
C1 = E1 * F1 // P
TOP = S // 2
EPS = 1e-5
EPS_GATE = 1e-6
NEG = -1e30
RSTEPS = 17


def build(nc, a, out):
    ctx = ExitStack()
    with ctx:
        def sb(name, shape, dt=F32):
            return ctx.enter_context(nc.sbuf_tensor(name, shape, dt))

        def sem(name):
            return ctx.enter_context(nc.semaphore(name))

        X = sb("X", [P, NT, D])
        ctxT = sb("ctxT", [P, KC, B * SK])
        wattn = sb("wattn", [P, 4, KC, D])
        wffn = sb("wffn", [P, 3 * E0 * KC * D])
        w0 = wffn[:, :].rearrange("p (w e k n) -> p w e k n", w=3, e=E0, k=KC)
        w1f = wffn[:, 0:KC * E1 * F1].rearrange("p (k n) -> p k n", k=KC)
        w2f = wffn[:, KC * E1 * F1:KC * E1 * F1 + C1 * D].rearrange("p (c n) -> p c n", c=C1)
        sw12 = sb("sw12", [P, 2, KC, I0])
        sw3 = sb("sw3", [P, I0 // P, D])
        gatew = sb("gatew", [P, KC, E0])
        wg = sb("wg", [P, KC, E1])
        b23 = sb("b23", [P, 2, E0, D])
        b1c = sb("b1c", [P, E0, KC])
        b1f = sb("b1f", [P, C1])
        bqk = sb("bqk", [P, 2, KC])
        rows = sb("rows", [P, 5, D])
        bgr = sb("bgr", [P, E1])
        gates = sb("gates", [P, 4])
        tg = sb("tg", [P, 4])
        ident = sb("ident", [P, P])
        headm = sb("headm", [P, HG])
        same_e = sb("same_e", [P, P])
        codes = sb("codes", [P, 2, E1])
        selp = sb("selp", [3 * E0, E0, P], BF16)
        selh = sb("selh", [E1, C1, P], BF16)
        identb = sb("identb", [P, P], BF16)
        b2f = sb("b2f", [E1, D])
        b2s = sb("b2s", [E1, 3, D], BF16)
        b2r = sb("b2r", [E1, 2, D])
        mrow8 = sb("mrow8", [1, B * SK], U8)
        mrow = sb("mrow", [1, B * SK], BF16)
        ones1 = sb("ones1", [1, P], BF16)
        mcol8 = sb("mcol8", [SK, B], U8)
        keep = sb("keep", [SK, B])
        epsm = sb("epsm", [P, NT])
        mhalf = sb("mhalf", [P, NT])
        bnraw = sb("bnraw", [P, NT, 6])
        mean = sb("mean", [P, NT])
        rstd = sb("rstd", [P, NT])
        st = sb("st", [P, 4, NT])

        arena = sb("arena", [P, 14336])
        at = [0]

        def carve(parts, *shape):
            n = 1
            for s in shape:
                n *= s
            v = arena[0:parts, at[0]:at[0] + n]
            at[0] += n
            names = "abcd"[:len(shape)]
            if len(shape) > 1:
                v = v.rearrange(f"p ({' '.join(names)}) -> p {' '.join(names)}",
                                **{k: s for k, s in zip(names, shape)})
            return v

        kT = carve(P, KC, B * SK)
        Vb = carve(SK, B, H * V1)
        xn_a = carve(P, 2, D)
        xnT_a = carve(P, KC, P)
        qT = carve(P, KC, P)
        Kbd = carve(P, 2, KC, HG, SK)
        nmx = carve(P, H)
        Pr = carve(P, 2, H, SK)
        PT = carve(SK, H, P)
        rec = carve(P, H)
        o_a = carve(P, D)
        oT = carve(P, KC, P)
        at[0] = 0
        xn4 = carve(P, GT, D)
        xT = carve(P, KC, GN)
        acc = carve(P, GT, D)
        swiT = carve(P, I0 // P, GN)
        sil = carve(P, 2, GN)
        pb = carve(P, GN)
        u = carve(P, KC, GN)
        h = carve(P, KC, GN)
        x3 = carve(P, GT, D)
        x2 = carve(P, GT, D)
        x23 = x2
        at[0] = 2 * GT * D
        hg = carve(P, 2, GN)
        hm = carve(P, 2, GN)
        z = carve(P, GT, D)
        zs = carve(P, 4, GT)
        zraw = carve(P, GT, 6)
        zmean = carve(P, GT)
        zrstd = carve(P, GT)
        lg = carve(P, NT * E1)
        smT = carve(E1, NT * P)
        R1 = {n: carve(P, NT * E1) for n in ("a", "b", "p", "oh1", "oh2")}
        route = carve(P, 2, S)
        rden = carve(P, S)
        selb = carve(P, S).bitcast(BF16).rearrange("p (j s) -> p j s", j=2)
        selT = smT[:, 0:B * S // 2].bitcast(BF16).rearrange("p (b s) -> p b s", b=B)
        selg = carve(E1, GN // 2).bitcast(BF16)
        top8 = sb("top8", [P, 2, 8])
        R0 = {n: sb("r_" + n, [P, GT * E0]) for n in ("a", "b", "oh1", "oh2")}
        rm = sb("rm", [P, 5, NT])
        prob = sb("prob", [P, GT, E0])
        chosen = sb("chosen", [P, GT, E0])
        psp = sb("psp", [P, GT, 3 * E0], BF16)
        prs = sb("prs", [P, 2, GT * E0])
        pT = sb("pT", [3 * E0, GN], BF16)
        ps = ctx.enter_context(nc.psum_tensor("ps", [P, 8, 512], F32))

        L = {n: sem("ld_" + n) for n in ("const", "x", "kv", "attn0", "attn1", "ffn0", "ffn1")}
        names = """prep cst tanh hbc stat statc kps kcp vps vcp vmk
            xn xnTps xnT qps q kbd sc mx sub ex ptps pt pv rec on oTps oT y res bn
            fxn fxTps fxT lps rst rex pTps pTc gA gAs gB gG zps zcp pps pb ups u h x3ps x3 x2ps x2 x23 acc fres fbn
            lgps lgc rst1 rex1 smps smc rt dps tk sel selT selg hps gelu mps hm yps z zbn zst zpow zn zo out
            bsp msk sel0 zmn hmr""".split()
        s = {n: sem("s_" + n) for n in names}

        def wait(e, key, v):
            if isinstance(v, int) and v <= 0:
                return
            e.wait_ge(s[key], v)

        block = ctx.enter_context(nc.Block())

        A_STATS = {0: 1, 1: 3}

        def bank(n):
            return ps[:, n, :]

        @block.sync
        def _(sp):
            def ld(key, dst, src):
                sp.dma_start(dst, src).then_inc(L[key], 16)

            ld("x", X[:, 0:NT // 2, :], a["x"][:, 0:NT // 2, :])
            ld("x", X[:, NT // 2:NT, :], a["x"][:, NT // 2:NT, :])
            for k in range(4):
                ld("attn0", wattn[:, k], a["wattn0"][:, k])
            ld("kv", ctxT[:, :, :], a["ctxT"])
            ld("kv", mrow8[:, :], a["mrow"])
            ld("kv", mcol8[:, :], a["mcol"])
            ld("const", ident[:, :], a["ident"])
            ld("const", headm[:, :], a["headm"])
            ld("const", identb[:, :], a["identb"])
            ld("const", same_e[:, :], a["same_e"])
            ld("const", codes[:, :, :], a["codes"])
            ld("const", selp[:, :, :], a["selp"])
            ld("const", selh[:, :, :], a["selh"])
            ld("const", bqk[:, :, :], a["bqk"])
            for k in range(5):
                ld("const", rows[:, k, :], a["rows"][k:k + 1, :].partition_broadcast(P))
            ld("const", bgr[:, :], a["bg"].partition_broadcast(P))
            ld("const", gates[:, :], a["gates"].partition_broadcast(P))
            ld("const", b2f[:, :], a["b2f"])
            ld("const", b1f[:, :], a["b1f"])
            ld("const", wg[:, :, :], a["wg"])
            for k in range(3):
                ld("ffn0", w0[:, k], a["w0"][:, k])
            ld("ffn0", sw12[:, :, :, :], a["sw12"])
            ld("ffn0", sw3[:, :, :], a["sw3"])
            ld("ffn0", gatew[:, :, :], a["gatew"])
            for k in range(2):
                ld("ffn0", b23[:, k].rearrange("p e d -> p (e d)"), a["b23"][k:k + 1, :].partition_broadcast(P))
            ld("ffn0", b1c[:, :, :], a["b1c"])
            wait(sp, "y", NT)
            for k in range(4):
                ld("attn1", wattn[:, k], a["wattn1"][:, k])
            wait(sp, "x2ps", 2 * E0 * NG)
            ld("ffn1", w1f, a["w1f"])
            ld("ffn1", w2f, a["w2f"])
            wait(sp, "smc", NT // 4)
            for b in range(B):
                sp.dma_start(route[E1 * (b % 8):E1 * (b % 8 + 1), b // 8, :],
                             smT[:, b * S:(b + 1) * S]).then_inc(s["rt"], 16)
            wait(sp, "sel", 1)
            for b in range(B):
                sp.dma_start(selT[:, b, :], selb[E1 * (b % 8):E1 * (b % 8 + 1), b // 8, :]).then_inc(s["selT"], 16)
            for g in range(NG):
                wait(sp, "zo", 2 * (g + 1))
                sp.dma_start(out[:, GT * g:GT * (g + 1), :], X[:, GT * g:GT * (g + 1), :]).then_inc(s["out"], 16)
            wait(sp, "out", 16 * NG)

        @block.gpsimd
        def _(pool):
            pool.memset(ones1[:, :], 1.0).then_inc(s["cst"], 1)
            pool.memset(mhalf[:, :], -0.5).then_inc(s["cst"], 1)

            def rsqrt(k):
                wait(pool, "stat", k)
                pool.tensor_tensor(rstd[:, :], epsm[:, :], mhalf[:, :], ALU.pow).then_inc(s["statc"], 1)

            pool.wait_ge(s["cst"], 2)
            rsqrt(1)
            rsqrt(2)

            def feed0(g):
                for e in range(E0):
                    n = g * E0 + e
                    for hf in range(2):
                        if e == 0 and hf == 0:
                            wait(pool, "zcp", 2 * g + 2)
                        wait(pool, "x23", 2 * n + hf + 1)
                        if e > 0:
                            wait(pool, "acc", 2 * n - 1 + hf)
                        t = slice(2 * hf, 2 * hf + 2)
                        pool.tensor_tensor(acc[:, t, :], acc[:, t, :], x23[:, t, :], ALU.add).then_inc(s["acc"], 1)

            feed0(0)
            with pool.Fori(1, NG) as g:
                feed0(g)
            rsqrt(3)
            rsqrt(4)

            def feed1(g):
                wait(pool, "yps", g)
                pool.tensor_copy(selg[:, :], selT[:, :, :].rearrange("e b s -> e (b s)")[:, bass.ds(g * GN, GN)]
                                 ).then_inc(s["selg"], 1)
                wait(pool, "zst", 5 * g + 5)
                pool.tensor_tensor(zrstd, zs[:, 3, :], mhalf[:, 0:GT], ALU.pow).then_inc(s["zpow"], 1)

            wait(pool, "selT", 16 * B)
            feed1(0)
            with pool.Fori(1, NG) as g:
                feed1(g)

        @block.scalar
        def _(act):
            act.wait_ge(L["const"], 16 * 18)
            act.activation(tg[:, :], gates[:, :], ACT.Tanh).then_inc(s["tanh"], 1)

            def kv(l):
                if l == 1:
                    wait(act, "fres", NG)
                for oc in range(KC):
                    for n in range(3):
                        c = oc * 3 + n
                        lo, hi = n * 411, min(B * SK, n * 411 + 411)
                        wait(act, "kps", 6 * l + c + 1)
                        src = ps[:, c % 2, 0:hi - lo]
                        if l == 0:
                            act.activation(kT[:, oc, lo:hi], src, ACT.Identity,
                                           bias=bqk[:, 1, oc:oc + 1]).then_inc(s["kcp"], 1)
                        else:
                            act.copy(kT[:, oc, lo:hi], src).then_inc(s["kcp"], 1)

            def xnT_copy(T, v):
                wait(act, "xnTps", v + 1)
                act.copy(xnT_a, ps[:, 6, 0:D].rearrange("p (k t) -> p k t", k=KC)).then_inc(s["xnT"], 1)

            def q_copy(l, v):
                wait(act, "qps", v + 1)
                for oc in range(KC):
                    src = ps[:, 6, D + oc * P:D + (oc + 1) * P]
                    if l == 0:
                        i = act.activation(qT[:, oc, :], src, ACT.Identity, bias=bqk[:, 0, oc:oc + 1],
                                           scale=HD ** -0.5)
                    else:
                        i = act.mul(qT[:, oc, :], src, HD ** -0.5)
                i.then_inc(s["q"], 1)

            def exp(k, v):
                wait(act, "sub", v + 1)
                act.activation(Pr[:, k % 2], Pr[:, k % 2], ACT.Exp).then_inc(s["ex"], 1)

            def pt_copy(v):
                for g in range(4):
                    wait(act, "ptps", 4 * v + g + 1)
                    act.copy(PT[:, 4 * g:4 * g + 4, :],
                             ps[0:SK, 4 + g % 2, :].rearrange("p (h t) -> p h t", h=4)).then_inc(s["pt"], 1)

            def oT_copy(v):
                wait(act, "oTps", v + 1)
                act.copy(oT, ps[:, 7, 0:D].rearrange("p (k t) -> p k t", k=KC)).then_inc(s["oT"], 1)

            def attention(l):
                base = NT * l
                if l == 0:
                    wait(act, "msk", 5)

                def step(t, k, first=False, last=False):
                    v = t + base
                    if not first:
                        pt_copy(v - 1)
                    if not last:
                        exp(k, v)
                    if not first:
                        oT_copy(v - 1)

                kv(l)
                xnT_copy(0, base)
                q_copy(l, base)
                for k in range(4):
                    step(k, k, first=(k == 0))
                    xnT_copy(k + 1, base + k + 1)
                    q_copy(l, base + k + 1)
                with act.Fori(4, NT - 4, 4) as t0:
                    for k in range(4):
                        step(t0 + k, k)
                        xnT_copy(t0 + k + 1, t0 + (base + k + 1))
                        q_copy(l, t0 + (base + k + 1))
                for k in range(4):
                    t = NT - 4 + k
                    step(t, k)
                    if t + 1 < NT:
                        xnT_copy(t + 1, base + t + 1)
                        q_copy(l, base + t + 1)
                step(NT, 0, last=True)

            def xT_copy(v):
                for kc in range(KC):
                    wait(act, "fxTps", KC * v + kc + 1)
                    act.copy(xT[:, kc, :], bank(kc)).then_inc(s["fxT"], 1)

            def feed0(g):
                xT_copy(g)
                wait(act, "rst", RSTEPS * g + 2)
                act.activation(R0["a"][:, :], R0["a"][:, :], ACT.Exp).then_inc(s["rex"], 1)
                for ic in range(4):
                    wait(act, "gA", 4 * g + ic + 1)
                    if ic >= 2:
                        wait(act, "gG", 4 * g + ic - 1)
                    act.activation(sil[:, ic % 2, :], bank(2 * (ic % 2)), ACT.Silu).then_inc(s["gAs"], 1)
                wait(act, "pTps", g + 1)
                act.copy(pT[:, :], ps[0:3 * E0, 6, 0:GN // 2].bitcast(BF16)).then_inc(s["pTc"], 1)
                for hf in range(2):
                    wait(act, "zps", 2 * g + hf + 1)
                    act.copy(acc[:, 2 * hf:2 * hf + 2, :],
                             bank(4 + hf).rearrange("p (t d) -> p t d", t=2)).then_inc(s["zcp"], 1)
                for e in range(E0):
                    n = g * E0 + e
                    wait(act, "pps", n + 1)
                    wait(act, "u", 2 * n)
                    act.copy(pb, bank(6)).then_inc(s["pb"], 1)
                    for oc in range(KC):
                        wait(act, "u", 2 * n + oc + 1)
                        act.activation(h[:, oc, :], u[:, oc, :], ACT.Silu, bias=b1c[:, e, oc:oc + 1]
                                       ).then_inc(s["h"], 1)

            def feed1(g):
                xT_copy(g + NG + NG)
                for c in range(C1):
                    m = g * C1 + c
                    wait(act, "hps", m + 1)
                    wait(act, "hm", m - 1)
                    act.activation(hg[:, c % 2, :], bank(c % 2), ACT.Gelu, bias=b1f[:, c:c + 1]
                                   ).then_inc(s["gelu"], 1)

            attention(0)
            act.wait_ge(L["ffn0"], 16 * 9)
            wait(act, "fbn", 0)
            feed0(0)
            with act.Fori(1, NG) as g:
                feed0(g)
            attention(1)

            def router1(g):
                xT_copy(g + NG)

            router1(0)
            with act.Fori(1, NG) as g:
                router1(g)
            wait(act, "rst1", 3)
            act.activation(R1["a"], R1["a"], ACT.Exp).then_inc(s["rex1"], 1)
            for k in range(NT // 4):
                wait(act, "smps", k + 1)
                act.copy(smT[:, k * 512:(k + 1) * 512], ps[0:E1, 4 + k % 2, :]).then_inc(s["smc"], 1)
            feed1(0)
            with act.Fori(1, NG) as g:
                feed1(g)

        @block.vector
        def _(v):
            def stats(k):
                c = 5 * (k - 1)
                me, qe, mo, qo = bnraw[:, :, 1], bnraw[:, :, 2], bnraw[:, :, 4], bnraw[:, :, 5]

                def link(i):
                    nonlocal c
                    c += 1
                    i.then_inc(s["hbc"], 1)
                    v.wait_ge(s["hbc"], c)

                link(v.tensor_tensor(st[:, 0, :], me, mo, ALU.subtract))
                link(v.tensor_tensor(st[:, 1, :], st[:, 0, :], st[:, 0, :], ALU.mult))
                link(v.tensor_tensor(st[:, 2, :], qe, qo, ALU.add))
                link(v.tensor_tensor(mean[:, :], me, mo, ALU.add))
                link(v.tensor_scalar(st[:, 3, :], st[:, 1, :], D / 4.0, None, ALU.mult))
                v.tensor_scalar(mean[:, :], mean[:, :], 0.5, None, ALU.mult).then_inc(s["bsp"], 1)
                v.tensor_tensor(st[:, 0, :], st[:, 3, :], st[:, 2, :], ALU.add).then_inc(s["bsp"], 1)
                v.wait_ge(s["bsp"], 2 * k)
                v.tensor_scalar(epsm[:, :], st[:, 0, :], 1.0 / D, EPS, ALU.mult, ALU.add).then_inc(s["stat"], 1)

            v.wait_ge(L["x"], 32)
            v.bn_stats(bnraw[:, 0, :], X[:, 0, :]).then_inc(s["bn"], 1)
            with v.Fori(1, NT) as t:
                v.bn_stats(bnraw[:, bass.ds(t, 1), :].rearrange("p a b -> p (a b)"),
                           X[:, bass.ds(t, 1), :].rearrange("p a b -> p (a b)")).then_inc(s["bn"], 1)
            wait(v, "bn", NT)
            stats(1)
            v.wait_ge(L["const"], 16 * 18)
            v.wait_ge(L["kv"], 48)
            v.tensor_scalar(mrow[:, :], mrow8[:, :], NEG, None, ALU.mult).then_inc(s["prep"], 1)
            v.tensor_scalar(keep[:, :], mcol8[:, :], -1.0, 1.0, ALU.mult, ALU.add).then_inc(s["prep"], 1)
            v.tensor_copy(b2s[:, 0, :], b2f[:, :]).then_inc(s["prep"], 1)
            v.wait_ge(s["prep"], 3)
            v.tensor_tensor(b2r[:, 0, :], b2f[:, :], b2s[:, 0, :], ALU.subtract).then_inc(s["prep"], 1)
            v.wait_ge(s["prep"], 4)
            v.tensor_copy(b2s[:, 1, :], b2r[:, 0, :]).then_inc(s["prep"], 1)
            v.wait_ge(s["prep"], 5)
            v.tensor_tensor(b2r[:, 1, :], b2r[:, 0, :], b2s[:, 1, :], ALU.subtract).then_inc(s["prep"], 1)
            v.wait_ge(s["prep"], 6)
            v.tensor_copy(b2s[:, 2, :], b2r[:, 1, :]).then_inc(s["prep"], 1)
            v.wait_ge(s["tanh"], 1)
            for r, g in ((1, 0), (2, 1), (3, 3), (4, 3)):
                v.tensor_scalar(rows[:, r, :], rows[:, r, :], tg[:, g:g + 1], None, ALU.mult).then_inc(s["msk"], 1)
            v.tensor_scalar(bqk[:, 0, :], bqk[:, 0, :], HD ** -0.5, None, ALU.mult).then_inc(s["msk"], 1)

            def kv(l):
                ones = Vb[:, :, :].rearrange("s b (h d) -> s b h d", h=H)[:, :, :, HD]
                for b in range(B):
                    wait(v, "vps", B * l + b + 1)
                    dst = Vb[:, b, :].rearrange("s (h d) -> s h d", h=H)[:, :, 0:HD]
                    src = ps[0:SK, 2 + b % 2, 0:D].rearrange("s (h d) -> s h d", h=H)
                    if l == 0:
                        v.tensor_tensor(dst, src, rows[0:SK, 0, :].rearrange("s (h d) -> s h d", h=H), ALU.add
                                        ).then_inc(s["vcp"], 1)
                    else:
                        v.tensor_copy(dst, src).then_inc(s["vcp"], 1)
                if l == 0:
                    v.memset(ones, 1.0).then_inc(s["vmk"], 1)
                    v.wait_ge(s["vmk"], 1)
                    v.wait_ge(s["vcp"], B)
                    for b in range(B):
                        v.tensor_scalar(Vb[:, b, :], Vb[:, b, :], keep[:, b:b + 1], None, ALU.mult
                                        ).then_inc(s["vmk"], 1)
                else:
                    v.memset(ones, 1.0).then_inc(s["vmk"], 1)

            def xat(t):
                return X[:, bass.ds(t, 1), :].rearrange("p a d -> p (a d)") if not isinstance(t, int) else X[:, t, :]

            def col(x, t):
                return x[:, bass.ds(t, 1)] if not isinstance(t, int) else x[:, t:t + 1]

            def attention(l):
                base = NT * l

                def norm(t, k):
                    wait(v, "xnTps", t + (base - 1))
                    v.tensor_scalar(xn_a[:, k % 2, :], xat(t), col(mean, t), col(rstd, t),
                                    ALU.subtract, ALU.mult).then_inc(s["xn"], 1)

                def keys(b, kb):
                    for j in range(HG):
                        c = b * SK
                        src = kT[:, :, bass.ds(c, SK)] if not isinstance(c, int) else kT[:, :, c:c + SK]
                        i = v.tensor_scalar(Kbd[:, kb, :, j, :], src, headm[:, j:j + 1], None, ALU.mult)
                    i.then_inc(s["kbd"], 1)

                def soft(t, k):
                    wait(v, "sc", t + (base + 1))
                    sc = ps[:, 0:4, 0:HG * SK].rearrange("p g (h s) -> p g h s", h=HG)
                    v.tensor_reduce(nmx.rearrange("p (g h) -> p g h", g=4), sc, AX.X, ALU.max).then_inc(s["mx"], 1)
                    wait(v, "mx", t + (base + 1))
                    v.tensor_tensor(Pr[:, k % 2].rearrange("p (g h) s -> p g h s", g=4), sc,
                                    nmx.rearrange("p (g h) -> p g h", g=4).unsqueeze(3).to_broadcast([P, 4, HG, SK]),
                                    ALU.subtract).then_inc(s["sub"], 1)

                def finish(t):
                    o = ps[:, 7, 0:H * V1].rearrange("p (h d) -> p h d", h=H)
                    wait(v, "pv", t + (base + 1))
                    v.reciprocal(rec, o[:, :, HD]).then_inc(s["rec"], 1)
                    wait(v, "rec", t + (base + 1))
                    v.tensor_tensor(o_a.rearrange("p (h d) -> p h d", h=H), o[:, :, 0:HD],
                                    rec.unsqueeze(2).to_broadcast([P, H, HD]), ALU.mult).then_inc(s["on"], 1)
                    wait(v, "y", t + (base + 1))
                    v.scalar_tensor_tensor(xat(t), ps[:, 7, 0:D], tg[:, l:l + 1], xat(t), ALU.mult, ALU.add
                                           ).then_inc(s["res"], 1)
                    wait(v, "res", 2 * t + (2 * base + 1))
                    v.tensor_tensor(xat(t), xat(t), rows[:, 1 + l, :], ALU.add).then_inc(s["res"], 1)
                    wait(v, "res", 2 * t + (2 * base + 2))
                    raw = bnraw[:, bass.ds(t, 1), :].rearrange("p a b -> p (a b)") if not isinstance(t, int) \
                        else bnraw[:, t, :]
                    v.bn_stats(raw, xat(t)).then_inc(s["bn"], 1)

                kv(l)
                wait(v, "kcp", 6 * (l + 1))
                keys(0, 0)
                wait(v, "statc", 1 + 2 * l)
                norm(0, 0)
                norm(1, 1)

                def step(t, k, b=None, first=False):
                    soft(t, k)
                    if b is not None:
                        keys(b, (k // TB + 1) % 2)
                    if not first:
                        finish(t - 1)

                for k in range(4):
                    step(k, k, b=k // TB + 1 if k % TB == TB - 1 else None, first=(k == 0))
                    norm(k + 2, k)
                with v.Fori(2, (NT - 4) // TB, 2) as b0:
                    for k in range(4):
                        step(b0 * TB + k, k, b=b0 + k // TB + 1 if k % TB == TB - 1 else None)
                        norm(b0 * TB + k + 2, k)
                for k in range(4):
                    t = NT - 4 + k
                    b = t // TB + 1
                    step(t, k, b=b if k % TB == TB - 1 and b < B else None)
                    if t + 2 < NT:
                        norm(t + 2, k)
                finish(NT - 1)

            def group_norm(g, done):
                wait(v, "fxTps", KC * done)
                for k in range(GT):
                    i = v.tensor_scalar(xn4[:, k, :], xat(g * GT + k), col(mean, g * GT + k), col(rstd, g * GT + k),
                                        ALU.subtract, ALU.mult)
                i.then_inc(s["fxn"], 1)

            def choose(R, T, E, src, bias, pr, code, sem_step, sem_exp, c0, x0, out_sel):
                def sh(x, n=E):
                    return x[:, 0:T * n].rearrange("p (t e) -> p t e", t=T)

                def bc(k):
                    return rm[:, k, 0:T].unsqueeze(2).to_broadcast([P, T, E])

                ra, rb = sh(R["a"]), sh(R["b"])
                oh1, oh2 = sh(R["oh1"]), sh(R["oh2"])
                cb = code.unsqueeze(1).to_broadcast([P, T, E])
                c = 0

                def link(i):
                    nonlocal c
                    c += 1
                    i.then_inc(s[sem_step], 1)
                    v.wait_ge(s[sem_step], c0 + c)

                if bias is not None:
                    link(v.tensor_tensor(src, src, bias, ALU.add))
                link(v.tensor_reduce(rm[:, 0, 0:T], src, AX.X, ALU.max))
                link(v.tensor_tensor(ra, src, bc(0), ALU.subtract))
                v.wait_ge(s[sem_exp], x0)
                link(v.tensor_reduce(rm[:, 1, 0:T], ra, AX.X, ALU.add))
                link(v.reciprocal(rm[:, 2, 0:T], rm[:, 1, 0:T]))
                link(v.tensor_tensor(pr, ra, bc(2), ALU.mult))
                link(v.tensor_reduce(rm[:, 3, 0:T], pr, AX.X, ALU.max))
                link(v.tensor_tensor(rb, pr, bc(3), ALU.is_equal))
                link(v.tensor_tensor(rb, rb, cb, ALU.mult))
                link(v.tensor_reduce(rm[:, 3, 0:T], rb, AX.X, ALU.max))
                link(v.tensor_tensor(oh1, cb, bc(3), ALU.is_equal))
                link(v.scalar_tensor_tensor(ra, oh1, -2.0, pr, ALU.mult, ALU.add))
                link(v.tensor_reduce(rm[:, 4, 0:T], ra, AX.X, ALU.max))
                link(v.tensor_tensor(rb, ra, bc(4), ALU.is_equal))
                link(v.tensor_tensor(rb, rb, cb, ALU.mult))
                link(v.tensor_reduce(rm[:, 4, 0:T], rb, AX.X, ALU.max))
                link(v.tensor_tensor(oh2, cb, bc(4), ALU.is_equal))
                link(v.tensor_tensor(out_sel, oh1, oh2, ALU.add))
                return c

            def feed0(g):
                wait(v, "lps", g + 1)
                src = ps[:, 7, 0:GT * E0].rearrange("p (t e) -> p t e", t=GT)
                c = choose(R0, GT, E0, src, None, prob[:, :, :], codes[:, 0, 0:E0], "rst", "rex",
                           RSTEPS * g, g + 1, chosen[:, :, :])
                assert c == RSTEPS
                pf = prob[:, :, :]
                ph, pm, pl = (psp[:, :, E0 * k:E0 * k + E0] for k in range(3))
                r1 = prs[:, 0, :].rearrange("p (t e) -> p t e", t=GT)
                r2 = prs[:, 1, :].rearrange("p (t e) -> p t e", t=GT)
                for k, i in enumerate((lambda: v.tensor_copy(ph, pf), lambda: v.tensor_tensor(r1, pf, ph, ALU.subtract),
                                       lambda: v.tensor_copy(pm, r1), lambda: v.tensor_tensor(r2, r1, pm, ALU.subtract),
                                       lambda: v.tensor_copy(pl, r2))):
                    i().then_inc(s["sel0"], 1)
                    v.wait_ge(s["sel0"], 5 * g + k + 1)
                for ic in range(4):
                    wait(v, "gB", 4 * g + ic + 1)
                    wait(v, "gAs", 4 * g + ic + 1)
                    v.tensor_tensor(swiT[:, ic, :], sil[:, ic % 2, :], bank(2 * (ic % 2) + 1), ALU.mult
                                    ).then_inc(s["gG"], 1)
                for e in range(E0):
                    n = g * E0 + e
                    wait(v, "pb", n + 1)
                    wait(v, "h", 2 * n)
                    for oc in range(KC):
                        wait(v, "ups", 2 * n + oc + 1)
                        v.tensor_tensor(u[:, oc, :], pb, bank(oc), ALU.mult).then_inc(s["u"], 1)
                    wait(v, "x23", 2 * n)
                    for k in range(GT):
                        if k % 2 == 0:
                            wait(v, "x3ps", 2 * n + k // 2 + 1)
                        v.scalar_tensor_tensor(x3[:, k, :], ps[:, 2 + k // 2, (k % 2) * D:(k % 2 + 1) * D],
                                               prob[:, k, e:e + 1], b23[:, 1, e, :], ALU.mult, ALU.add
                                               ).then_inc(s["x3"], 1)
                    for hf in range(2):
                        wait(v, "x2ps", 2 * n + hf + 1)
                        wait(v, "acc", 2 * n + (hf - 1))
                        v.tensor_tensor(x2[:, 2 * hf:2 * hf + 2, :],
                                        bank(4 + hf).rearrange("p (t d) -> p t d", t=2),
                                        b23[:, 0, e, :].unsqueeze(1).to_broadcast([P, 2, D]), ALU.add
                                        ).then_inc(s["x2"], 1)
                        wait(v, "x2", 2 * n + hf + 1)
                        wait(v, "x3", 4 * n + 2 * hf + 2)
                        for k in range(2 * hf, 2 * hf + 2):
                            i = v.scalar_tensor_tensor(x23[:, k, :], x2[:, k, :], chosen[:, k, e:e + 1], x3[:, k, :],
                                                       ALU.mult, ALU.mult)
                        i.then_inc(s["x23"], 1)
                    if e == E0 - 2:
                        next_norm[0]()
                wait(v, "acc", 2 * E0 * g + 2 * E0)
                xg = X[:, bass.ds(g * GT, GT), :] if not isinstance(g, int) else X[:, g * GT:g * GT + GT, :]
                v.scalar_tensor_tensor(xg, acc, tg[:, 2:3], xg, ALU.mult, ALU.add).then_inc(s["fres"], 1)
                wait(v, "fres", g + 1)
                for k in range(GT):
                    t = g * GT + k
                    raw = bnraw[:, bass.ds(t, 1), :].rearrange("p a b -> p (a b)") if not isinstance(t, int) \
                        else bnraw[:, t, :]
                    v.bn_stats(raw, xat(t)).then_inc(s["fbn"], 1)

            next_norm = [lambda: None]

            attention(0)
            wait(v, "bn", 2 * NT)
            stats(2)
            v.wait_ge(L["ffn0"], 16 * 9)
            wait(v, "statc", 2)
            group_norm(0, 0)
            next_norm[0] = lambda: group_norm(1, 1)
            feed0(0)
            with v.Fori(1, NG - 1) as g:
                next_norm[0] = lambda: group_norm(g + 1, g + 1)
                feed0(g)
            next_norm[0] = lambda: None
            feed0(NG - 1)
            wait(v, "fbn", NT)
            stats(3)
            attention(1)
            wait(v, "bn", 3 * NT)
            stats(4)
            wait(v, "statc", 4)

            def router1(g):
                group_norm(g, NG + g)
                wait(v, "lgps", g + 1)
                dst = lg[:, bass.ds(g * GT * E1, GT * E1)] if not isinstance(g, int) \
                    else lg[:, g * GT * E1:(g + 1) * GT * E1]
                v.tensor_copy(dst, ps[:, 7, 0:GT * E1]).then_inc(s["lgc"], 1)

            router1(0)
            with v.Fori(1, NG) as g:
                router1(g)
            wait(v, "lgc", NG)
            lg3 = lg.rearrange("p (t e) -> p t e", t=NT)
            pr3 = R1["p"].rearrange("p (t e) -> p t e", t=NT)
            c = choose(R1, NT, E1, lg3, bgr[:, :].unsqueeze(1).to_broadcast([P, NT, E1]), pr3, codes[:, 1, :],
                       "rst1", "rex1", 0, 1, R1["a"].rearrange("p (t e) -> p t e", t=NT))
            v.tensor_tensor(R1["b"], R1["a"], R1["p"], ALU.mult).then_inc(s["rst1"], 1)
            wait(v, "dps", 1)
            v.tensor_scalar(rden[:, :], ps[:, 6, 0:S], EPS_GATE, None, ALU.add).then_inc(s["tk"], 1)
            wait(v, "tk", 1)
            v.reciprocal(rden[:, :], rden[:, :]).then_inc(s["tk"], 1)
            wait(v, "tk", 2)
            for j in range(2):
                v.scalar_tensor_tensor(route[:, j, :], route[:, j, :], float(B), rden[:, :], ALU.mult, ALU.mult
                                       ).then_inc(s["tk"], 1)
            n = 4
            for r in range(TOP // 8):
                wait(v, "tk", n)
                for j in range(2):
                    v.max(top8[:, j, :], route[:, j, :]).then_inc(s["tk"], 1)
                n += 2
                wait(v, "tk", n)
                for j in range(2):
                    v.match_replace(route[:, j, :], top8[:, j, :], route[:, j, :], -1.0).then_inc(s["tk"], 1)
                n += 2
            wait(v, "tk", n)
            v.tensor_scalar(selb[:, :, :], route[:, :, :], 0.0, None, ALU.is_lt).then_inc(s["sel"], 1)

            def feed1(g):
                for c in range(C1):
                    m = g * C1 + c
                    wait(v, "gelu", m + 1)
                    wait(v, "mps", m + 1)
                    wait(v, "hmr", m - 1)
                    v.tensor_tensor(hm[:, c % 2, :], hg[:, c % 2, :], bank(2 + c % 2), ALU.mult).then_inc(s["hm"], 1)
                wait(v, "yps", g + 1)
                v.tensor_tensor(z, xn4, ps[:, 4:8, 0:D], ALU.add).then_inc(s["z"], 1)
                wait(v, "z", g + 1)
                for k in range(GT):
                    i = v.bn_stats(zraw[:, k, :], z[:, k, :])
                i.then_inc(s["zbn"], 1)
                wait(v, "zbn", g + 1)
                me, qe, mo, qo = zraw[:, :, 1], zraw[:, :, 2], zraw[:, :, 4], zraw[:, :, 5]
                c = 5 * g

                def link(i, k):
                    i.then_inc(s["zst"], 1)
                    v.wait_ge(s["zst"], 5 * g + k)

                link(v.tensor_tensor(zs[:, 0, :], me, mo, ALU.subtract), 1)
                link(v.tensor_tensor(zs[:, 1, :], zs[:, 0, :], zs[:, 0, :], ALU.mult), 2)
                link(v.tensor_tensor(zs[:, 2, :], qe, qo, ALU.add), 3)
                link(v.scalar_tensor_tensor(zs[:, 0, :], zs[:, 1, :], D / 4.0, zs[:, 2, :], ALU.mult, ALU.add), 4)
                v.tensor_tensor(zs[:, 1, :], me, mo, ALU.add).then_inc(s["zmn"], 1)
                link(v.tensor_scalar(zs[:, 3, :], zs[:, 0, :], 1.0 / D, EPS, ALU.mult, ALU.add), 5)
                wait(v, "zmn", 2 * g + 1)
                v.tensor_scalar(zmean, zs[:, 1, :], 0.5, None, ALU.mult).then_inc(s["zmn"], 1)
                xg = X[:, bass.ds(g * GT, GT), :] if not isinstance(g, int) else X[:, g * GT:g * GT + GT, :]
                v.tensor_tensor(xg, xg, rows[:, 4, :].unsqueeze(1).to_broadcast([P, GT, D]), ALU.add
                                ).then_inc(s["zo"], 1)
                next_norm[0]()
                wait(v, "zpow", g + 1)
                wait(v, "zmn", 2 * g + 2)
                for k in range(GT):
                    i = v.tensor_scalar(z[:, k, :], z[:, k, :], zmean[:, k:k + 1], zrstd[:, k:k + 1],
                                        ALU.subtract, ALU.mult)
                i.then_inc(s["zn"], 1)
                wait(v, "zn", 2 * g + 1)
                v.tensor_tensor(z, z, rows[:, 3, :].unsqueeze(1).to_broadcast([P, GT, D]), ALU.mult
                                ).then_inc(s["zn"], 1)
                wait(v, "zn", 2 * g + 2)
                v.tensor_tensor(xg, xg, z, ALU.add).then_inc(s["zo"], 1)

            group_norm(0, 2 * NG)
            next_norm[0] = lambda: group_norm(1, 2 * NG + 1)
            feed1(0)
            with v.Fori(1, NG - 1) as g:
                next_norm[0] = lambda: group_norm(g + 1, g + (2 * NG + 1))
                feed1(g)
            next_norm[0] = lambda: None
            feed1(NG - 1)

        @block.tensor
        def _(pe):
            pe.wait_ge(L["const"], 16 * 18)
            pe.wait_ge(L["kv"], 48)
            pe.wait_ge(L["attn0"], 64)
            pe.wait_ge(s["cst"], 2)
            wait(pe, "prep", 2)

            def kv(l):
                for oc in range(KC):
                    for n in range(3):
                        c = oc * 3 + n
                        lo, hi = n * 411, min(B * SK, n * 411 + 411)
                        if c >= 2:
                            wait(pe, "kcp", 6 * l + c - 1)
                        for kc in range(KC):
                            i = pe.matmul(ps[:, c % 2, 0:hi - lo], wattn[:, 1, kc, oc * P:(oc + 1) * P],
                                          ctxT[:, kc, lo:hi], start=(kc == 0), stop=(kc == KC - 1))
                        i.then_inc(s["kps"], 1)
                for b in range(B):
                    if b >= 2:
                        wait(pe, "vcp", B * l + b - 1)
                    for kc in range(KC):
                        i = pe.matmul(ps[0:SK, 2 + b % 2, 0:D], ctxT[:, kc, b * SK:(b + 1) * SK],
                                      wattn[:, 2, kc, :], start=(kc == 0), stop=(kc == KC - 1))
                    i.then_inc(s["vps"], 1)

            def attention(l):
                base = NT * l

                def turn(t, k):
                    wait(pe, "xn", t + (base + 1))
                    wait(pe, "q", t + base)
                    for kc in range(KC):
                        i = pe.transpose(ps[:, 6, kc * P:(kc + 1) * P], xn_a[:, k % 2, kc * P:(kc + 1) * P],
                                         ident[:, :])
                    i.then_inc(s["xnTps"], 1)

                def query(t):
                    wait(pe, "xnT", t + (base + 1))
                    for oc in range(KC):
                        for kc in range(KC):
                            i = pe.matmul(ps[:, 6, D + oc * P:D + (oc + 1) * P], wattn[:, 0, kc, oc * P:(oc + 1) * P],
                                          xnT_a[:, kc, :], start=(kc == 0), stop=(kc == KC - 1))
                    i.then_inc(s["qps"], 1)

                def scores(t, k, b):
                    wait(pe, "q", t + (base + 1))
                    wait(pe, "sub", t + base)
                    wait(pe, "kbd", b + (B * l + 1))
                    for g in range(4):
                        c, r = g // 2, 64 * (g % 2)
                        dst = ps[:, g, 0:HG * SK]
                        i = pe.matmul(dst, qT[r:r + 64, c, :],
                                      Kbd[r:r + 64, (k // TB) % 2, c].rearrange("p h s -> p (h s)"),
                                      start=True, stop=(l == 1))
                        if l == 0:
                            off = b * SK
                            m = mrow[:, bass.ds(off, SK)] if not isinstance(off, int) else mrow[:, off:off + SK]
                            i = pe.matmul(dst, ones1[:, :], m.unsqueeze(1).to_broadcast([1, HG, SK]),
                                          start=False, stop=True)
                    i.then_inc(s["sc"], 1)

                def turn_probs(t, k):
                    wait(pe, "ex", t + (base + 1))
                    for g in range(4):
                        wait(pe, "pt", 4 * t + (4 * base + g - 1))
                        for j in range(4):
                            i = pe.transpose(ps[0:SK, 4 + g % 2, j * P:(j + 1) * P], Pr[:, k % 2, 4 * g + j, :],
                                             ident[:, :])
                        i.then_inc(s["ptps"], 1)

                def weigh(t, b):
                    wait(pe, "res", 2 * t + (2 * base - 1))
                    for hh in range(H):
                        if hh % 4 == 0:
                            wait(pe, "pt", 4 * t + (4 * base + hh // 4 + 1))
                        vb = Vb[:, bass.ds(b, 1), hh * V1:(hh + 1) * V1].rearrange("s a d -> s (a d)") \
                            if not isinstance(b, int) else Vb[:, b, hh * V1:(hh + 1) * V1]
                        i = pe.matmul(ps[:, 7, hh * V1:(hh + 1) * V1], PT[:, hh, :], vb, start=True, stop=True)
                    i.then_inc(s["pv"], 1)

                def turn_out(t):
                    wait(pe, "on", t + (base + 1))
                    for kc in range(KC):
                        i = pe.transpose(ps[:, 7, kc * P:(kc + 1) * P], o_a[:, kc * P:(kc + 1) * P], ident[:, :])
                    i.then_inc(s["oTps"], 1)

                def project(t):
                    wait(pe, "oT", t + (base + 1))
                    for kc in range(KC):
                        i = pe.matmul(ps[:, 7, 0:D], oT[:, kc, :], wattn[:, 3, kc, :],
                                      start=(kc == 0), stop=(kc == KC - 1))
                    i.then_inc(s["y"], 1)

                kv(l)
                wait(pe, "vmk", 1 + B if l == 0 else 2 + B)
                wait(pe, "vcp", B * (l + 1))
                wait(pe, "kcp", 6 * (l + 1))
                turn(0, 0)
                query(0)

                def step(t, k, b, bp, first=False):
                    scores(t, k, b)
                    if not first:
                        turn_probs(t - 1, k + 1)
                        weigh(t - 1, bp)
                        turn_out(t - 1)

                for k in range(4):
                    step(k, k, k // TB, (k - 1) // TB, first=(k == 0))
                    turn(k + 1, k + 1)
                    if k:
                        project(k - 1)
                    query(k + 1)
                with pe.Fori(2, (NT - 4) // TB, 2) as b0:
                    for k in range(4):
                        t = b0 * TB + k
                        step(t, k, b0 + k // TB, b0 + (k - 1) // TB)
                        turn(t + 1, k + 1)
                        project(t - 1)
                        query(t + 1)
                for k in range(4):
                    t = NT - 4 + k
                    step(t, k, t // TB, (t - 1) // TB)
                    if t + 1 < NT:
                        turn(t + 1, k + 1)
                    project(t - 1)
                    if t + 1 < NT:
                        query(t + 1)
                turn_probs(NT - 1, 1)
                weigh(NT - 1, B - 1)
                turn_out(NT - 1)
                project(NT - 1)

            def turn_group(g, n):
                wait(pe, "fxn", n + 1)
                for kc in range(KC):
                    for k in range(GT):
                        i = pe.transpose(ps[:, kc, k * P:(k + 1) * P], xn4[:, k, kc * P:(kc + 1) * P], ident[:, :])
                    i.then_inc(s["fxTps"], 1)
                wait(pe, "fxT", KC * n + KC)

            def logits(w, E):
                for k in range(GT):
                    for kc in range(KC):
                        i = pe.matmul(ps[:, 7, k * E:(k + 1) * E], xT[:, kc, k * P:(k + 1) * P], w[:, kc, :],
                                      start=(kc == 0), stop=(kc == KC - 1))
                return i

            def feed0(g):
                wait(pe, "u", 2 * E0 * g)
                turn_group(g, g)
                logits(gatew, E0).then_inc(s["lps"], 1)
                for ic in range(4):
                    if ic >= 2:
                        wait(pe, "gG", 4 * g + ic - 1)
                    elif ic == 1:
                        wait(pe, "x3", 4 * E0 * g)
                    for half in range(2):
                        for kc in range(KC):
                            i = pe.matmul(bank(2 * (ic % 2) + half), sw12[:, half, kc, ic * P:(ic + 1) * P],
                                          xT[:, kc, :], start=(kc == 0), stop=(kc == KC - 1))
                        i.then_inc(s["gA" if half == 0 else "gB"], 1)
                wait(pe, "sel0", 5 * g + 5)
                wait(pe, "pb", E0 * g)
                pv = ps[0:3 * E0, 6, 0:GN // 2].bitcast(BF16)
                for k in range(GT):
                    i = pe.transpose(pv[:, k * P:(k + 1) * P], psp[:, k, :], identb[:, :])
                i.then_inc(s["pTps"], 1)
                wait(pe, "gG", 4 * g + 4)
                wait(pe, "x2", 2 * E0 * g)
                for k in range(GT):
                    for ic in range(4):
                        i = pe.matmul(ps[:, 4 + k // 2, (k % 2) * D:(k % 2 + 1) * D], swiT[:, ic, k * P:(k + 1) * P],
                                      sw3[:, ic, :], start=(ic == 0), stop=(ic == 3))
                    if k % 2:
                        i.then_inc(s["zps"], 1)
                wait(pe, "pTc", g + 1)
                for e in range(E0):
                    n = g * E0 + e
                    wait(pe, "pb", n)
                    pe.matmul(bank(6), selp[:, e, :], pT[:, :], start=True, stop=True).then_inc(s["pps"], 1)
                    wait(pe, "u", 2 * n)
                    for oc in range(KC):
                        for kc in range(KC):
                            i = pe.matmul(bank(oc), w0[:, 0, e, kc, oc * P:(oc + 1) * P], xT[:, kc, :],
                                          start=(kc == 0), stop=(kc == KC - 1))
                        i.then_inc(s["ups"], 1)
                    wait(pe, "x3", 4 * n)
                    for k in range(GT):
                        for kc in range(KC):
                            i = pe.matmul(ps[:, 2 + k // 2, (k % 2) * D:(k % 2 + 1) * D],
                                          xT[:, kc, k * P:(k + 1) * P], w0[:, 2, e, kc, :],
                                          start=(kc == 0), stop=(kc == KC - 1))
                        if k % 2:
                            i.then_inc(s["x3ps"], 1)
                    wait(pe, "h", 2 * n + 2)
                    wait(pe, "x2", 2 * n)
                    if e == 0:
                        wait(pe, "zcp", 2 * g + 2)
                    for k in range(GT):
                        for kc in range(KC):
                            i = pe.matmul(ps[:, 4 + k // 2, (k % 2) * D:(k % 2 + 1) * D],
                                          h[:, kc, k * P:(k + 1) * P], w0[:, 1, e, kc, :],
                                          start=(kc == 0), stop=(kc == KC - 1))
                        if k % 2:
                            i.then_inc(s["x2ps"], 1)

            attention(0)
            pe.wait_ge(L["ffn0"], 16 * 9)
            wait(pe, "prep", 7)
            wait(pe, "res", 2 * NT)
            feed0(0)
            with pe.Fori(1, NG) as g:
                feed0(g)
            pe.wait_ge(L["attn1"], 64)
            wait(pe, "x2", 2 * E0 * NG)
            attention(1)

            def router1(g):
                turn_group(g, g + NG)
                wait(pe, "lgc", g)
                logits(wg, E1).then_inc(s["lgps"], 1)

            wait(pe, "res", 4 * NT)
            router1(0)
            with pe.Fori(1, NG) as g:
                router1(g)
            wait(pe, "rst1", RSTEPS + 2)
            for k in range(NT // 4):
                wait(pe, "smc", k - 1)
                for j in range(4):
                    t = 4 * k + j
                    i = pe.transpose(ps[0:E1, 4 + k % 2, j * P:(j + 1) * P], R1["b"][:, t * E1:(t + 1) * E1],
                                     ident[:, :])
                i.then_inc(s["smps"], 1)
            wait(pe, "rt", 16 * B)
            for j in range(2):
                i = pe.matmul(ps[:, 6, 0:S], same_e[:, :], route[:, j, :], start=(j == 0), stop=(j == 1))
            i.then_inc(s["dps"], 1)
            pe.wait_ge(L["ffn1"], 32)

            def feed1(g):
                wait(pe, "gelu", C1 * g)
                turn_group(g, g + 2 * NG)
                wait(pe, "selg", g + 1)

                def hidden(c, m):
                    wait(pe, "gelu", m - 1)
                    for kc in range(KC):
                        i = pe.matmul(bank(c % 2), w1f[:, kc, c * P:(c + 1) * P], xT[:, kc, :],
                                      start=(kc == 0), stop=(kc == KC - 1))
                    i.then_inc(s["hps"], 1)
                    wait(pe, "hm", m - 1)
                    pe.matmul(bank(2 + c % 2), selh[:, c, :], selg[:, :], start=True, stop=True
                              ).then_inc(s["mps"], 1)

                def down(c, m):
                    wait(pe, "hm", m + 1)
                    if c == 0:
                        wait(pe, "z", g)
                    for k in range(GT):
                        i = pe.matmul(ps[:, 4 + k, 0:D], hm[:, c % 2, k * P:(k + 1) * P], w2f[:, c, :],
                                      start=(c == 0), stop=False)
                    i.then_inc(s["hmr"], 1)

                for c in range(C1):
                    hidden(c, g * C1 + c)
                    if c:
                        down(c - 1, g * C1 + (c - 1))
                down(C1 - 1, g * C1 + (C1 - 1))
                for k in range(GT):
                    for j in range(3):
                        i = pe.matmul(ps[:, 4 + k, 0:D], selg[:, k * P:(k + 1) * P], b2s[:, j, :],
                                      start=False, stop=(j == 2))
                i.then_inc(s["yps"], 1)

            feed1(0)
            with pe.Fori(1, NG) as g:
                feed1(g)


def kernel(**inputs):
    import numpy as np
    import concourse.bacc as _bacc
    from concourse.bass_utils import run_bass_kernel_spmd as _run

    def n(k):
        return np.ascontiguousarray(inputs[k])

    def chunks(w):
        return np.ascontiguousarray(np.moveaxis(w.reshape((w.shape[0] // P, P) + w.shape[1:]), 0, 1))

    f = np.float32
    arrays = {}
    arrays["x"] = np.ascontiguousarray(n("x").reshape(NT, P, D).transpose(1, 0, 2))
    arrays["ctxT"] = chunks(n("ctx_1024").reshape(B * SK, D).T)
    mask = n("mask_BxS2_bf0")
    arrays["mrow"] = mask.reshape(1, B * SK)
    arrays["mcol"] = np.ascontiguousarray(mask.T)
    for l, ks in ((0, ("wq", "wk", "wv", "wo")), (1, ("Wq", "Wk", "Wv", "Wo"))):
        arrays[f"wattn{l}"] = np.ascontiguousarray(
            np.stack([chunks(n(f"L{l}_xattn_{k}").T) for k in ks], axis=1))
    arrays["bqk"] = np.ascontiguousarray(
        np.stack([n("L0_xattn_bq").reshape(KC, P).T, n("L0_xattn_bk").reshape(KC, P).T], axis=1))
    arrays["rows"] = np.stack([n("L0_xattn_bv"), n("L0_xattn_bo"), n("L1_xattn_bo"), n("L1_ffn_gamma"),
                               n("L1_ffn_beta")])
    arrays["bg"] = n("L1_ffn_bg").reshape(1, E1)
    arrays["gates"] = np.concatenate([n("g_xattn"), n("g_ffn")]).reshape(1, 4)
    arrays["w0"] = np.ascontiguousarray(
        np.stack([chunks(n(f"L0_ffn_{k}").transpose(2, 0, 1)).transpose(0, 2, 1, 3) for k in ("w1", "w2", "w3")],
                 axis=1))
    arrays["b23"] = np.stack([n("L0_ffn_b2").reshape(-1), n("L0_ffn_b3").reshape(-1)])
    arrays["b1c"] = np.ascontiguousarray(n("L0_ffn_b1").reshape(E0, KC, P).transpose(2, 0, 1))
    arrays["sw12"] = np.ascontiguousarray(np.stack([chunks(n("L0_ffn_sw1").T), chunks(n("L0_ffn_sw2").T)], axis=1))
    arrays["sw3"] = chunks(n("L0_ffn_sw3").T)
    arrays["gatew"] = chunks(n("L0_ffn_gate_w").T)
    arrays["wg"] = chunks(n("L1_ffn_wg"))
    arrays["w1f"] = chunks(n("L1_ffn_w1").transpose(1, 0, 2).reshape(D, E1 * F1))
    arrays["w2f"] = chunks(n("L1_ffn_w2").reshape(E1 * F1, D))
    arrays["b1f"] = np.ascontiguousarray(n("L1_ffn_b1").reshape(C1, P).T)
    arrays["b2f"] = n("L1_ffn_b2")
    r = np.arange(P)
    arrays["ident"] = np.eye(P, dtype=f)
    arrays["headm"] = ((r[:, None] % (HG * HD)) // HD == np.arange(HG)).astype(f)
    arrays["same_e"] = (r[:, None] % E1 == r % E1).astype(f)
    codes = np.zeros((P, 2, E1), f)
    codes[:, 0, :E0] = E0 - np.arange(E0)
    codes[:, 1, :] = E1 - np.arange(E1)
    arrays["codes"] = codes
    bf = np.dtype("bfloat16")
    arrays["identb"] = np.eye(P, dtype=f).astype(bf)
    arrays["selp"] = np.repeat(np.tile(np.eye(E0, dtype=f), (3, 1)), P, axis=1).astype(bf).reshape(3 * E0, E0, P)
    arrays["selh"] = np.repeat(np.eye(E1, dtype=f), F1, axis=1).astype(bf).reshape(E1, C1, P)

    nc = _bacc.Bacc("TRN2", target_bir_lowering=False, num_devices=1)
    aps = {}
    ins = {}
    for k, x in arrays.items():
        x = np.ascontiguousarray(x)
        ins[f"in_{k}"] = x
        aps[k] = nc.dram_tensor(f"in_{k}", x.shape, mybir.dt.from_np(x.dtype), kind="ExternalInput").ap()
    out = nc.dram_tensor("out_0", (P, NT, D), F32, kind="ExternalOutput").ap()
    build(nc, aps, out)
    got = _run(nc, [ins], core_ids=[0]).results[0]["out_0"]
    return np.ascontiguousarray(got.reshape(P, NT, D).transpose(1, 0, 2).reshape(B, S, D))
```

```python
from contextlib import ExitStack

import concourse.bass as bass
from concourse import mybir

ALU = mybir.AluOpType
ACT = mybir.ActivationFunctionType
F32 = mybir.dt.float32
BF16 = mybir.dt.bfloat16
F16 = mybir.dt.float16
F32R = mybir.dt.float32r
U8 = mybir.dt.uint8
AX = mybir.AxisListType

P = 128
B, S, D = 16, 256, 256
SK = 77
H, HD = 16, 16
KC = D // P
NT = B * S // P
TB = S // P
GT = 4
NG = NT // GT
GN = GT * P
HG = 4
V1 = HD + 1
E0, E1 = 8, 16
I0 = 512
F1 = 64
C1 = E1 * F1 // P
KVN = 412
TOP = S // 2
EPS = 1e-5
EPS_GATE = 1e-6
NEG = -1e30
RSTEPS = 17
CST = 2 * P + HG + 2 * E1 + 2 * KC + C1 + 3 * E0 * KC + KC * E0 + KC * E1
BCST = 5 * D + E1 + 4
PARTS = ((1, 0), (0, 1), (0, 0))


def build(nc, a, out):
    ctx = ExitStack()
    with ctx:
        def sb(name, shape, dt=F32):
            return ctx.enter_context(nc.sbuf_tensor(name, shape, dt))

        def sem(name):
            return ctx.enter_context(nc.semaphore(name))

        X = sb("X", [P, NT, D])
        cst = sb("cst", [P, CST])
        o = [0]

        def const(n):
            o[0] += n
            return cst[:, o[0] - n:o[0]]

        ident = const(P)
        headm = const(HG)
        same_e = const(P)
        codes = const(2 * E1).rearrange("p (l e) -> p l e", l=2)
        bqk = const(2 * KC).rearrange("p (w k) -> p w k", w=2)
        b1f = const(C1)
        b1c = const(E0 * KC).rearrange("p (e k) -> p e k", e=E0)
        b23c = const(2 * E0 * KC).rearrange("p (w e k) -> p w e k", w=2, e=E0)
        gates_raw = const(KC * (E0 + E1))
        bc = sb("bc", [P, BCST])
        rows = bc[:, 0:5 * D].rearrange("p (r d) -> p r d", r=5)
        bgr = bc[:, 5 * D:5 * D + E1]
        gates = bc[:, 5 * D + E1:5 * D + E1 + 4]
        tg = sb("tg", [P, 4])
        rw = sb("rw", [P, 2, KC * (E0 + E1)], F32R)
        gatew = rw[:, :, 0:KC * E0].rearrange("p l (k e) -> p l k e", k=KC)
        wg = rw[:, :, KC * E0:].rearrange("p l (k e) -> p l k e", k=KC)
        selp = sb("selp", [3 * E0, E0, P], BF16)
        identb = sb("identb", [P, P], BF16)
        identh = sb("identh", [P, P], F16)
        ones1 = sb("ones1", [1, P], BF16)
        mcol8 = sb("mcol8", [SK, B], U8)
        keep = sb("keep", [SK, B])
        epsm = sb("epsm", [P, NT])
        mhalf = sb("mhalf", [P, NT])
        one = sb("one", [P, 8])
        bnraw = sb("bnraw", [P, NT, 6])
        mean = sb("mean", [P, NT])
        rstd = sb("rstd", [P, NT])
        st = sb("st", [P, 4, NT])

        top8 = sb("top8", [P, 2, 8])
        R0 = {n: sb("r_" + n, [P, GT * E0]) for n in ("a", "b", "oh1", "oh2")}
        rm = sb("rm", [P, 5, NT])
        prob = sb("prob", [P, GT, E0])
        chosen = sb("chosen", [P, GT, E0])
        psp = sb("psp", [P, GT, 3 * E0], BF16)
        prs = sb("prs", [P, 2, GT * E0])
        pT = sb("pT", [3 * E0, GN], BF16)
        def over():
            return ExitStack()

        def tmp(stack, name, shape, dt=F32):
            return stack.enter_context(nc.sbuf_tensor(name, shape, dt))[(slice(None),) * len(shape)]

        with over() as att:
            with over() as raw:
                wattn_raw = tmp(raw, "wattn_raw", [P, 4, 2, KC * D])
                ctx_raw = tmp(raw, "ctx_raw", [P, 2, KC, B * SK])
            wattn = tmp(att, "wattn", [P, 4, 2, KC * D], F32R)
            ctxT = tmp(att, "ctxT", [P, 2, KC, B * SK], F32R)
            kT = tmp(att, "kT", [P, 2, KC, B * SK], F32R)
            Vb = tmp(att, "Vb", [SK, 3, B, H * V1], BF16)
            Vc = [tmp(att, f"Vc{k}", [SK, H, 3, V1], BF16) for k in range(2)]
            Kbd = [tmp(att, f"Kbd{k}", [P, 2, KC, HG * SK], F32R) for k in range(2)]
            Pf = tmp(att, "Pf", [P, H, SK])
            Phl = [tmp(att, f"Phl{k}", [P, 2, H, SK], F16) for k in range(2)]
            mrow8 = tmp(att, "mrow8", [1, B * SK], U8)
            mrow = tmp(att, "mrow", [1, B * SK], BF16)
            xn_a = tmp(att, "xn_a", [P, 2, D])
            xnT_a = tmp(att, "xnT_a", [P, 2, KC, P], F32R)
            qT = tmp(att, "qT", [P, 2, KC, P], F32R)
            nmx = tmp(att, "nmx", [P, H])
            o_s = tmp(att, "o_s", [P, H, V1])
            rec = tmp(att, "rec", [P, H])
            o_a = tmp(att, "o_a", [P, D])
            oT = tmp(att, "oT", [P, 2, KC, P], F32R)
            with over() as early:
                vf = tmp(early, "vf", [SK, 2, D])
                vr = tmp(early, "vr", [SK, 2, D])
            PT = tmp(att, "PT", [SK, 4, 2, 4, P], F16)

        xn4 = tmp(ctx, "xn4", [P, GT, D])
        xT = tmp(ctx, "xT", [P, 2, KC, GN], F32R)
        with over() as f0:
            with over() as raw:
                w0_raw = tmp(raw, "w0_raw", [P, E0, 3, 2, KC * D])
                sw12_raw = tmp(raw, "sw12_raw", [P, 2, 2, KC * I0])
                sw3_raw = tmp(raw, "sw3_raw", [P, 2, I0 // P * D])
            w0 = tmp(f0, "w0", [P, E0, 3, 2, KC * D], F32R)
            sw12 = tmp(f0, "sw12", [P, 2, 2, KC * I0], F32R)
            sw3 = tmp(f0, "sw3", [P, 2, I0 // P * D], F32R)
            pb = tmp(f0, "pb", [P, 2, GN])
            x23 = tmp(f0, "x23", [P, KC, GN])
            sil, swf = pb, x23
            yT = tmp(f0, "yT", [P, KC, GN])
            mb = tmp(f0, "mb", [P, GN], BF16)
            with over() as shared:
                swi = tmp(shared, "swi", [P, 2, I0 // P, GN], F32R)
            u = tmp(f0, "u", [P, KC, GN])
            h = tmp(f0, "h", [P, 2, KC, GN], F32R)
            x3 = tmp(f0, "x3", [P, KC, GN])

        with over() as f1:
            with over() as raw:
                w1f_raw = tmp(raw, "w1f_raw", [P, 2, KC * E1 * F1])
                w2f_raw = tmp(raw, "w2f_raw", [P, 2, C1 * D])
            w1f = tmp(f1, "w1f", [P, 2, KC * E1 * F1], F32R)
            w2f = tmp(f1, "w2f", [P, 2, C1 * D], F32R)
            selh = tmp(f1, "selh", [E1, C1, P], BF16)
            b2f = tmp(f1, "b2f", [E1, D])
            b2r = tmp(f1, "b2r", [E1, 2, D])
            b2s = tmp(f1, "b2s", [E1, 3, D], BF16)
            xn4b = tmp(f1, "xn4b", [P, GT, D])
            xTb = tmp(f1, "xTb", [P, 2, KC, GN], F32R)
            R1 = {n: tmp(f1, "r1_" + n, [P, NT * E1]) for n in ("a", "b", "p", "oh1", "oh2")}
            lg = tmp(f1, "lg", [P, NT * E1])
            smT = tmp(f1, "smT", [E1, NT * P])
            route = tmp(f1, "route", [P, 2, S])
            rden = tmp(f1, "rden", [P, S])
            selb = tmp(f1, "selb", [P, 2, S], BF16)
            selT = smT[:, 0:B * S // 2].bitcast(BF16).rearrange("p (b s) -> p b s", b=B)
            selg = tmp(f1, "selg", [E1, GN], BF16)
            hgf = tmp(f1, "hgf", [P, 2, GN])
            hmf = tmp(f1, "hmf", [P, 2, GN])
            hm = tmp(f1, "hm", [P, 2, 2, GN], F32R)
            z = tmp(f1, "z", [P, GT, D])
            zs = tmp(f1, "zs", [P, 4, GT])
            zraw = tmp(f1, "zraw", [P, GT, 6])
            zmean = tmp(f1, "zmean", [P, GT])
            zrstd = tmp(f1, "zrstd", [P, GT])

        ps = ctx.enter_context(nc.psum_tensor("ps", [P, 8, 512], F32))

        L = {n: sem("ld_" + n) for n in ("const", "small", "x", "kv", "attn0", "shared", "feed0", "attn1", "ctx1", "feed1", "late")}
        Le = [sem(f"ld_expert{e}") for e in range(E0)]
        names = """prep cst tanh stc stat statc wsh wsl csh csl kps kcp kl vps vf vh vl vp vc vmk
            xn xnTps xnT xl qps q ql kbd sc mx sub ex ph pl ptps pt pv osum rec on oTps oT ol y res res2 bn
            stg chk fxn fxTps fxT fxf fxl lps rst rex sel0 pTps pTc gA gAs gB gG gGh gGl zps zcp
            pps pb mb ups u hf hh hl x3ps x3 x3m x2ps x23 acc yps0 fres fbn wh wl sh sl rws b2
            lgps lgc rst1 rex1 smps smc rt dps tk sel selT selg hps gelu mps hm hmh hml hmr yps z zbn zst zmn
            zpow zn zo out bsp msk""".split()
        s = {n: sem("s_" + n) for n in names}

        def counted(v):
            return not isinstance(v, int) or v > 0

        def tile_of(x, t):
            return x[:, t, :] if isinstance(t, int) else x[:, bass.ds(t, 1), :].rearrange("p a d -> p (a d)")

        def col(x, t):
            return x[:, t:t + 1] if isinstance(t, int) else x[:, bass.ds(t, 1)]

        def span(x, c, n):
            return x[..., c:c + n] if isinstance(c, int) else x[..., bass.ds(c, n)]

        def group_of(x, g):
            return x[:, g * GT:(g + 1) * GT, :] if isinstance(g, int) else x[:, bass.ds(g * GT, GT), :]

        block = ctx.enter_context(nc.Block())

        def bank(n):
            return ps[:, n, :]

        @block.sync
        def _(sp):
            def ld(key, dst, src):
                sp.dma_start(dst, src).then_inc(L[key], 16)

            ld("attn0", wattn_raw[:, :, 1, :], a["wattn0"])
            ld("kv", ctx_raw[:, 1], a["ctxT"])
            ld("const", cst[:, :], a["cst"])
            ld("const", bc[:, :], a["bc"].partition_broadcast(P))
            ld("small", mrow8, a["mrow"])
            ld("small", mcol8[:, :], a["mcol"])
            ld("small", identb[:, :], a["identb"])
            ld("small", identh[:, :], a["identh"])
            ld("small", selp[:, :, :], a["selp"])
            sp.wait_ge(s["bn"], 2 * NT)
            ld("shared", sw12_raw[:, :, 1, :], a["sw12"])
            ld("shared", sw3_raw[:, 1, :], a["sw3"])
            for e in range(E0):
                sp.dma_start(w0_raw[:, e, :, 1, :], a["feed0"][:, e]).then_inc(Le[e], 16)
            sp.wait_ge(s["fres"], NG)
            ld("attn1", wattn_raw[:, :, 1, :], a["wattn1"])
            ld("ctx1", ctx_raw[:, 1], a["ctxT"])
            sp.wait_ge(s["bn"], 3 * NT)
            ld("feed1", w1f_raw[:, 1, :], a["w1f"])
            ld("feed1", w2f_raw[:, 1, :], a["w2f"])
            ld("late", selh, a["selh"])
            ld("late", b2f, a["b2f"])
            for b in range(B):
                sp.wait_ge(s["smc"], b // 2 + 1)
                sp.dma_start(route[E1 * (b % 8):E1 * (b % 8 + 1), b // 8, :],
                             smT[:, b * S:(b + 1) * S]).then_inc(s["rt"], 16)
            sp.wait_ge(s["sel"], 1)
            for b in range(B):
                sp.dma_start(selT[:, b, :], selb[E1 * (b % 8):E1 * (b % 8 + 1), b // 8, :]).then_inc(s["selT"], 16)
            for g in range(NG):
                sp.wait_ge(s["zo"], 2 * (g + 1))
                sp.dma_start(out[:, GT * g:GT * (g + 1), :], X[:, GT * g:GT * (g + 1), :]).then_inc(s["out"], 16)
            sp.wait_ge(s["out"], 16 * NG)

        @block.gpsimd
        def _(pool):
            pool.memset(ones1[:, :], 1.0).then_inc(s["cst"], 1)
            pool.memset(mhalf[:, :], -0.5).then_inc(s["cst"], 1)
            pool.memset(one[:, :], 1.0).then_inc(s["cst"], 1)

            def rsqrt(k):
                pool.wait_ge(s["stat"], k)
                pool.tensor_tensor(rstd[:, :], epsm[:, :], mhalf[:, :], ALU.pow).then_inc(s["statc"], 1)

            pool.wait_ge(s["cst"], 3)
            rsqrt(1)

            def split(key, n, hi, lo, src):
                pool.tensor_copy(hi, src).then_inc(s[key], 1)
                pool.wait_ge(s[key], n + 1)
                pool.tensor_tensor(lo, src, hi, ALU.subtract).then_inc(s[key], 1)

            def attention(l):
                base = NT * l

                for b in range(B):
                    heads = [Vb[:, k, b, :].rearrange("s (h d) -> s h d", h=H)[:, :, 0:HD] for k in (1, 2)]
                    pool.wait_ge(s["vl"], B * l + b + 1)
                    split("vp", 2 * (B * l + b), heads[0], heads[1],
                          vr[:, b % 2, :].rearrange("s (h d) -> s h d", h=H))

                def halve(t, k):
                    for j in range(2):
                        hs = slice(8 * j, 8 * j + 8)
                        pool.wait_ge(s["ex"], 2 * t + (2 * base + j + 1))
                        pool.tensor_tensor(Phl[k % 2][:, 0, hs, :], Pf[:, hs, :],
                                           one[:, :].unsqueeze(2).to_broadcast([P, 8, SK]), ALU.mult
                                           ).then_inc(s["ph"], 1)
                        pool.wait_ge(s["ph"], 2 * t + (2 * base + j + 1))
                        pool.tensor_tensor(Phl[k % 2][:, 1, hs, :], Pf[:, hs, :], Phl[k % 2][:, 0, hs, :],
                                           ALU.subtract).then_inc(s["pl"], 1)

                def bias(t):
                    pool.wait_ge(s["res"], t + (base + 1))
                    pool.tensor_tensor(tile_of(X, t), tile_of(X, t), rows[:, 1 + l, :], ALU.add
                                       ).then_inc(s["res2"], 1)

                for k in range(4):
                    halve(k, k)
                    if k >= 2:
                        bias(k - 2)
                with pool.Fori(4, NT - 4, 4) as t0:
                    for k in range(4):
                        halve(t0 + k, k)
                        bias(t0 + (k - 2))
                for k in range(4):
                    halve(NT - 4 + k, k)
                    bias(NT - 6 + k)
                bias(NT - 2)
                bias(NT - 1)

            attention(0)
            rsqrt(2)

            def feed0(g):
                for e in range(E0):
                    n = g * E0 + e
                    for hf in range(2):
                        if e == 0 and hf == 0:
                            pool.wait_ge(s["zcp"], 2 * g + 2)
                        if e > 0:
                            pool.wait_ge(s["acc"], 2 * n - 1 + hf)
                        pool.wait_ge(s["x23"], 2 * n + hf + 1)
                        pool.tensor_tensor(yT[:, hf, :], yT[:, hf, :], x23[:, hf, :], ALU.add).then_inc(s["acc"], 1)

            def feed0_weights():
                pool.wait_ge(L["shared"], 32)
                split("sl", 0, sw12[:, :, 0, :], sw12[:, :, 1, :], sw12_raw[:, :, 1, :])
                split("sl", 2, sw3[:, 0, :], sw3[:, 1, :], sw3_raw[:, 1, :])
                for e in range(E0):
                    pool.wait_ge(Le[e], 16)
                    split("wl", 2 * e, w0[:, e, :, 0, :], w0[:, e, :, 1, :], w0_raw[:, e, :, 1, :])

            feed0_weights()
            feed0(0)
            with pool.Fori(1, NG) as g:
                feed0(g)
            rsqrt(3)
            attention(1)
            rsqrt(4)
            pool.wait_ge(L["feed1"], 32)
            split("wl", 2 * E0, w1f[:, 0, :], w1f[:, 1, :], w1f_raw[:, 1, :])
            split("wl", 2 * E0 + 2, w2f[:, 0, :], w2f[:, 1, :], w2f_raw[:, 1, :])

            def feed1(g):
                if counted(g):
                    pool.wait_ge(s["yps"], g)
                pool.tensor_copy(selg, span(selT.rearrange("e b s -> e (b s)"), g * GN, GN)).then_inc(s["selg"], 1)
                pool.wait_ge(s["zst"], 5 * g + 5)
                pool.tensor_tensor(zrstd, zs[:, 3, :], mhalf[:, 0:GT], ALU.pow).then_inc(s["zpow"], 1)

            pool.wait_ge(s["selT"], 16 * B)
            feed1(0)
            with pool.Fori(1, NG) as g:
                feed1(g)

        @block.scalar
        def _(act):
            act.dma_start(X[:, 0:NT // 2, :], a["x"][:, 0:NT // 2, :]).then_inc(L["x"], 16)
            act.dma_start(X[:, NT // 2:NT, :], a["x"][:, NT // 2:NT, :]).then_inc(L["x"], 16)
            act.wait_ge(L["attn0"], 16)
            raw = wattn_raw[:, :, 1, :]
            act.mul(wattn[:, 0, 0, :], raw[:, 0], HD ** -0.5).then_inc(s["wsh"], 1)
            act.copy(wattn[:, 1:4, 0, :], raw[:, 1:4]).then_inc(s["wsh"], 1)
            act.wait_ge(L["kv"], 16)
            act.copy(ctxT[:, 0], ctx_raw[:, 1]).then_inc(s["csh"], 1)
            act.wait_ge(L["const"], 32)
            act.activation(tg[:, :], gates, ACT.Tanh).then_inc(s["tanh"], 1)

            def kv(l):
                if l == 1:
                    act.wait_ge(L["attn1"], 16)
                    act.copy(wattn[:, :, 0, :], wattn_raw[:, :, 1, :]).then_inc(s["wsh"], 1)
                    act.wait_ge(L["ctx1"], 16)
                    act.copy(ctxT[:, 0], ctx_raw[:, 1]).then_inc(s["csh"], 1)
                for oc in range(KC):
                    for n in range(3):
                        c = oc * 3 + n
                        lo, hi = n * KVN, min(B * SK, (n + 1) * KVN)
                        act.wait_ge(s["kps"], 6 * l + c + 1)
                        src = ps[:, c % 2, 0:hi - lo]
                        if l == 0:
                            act.activation(kT[:, 0, oc, lo:hi], src, ACT.Identity,
                                           bias=bqk[:, 1, oc:oc + 1]).then_inc(s["kcp"], 1)
                        else:
                            act.copy(kT[:, 0, oc, lo:hi], src).then_inc(s["kcp"], 1)
                for b in range(B):
                    dst = Vb[:, 0, b, :].rearrange("s (h d) -> s h d", h=H)[:, :, 0:HD]
                    if l == 0:
                        act.wait_ge(s["vf"], b + 1)
                        act.mul(dst, vf[:, b % 2, :].rearrange("s (h d) -> s h d", h=H), keep[:, b:b + 1]
                                ).then_inc(s["vh"], 1)
                    else:
                        act.wait_ge(s["vps"], B * l + b + 1)
                        act.copy(dst, ps[0:SK, 2 + b % 2, 0:D].rearrange("s (h d) -> s h d", h=H)
                                 ).then_inc(s["vh"], 1)

            def xnT_copy(v):
                act.wait_ge(s["xnTps"], v + 1)
                act.copy(xnT_a[:, 0], ps[:, 6, 0:D].rearrange("p (k t) -> p k t", k=KC)).then_inc(s["xnT"], 1)

            def q_copy(l, v):
                act.wait_ge(s["qps"], v + 1)
                if l == 0:
                    for oc in range(KC):
                        i = act.activation(qT[:, 0, oc, :], ps[:, 6, D + oc * P:D + (oc + 1) * P], ACT.Identity,
                                           bias=bqk[:, 0, oc:oc + 1])
                else:
                    i = act.mul(qT[:, 0], ps[:, 6, D:2 * D].rearrange("p (k t) -> p k t", k=KC), HD ** -0.5)
                i.then_inc(s["q"], 1)

            def exp(j, v):
                act.wait_ge(s["sub"], 2 * v + (j + 1))
                act.activation(Pf[:, 8 * j:8 * j + 8, :], Pf[:, 8 * j:8 * j + 8, :], ACT.Exp).then_inc(s["ex"], 1)

            def pt_copy(g, v):
                act.wait_ge(s["ptps"], 4 * v + (g + 1))
                act.copy(PT[:, g].rearrange("s l h t -> s (l h t)"), ps[0:SK, 4 + g % 2, :].bitcast(F16)
                         ).then_inc(s["pt"], 1)

            def oT_copy(v):
                act.wait_ge(s["oTps"], v + 1)
                act.copy(oT[:, 0], ps[:, 7, 0:D].rearrange("p (k t) -> p k t", k=KC)).then_inc(s["oT"], 1)

            def attention(l):
                base = NT * l

                def values(b, kb):
                    if counted(2 * b + (base - 2) if not isinstance(b, int) or b >= 2 else base):
                        act.wait_ge(s["pv"], 2 * b + (base - 2) if not isinstance(b, int) or b >= 2 else base)
                    src = Vb[:, :, b, :] if isinstance(b, int) \
                        else Vb[:, :, bass.ds(b, 1), :].rearrange("s k a n -> s k (a n)")
                    act.copy(Vc[kb].rearrange("s h k d -> s k h d"), src.rearrange("s k (h d) -> s k h d", h=H)
                             ).then_inc(s["vc"], 1)

                def step(t, b=True, c=True, n=True, x=True, vb=None, kb=0):
                    v = t + base
                    if n:
                        xnT_copy(v + 1)
                    if b:
                        pt_copy(0, v + (-1))
                    if x:
                        exp(0, v)
                    if n:
                        q_copy(l, v + 1)
                    if b:
                        pt_copy(1, v + (-1))
                    if x:
                        exp(1, v)
                    if c:
                        oT_copy(v + (-2))
                    if b:
                        pt_copy(2, v + (-1))
                        pt_copy(3, v + (-1))
                    if vb is not None:
                        values(vb, kb)

                kv(l)
                act.wait_ge(s["vmk"], 4 if l == 0 else 7)
                act.wait_ge(s["vp"], 2 * B * (l + 1))
                values(0, 0)
                if l == 0:
                    act.wait_ge(s["msk"], 5)
                xnT_copy(base)
                q_copy(l, base)
                def entry(k, b0):
                    return b0 + (k // TB + 1) if k % TB == TB - 1 else None

                for k in range(4):
                    step(k, b=k >= 1, c=k >= 2, vb=entry(k, 0), kb=(k // TB + 1) % 2)
                with act.Fori(2, (NT - 4) // TB, 2) as b0:
                    for k in range(4):
                        step(b0 * TB + k, vb=entry(k, b0), kb=(k // TB + 1) % 2)
                for t in range(NT - 4, NT + 2):
                    k = t % 4
                    step(t, b=t <= NT, n=t + 1 < NT, x=t < NT, kb=(k // TB + 1) % 2,
                         vb=entry(k, B - 2) if t < NT - 1 else None)

            def xT_copy(v, dst, first_bank=0):
                for kc in range(KC):
                    act.wait_ge(s["fxTps"], KC * v + (kc + 1))
                    act.copy(dst[:, kc, :], bank(first_bank + kc)).then_inc(s["fxT"], 1)

            def feed0(g):
                if counted(2 * E0 * g):
                    act.wait_ge(s["x2ps"], 2 * E0 * g)
                xT_copy(g, xT[:, 0])
                act.wait_ge(s["rst"], RSTEPS * g + 2)
                act.activation(R0["a"][:, :], R0["a"][:, :], ACT.Exp).then_inc(s["rex"], 1)
                for ic in range(5):
                    if ic < 4:
                        if ic == 0:
                            if counted(2 * E0 * g):
                                act.wait_ge(s["x23"], 2 * E0 * g)
                        act.wait_ge(s["gA"], 4 * g + ic + 1)
                        if ic >= 2:
                            act.wait_ge(s["gG"], 4 * g + ic - 1)
                        act.activation(sil[:, ic % 2, :], bank(2 * (ic % 2)), ACT.Silu).then_inc(s["gAs"], 1)
                    if ic >= 1:
                        act.wait_ge(s["gG"], 4 * g + ic)
                        act.copy(swi[:, 0, ic - 1, :], swf[:, (ic - 1) % 2, :]).then_inc(s["gGh"], 1)
                act.wait_ge(s["pTps"], g + 1)
                act.copy(pT[:, :], ps[0:3 * E0, 6, 0:GN // 2].bitcast(BF16)).then_inc(s["pTc"], 1)
                for oc in range(KC):
                    if oc == 0:
                        if counted(g):
                            act.wait_ge(s["yps0"], g)
                    act.wait_ge(s["zps"], 2 * g + oc + 1)
                    act.copy(yT[:, oc, :], bank(4 + oc)).then_inc(s["zcp"], 1)
                for e in range(E0):
                    n = g * E0 + e
                    if e >= 2:
                        act.wait_ge(s["x3"], 2 * n - 2)
                        act.wait_ge(s["mb"], n - 1)
                    elif e == 0:
                        act.wait_ge(s["gG"], 4 * g + 4)
                    act.wait_ge(s["pps"], n + 1)
                    act.copy(pb[:, e % 2, :], bank(6)).then_inc(s["pb"], 1)
                    if counted(2 * n):
                        act.wait_ge(s["x2ps"], 2 * n)
                    for oc in range(KC):
                        act.wait_ge(s["u"], 2 * n + oc + 1)
                        act.activation(u[:, oc, :], u[:, oc, :], ACT.Silu, bias=b1c[:, e, oc:oc + 1]
                                       ).then_inc(s["hf"], 1)
                        act.wait_ge(s["hf"], 2 * n + oc + 1)
                        act.copy(h[:, 0, oc, :], u[:, oc, :]).then_inc(s["hh"], 1)

            def feed1(g):
                if counted(C1 * g):
                    act.wait_ge(s["hps"], C1 * g)
                xT_copy(g + 2 * NG, xT[:, 0])
                for c in range(C1):
                    m = g * C1 + c
                    act.wait_ge(s["hps"], m + 1)
                    if counted(m - 1):
                        act.wait_ge(s["hm"], m - 1)
                    act.activation(hgf[:, c % 2, :], bank(c % 2), ACT.Gelu, bias=b1f[:, c:c + 1]
                                   ).then_inc(s["gelu"], 1)
                    act.wait_ge(s["hm"], m + 1)
                    if counted(m - 1):
                        act.wait_ge(s["hmr"], m - 1)
                    act.copy(hm[:, c % 2, 0, :], hmf[:, c % 2, :]).then_inc(s["hmh"], 1)

            attention(0)
            feed0(0)
            with act.Fori(1, NG) as g:
                feed0(g)
            attention(1)

            def router1(g, k):
                if counted(g + (-1)):
                    act.wait_ge(s["lgps"], g + (-1))
                xT_copy(g + NG, (xT, xTb)[k][:, 0], 2 * k)

            router1(0, 0)
            router1(1, 1)
            with act.Fori(2, NG, 2) as g:
                router1(g, 0)
                router1(g + 1, 1)
            act.wait_ge(s["rst1"], 3)
            act.activation(R1["a"], R1["a"], ACT.Exp).then_inc(s["rex1"], 1)
            for k in range(NT // 4):
                act.wait_ge(s["smps"], k + 1)
                act.copy(smT[:, k * 512:(k + 1) * 512], ps[0:E1, 4 + k % 2, :]).then_inc(s["smc"], 1)
            feed1(0)
            with act.Fori(1, NG) as g:
                feed1(g)

        @block.vector
        def _(v):
            def stats(k):
                c = 5 * (k - 1)
                me, qe, mo, qo = bnraw[:, :, 1], bnraw[:, :, 2], bnraw[:, :, 4], bnraw[:, :, 5]

                def link(i):
                    nonlocal c
                    c += 1
                    i.then_inc(s["stc"], 1)
                    v.wait_ge(s["stc"], c)

                link(v.tensor_tensor(st[:, 0, :], me, mo, ALU.subtract))
                link(v.tensor_tensor(st[:, 1, :], st[:, 0, :], st[:, 0, :], ALU.mult))
                link(v.tensor_tensor(st[:, 2, :], qe, qo, ALU.add))
                link(v.tensor_tensor(mean[:, :], me, mo, ALU.add))
                link(v.tensor_scalar(st[:, 3, :], st[:, 1, :], D / 4.0, None, ALU.mult))
                v.tensor_scalar(mean[:, :], mean[:, :], 0.5, None, ALU.mult).then_inc(s["bsp"], 1)
                v.tensor_tensor(st[:, 0, :], st[:, 3, :], st[:, 2, :], ALU.add).then_inc(s["bsp"], 1)
                v.wait_ge(s["bsp"], 2 * k)
                v.tensor_scalar(epsm[:, :], st[:, 0, :], 1.0 / D, EPS, ALU.mult, ALU.add).then_inc(s["stat"], 1)

            def context_lo(k):
                v.wait_ge(s["csh"], k)
                v.tensor_tensor(ctxT[:, 1], ctx_raw[:, 1], ctxT[:, 0], ALU.subtract).then_inc(s["csl"], 1)

            raw = wattn_raw[:, :, 1, :]
            v.wait_ge(s["wsh"], 1)
            v.scalar_tensor_tensor(wattn[:, 0, 1, :], raw[:, 0], HD ** -0.5, wattn[:, 0, 0, :],
                                   ALU.mult, ALU.subtract).then_inc(s["wsl"], 1)
            v.wait_ge(s["wsh"], 2)
            v.tensor_tensor(wattn[:, 1:4, 1, :], raw[:, 1:4], wattn[:, 1:4, 0, :], ALU.subtract
                            ).then_inc(s["wsl"], 1)
            context_lo(1)
            v.wait_ge(L["const"], 32)
            v.wait_ge(L["small"], 16 * 5)
            v.tensor_scalar(mrow[:, :], mrow8, NEG, None, ALU.mult).then_inc(s["prep"], 1)
            v.tensor_scalar(keep[:, :], mcol8[:, :], -1.0, 1.0, ALU.mult, ALU.add).then_inc(s["prep"], 1)
            v.tensor_copy(rw[:, 0, :], gates_raw).then_inc(s["rws"], 1)
            v.wait_ge(s["rws"], 1)
            v.tensor_tensor(rw[:, 1, :], gates_raw, rw[:, 0, :], ALU.subtract).then_inc(s["rws"], 1)
            v.wait_ge(s["tanh"], 1)
            for r, g in ((1, 0), (2, 1), (3, 3), (4, 3)):
                v.tensor_scalar(rows[:, r, :], rows[:, r, :], tg[:, g:g + 1], None, ALU.mult).then_inc(s["msk"], 1)
            v.tensor_scalar(bqk[:, 0, :], bqk[:, 0, :], HD ** -0.5, None, ALU.mult).then_inc(s["msk"], 1)

            def kv(l):
                if l == 1:
                    v.wait_ge(s["wsh"], 3)
                    v.tensor_tensor(wattn[:, :, 1, :], wattn_raw[:, :, 1, :], wattn[:, :, 0, :],
                                    ALU.subtract).then_inc(s["wsl"], 1)
                    context_lo(2)
                for oc in range(KC):
                    for n in range(3):
                        c = oc * 3 + n
                        lo, hi = n * KVN, min(B * SK, (n + 1) * KVN)
                        v.wait_ge(s["kcp"], 6 * l + c + 1)
                        src = ps[:, c % 2, 0:hi - lo]
                        if l == 0:
                            v.scalar_tensor_tensor(kT[:, 1, oc, lo:hi], src, bqk[:, 1, oc:oc + 1],
                                                   kT[:, 0, oc, lo:hi], ALU.add, ALU.subtract).then_inc(s["kl"], 1)
                        else:
                            v.tensor_tensor(kT[:, 1, oc, lo:hi], src, kT[:, 0, oc, lo:hi], ALU.subtract
                                            ).then_inc(s["kl"], 1)

                def heads(x):
                    return x.rearrange("s (h d) -> s h d", h=H)

                def values_lo(b):
                    hi, lo = heads(Vb[:, 0, b, :])[:, :, 0:HD], heads(vr[:, b % 2, :])
                    v.wait_ge(s["vh"], B * l + b + 1)
                    if b >= 2 or l == 1:
                        v.wait_ge(s["vp"], 2 * (B * l + b - 1))
                    if l == 0:
                        v.scalar_tensor_tensor(lo, heads(vf[:, b % 2, :]), keep[:, b:b + 1], hi, ALU.mult, ALU.subtract
                                               ).then_inc(s["vl"], 1)
                    else:
                        v.tensor_tensor(lo, heads(ps[0:SK, 2 + b % 2, 0:D]), hi, ALU.subtract).then_inc(s["vl"], 1)

                for b in range(B):
                    if l == 0:
                        v.wait_ge(s["vps"], b + 1)
                        if counted(b - 1):
                            v.wait_ge(s["vl"], b - 1)
                        v.tensor_tensor(vf[:, b % 2, :], ps[0:SK, 2 + b % 2, 0:D], rows[0:SK, 0, :], ALU.add
                                        ).then_inc(s["vf"], 1)
                        if b:
                            values_lo(b - 1)
                    else:
                        values_lo(b)
                if l == 0:
                    values_lo(B - 1)
                for k in range(3):
                    v.memset(Vb[:, k, :, :].rearrange("s b (h d) -> s b h d", h=H)[:, :, :, HD], float(k == 0)
                             ).then_inc(s["vmk"], 1)
                if l == 0:
                    v.wait_ge(s["vmk"], 3)
                    ones = Vb[:, 0, :, :].rearrange("s b (h d) -> s b h d", h=H)[:, :, :, HD]
                    v.tensor_tensor(ones, ones, keep[:, :].unsqueeze(2).to_broadcast([SK, B, H]), ALU.mult
                                    ).then_inc(s["vmk"], 1)

            def attention(l):
                base = NT * l

                def norm(t, k):
                    if counted(t + (base - 1)):
                        v.wait_ge(s["xnTps"], t + (base - 1))
                    v.tensor_scalar(xn_a[:, k % 2, :], tile_of(X, t), col(mean, t), col(rstd, t),
                                    ALU.subtract, ALU.mult).then_inc(s["xn"], 1)

                def keys(b, kb):
                    kd = Kbd[kb].rearrange("p l c (j s) -> p l c j s", j=HG)
                    for j in range(HG):
                        i = v.tensor_scalar(kd[:, :, :, j, :], span(kT, b * SK, SK), headm[:, j:j + 1],
                                            None, ALU.mult)
                    i.then_inc(s["kbd"], 1)

                def top(t):
                    v.wait_ge(s["sc"], t + (base + 1))
                    sc = ps[:, 0:4, 0:HG * SK].rearrange("p g (h s) -> p g h s", h=HG)
                    v.tensor_reduce(nmx.rearrange("p (g h) -> p g h", g=4), sc, AX.X, ALU.max).then_inc(s["mx"], 1)
                    v.wait_ge(s["mx"], t + (base + 1))

                def less(t, j):
                    if counted(2 * t + (2 * base - 1 + j)):
                        v.wait_ge(s["pl"], 2 * t + (2 * base - 1 + j))
                    sc = ps[:, 2 * j:2 * j + 2, 0:HG * SK].rearrange("p g (h s) -> p g h s", h=HG)
                    mx = nmx[:, 8 * j:8 * j + 8].rearrange("p (g h) -> p g h", g=2).unsqueeze(3)
                    v.tensor_tensor(Pf[:, 8 * j:8 * j + 8, :].rearrange("p (g h) s -> p g h s", g=2), sc,
                                    mx.to_broadcast([P, 2, HG, SK]), ALU.subtract).then_inc(s["sub"], 1)

                def out_sum(t, j):
                    v.wait_ge(s["pv"], t + (base + 1))
                    if j == 0:
                        if counted(t + base):
                            v.wait_ge(s["on"], t + base)
                    hs = slice(8, 16) if j == 0 else slice(0, 8)
                    v.tensor_reduce(o_s[:, hs, :],
                                    ps[:, 5 if j == 0 else 7, 0:24 * V1].rearrange("p (h k d) -> p h d k", h=8, k=3),
                                    AX.X, ALU.add).then_inc(s["osum"], 1)

                def out_norm(t):
                    v.wait_ge(s["osum"], 2 * t + (2 * base + 2))
                    v.reciprocal(rec, o_s[:, :, HD]).then_inc(s["rec"], 1)
                    v.wait_ge(s["rec"], t + (base + 1))
                    v.tensor_tensor(o_a.rearrange("p (h d) -> p h d", h=H), o_s[:, :, 0:HD],
                                    rec.unsqueeze(2).to_broadcast([P, H, HD]), ALU.mult).then_inc(s["on"], 1)

                def o_lo(t):
                    v.wait_ge(s["oT"], t + (base + 1))
                    v.tensor_tensor(oT[:, 1], ps[:, 7, 0:D].rearrange("p (k t) -> p k t", k=KC), oT[:, 0],
                                    ALU.subtract).then_inc(s["ol"], 1)

                def x_lo(t):
                    v.wait_ge(s["xnT"], t + (base + 1))
                    v.tensor_tensor(xnT_a[:, 1], ps[:, 6, 0:D].rearrange("p (k t) -> p k t", k=KC), xnT_a[:, 0],
                                    ALU.subtract).then_inc(s["xl"], 1)

                def q_lo(t):
                    v.wait_ge(s["q"], t + (base + 1))
                    if l == 0:
                        for oc in range(KC):
                            i = v.scalar_tensor_tensor(qT[:, 1, oc, :], ps[:, 6, D + oc * P:D + (oc + 1) * P],
                                                       bqk[:, 0, oc:oc + 1], qT[:, 0, oc, :], ALU.add, ALU.subtract)
                    else:
                        i = v.scalar_tensor_tensor(qT[:, 1].rearrange("p k t -> p (k t)"), ps[:, 6, D:2 * D],
                                                   HD ** -0.5, qT[:, 0].rearrange("p k t -> p (k t)"),
                                                   ALU.mult, ALU.subtract)
                    i.then_inc(s["ql"], 1)

                def residual(t):
                    v.wait_ge(s["y"], t + (base + 1))
                    v.scalar_tensor_tensor(tile_of(X, t), ps[:, 7, 0:D], tg[:, l:l + 1], tile_of(X, t),
                                           ALU.mult, ALU.add).then_inc(s["res"], 1)

                def moments(t):
                    v.wait_ge(s["res2"], t + (base + 1))
                    v.bn_stats(tile_of(bnraw, t), tile_of(X, t)).then_inc(s["bn"], 1)

                kv(l)
                v.wait_ge(s["kl"], 6 * (l + 1))
                keys(0, 0)
                v.wait_ge(s["statc"], 1 + 2 * l)
                norm(0, 0)
                norm(1, 1)
                x_lo(0)
                q_lo(0)

                def step(t, k, b=None, n=True, c=True, x=True, m=True, nn=True):
                    if x:
                        top(t)
                    if n:
                        x_lo(t + 1)
                    if c:
                        out_sum(t + (-2), 0)
                    if x:
                        less(t, 0)
                    if c:
                        out_sum(t + (-2), 1)
                        out_norm(t + (-2))
                    if x:
                        less(t, 1)
                    if n:
                        q_lo(t + 1)
                    if b is not None:
                        keys(b, (k // TB + 1) % 2)
                    if c:
                        o_lo(t + (-2))
                        residual(t + (-2))
                    if nn:
                        norm(t + 2, k)
                    if m:
                        moments(t + (-3))

                for k in range(4):
                    step(k, k, b=k // TB + 1 if k % TB == TB - 1 else None, c=k >= 2, m=k >= 3)
                with v.Fori(2, (NT - 4) // TB, 2) as b0:
                    for k in range(4):
                        step(b0 * TB + k, k, b=b0 + (k // TB + 1) if k % TB == TB - 1 else None)
                for t in range(NT - 4, NT + 2):
                    k = t % 4
                    b = t // TB + 1
                    step(t, k, b=b if k % TB == TB - 1 and b < B else None, n=t + 1 < NT, x=t < NT, nn=t + 2 < NT)
                moments(NT - 1)

            def group_norm(g, done, dst):
                if counted(KC * done):
                    v.wait_ge(s["fxTps"], KC * done)
                for k in range(GT):
                    t = g * GT + k
                    i = v.tensor_scalar(dst[:, k, :], tile_of(X, t), col(mean, t), col(rstd, t),
                                        ALU.subtract, ALU.mult)
                i.then_inc(s["fxn"], 1)

            def group_lo(n, dst=xT, first_bank=0):
                for kc in range(KC):
                    v.wait_ge(s["fxT"], n + (kc + 1))
                    v.tensor_tensor(dst[:, 1, kc, :], bank(first_bank + kc), dst[:, 0, kc, :], ALU.subtract
                                    ).then_inc(s["fxl"], 1)

            def choose(R, T, E, src, bias, pr, code, sem_step, sem_exp, c0, x0, out_sel):
                def sh(x):
                    return x[:, 0:T * E].rearrange("p (t e) -> p t e", t=T)

                def bcast(k):
                    return rm[:, k, 0:T].unsqueeze(2).to_broadcast([P, T, E])

                ra, rb = sh(R["a"]), sh(R["b"])
                oh1, oh2 = sh(R["oh1"]), sh(R["oh2"])
                cb = code.unsqueeze(1).to_broadcast([P, T, E])
                c = 0

                def link(i):
                    nonlocal c
                    c += 1
                    i.then_inc(s[sem_step], 1)
                    v.wait_ge(s[sem_step], c0 + c)

                if bias is not None:
                    link(v.tensor_tensor(src, src, bias, ALU.add))
                link(v.tensor_reduce(rm[:, 0, 0:T], src, AX.X, ALU.max))
                link(v.tensor_tensor(ra, src, bcast(0), ALU.subtract))
                v.wait_ge(s[sem_exp], x0)
                link(v.tensor_reduce(rm[:, 1, 0:T], ra, AX.X, ALU.add))
                link(v.reciprocal(rm[:, 2, 0:T], rm[:, 1, 0:T]))
                link(v.tensor_tensor(pr, ra, bcast(2), ALU.mult))
                link(v.tensor_reduce(rm[:, 3, 0:T], pr, AX.X, ALU.max))
                link(v.tensor_tensor(rb, pr, bcast(3), ALU.is_equal))
                link(v.tensor_tensor(rb, rb, cb, ALU.mult))
                link(v.tensor_reduce(rm[:, 3, 0:T], rb, AX.X, ALU.max))
                link(v.tensor_tensor(oh1, cb, bcast(3), ALU.is_equal))
                link(v.scalar_tensor_tensor(ra, oh1, -2.0, pr, ALU.mult, ALU.add))
                link(v.tensor_reduce(rm[:, 4, 0:T], ra, AX.X, ALU.max))
                link(v.tensor_tensor(rb, ra, bcast(4), ALU.is_equal))
                link(v.tensor_tensor(rb, rb, cb, ALU.mult))
                link(v.tensor_reduce(rm[:, 4, 0:T], rb, AX.X, ALU.max))
                link(v.tensor_tensor(oh2, cb, bcast(4), ALU.is_equal))
                link(v.tensor_tensor(out_sel, oh1, oh2, ALU.add))
                return c

            def feed0(g, next_norm=None):
                group_lo(KC * g)
                v.wait_ge(s["lps"], g + 1)
                src = ps[:, 7, 0:GT * E0].rearrange("p (t e) -> p t e", t=GT)
                c = choose(R0, GT, E0, src, None, prob[:, :, :], codes[:, 0, 0:E0], "rst", "rex",
                           RSTEPS * g, g + 1, chosen[:, :, :])
                assert c == RSTEPS
                v.tensor_tensor(prob[:, :, :], prob[:, :, :], chosen[:, :, :], ALU.mult).then_inc(s["rws"], 1)
                v.wait_ge(s["rws"], 2 * g + 3)
                v.scalar_tensor_tensor(prob[:, :, :], chosen[:, :, :], -1.0, prob[:, :, :], ALU.add, ALU.add
                                       ).then_inc(s["rws"], 1)
                v.wait_ge(s["rws"], 2 * g + 4)
                pf = prob[:, :, :]
                ph, pm, pl = (psp[:, :, E0 * k:E0 * k + E0] for k in range(3))
                r1 = prs[:, 0, :].rearrange("p (t e) -> p t e", t=GT)
                r2 = prs[:, 1, :].rearrange("p (t e) -> p t e", t=GT)
                for k, i in enumerate((lambda: v.tensor_copy(ph, pf), lambda: v.tensor_tensor(r1, pf, ph, ALU.subtract),
                                       lambda: v.tensor_copy(pm, r1), lambda: v.tensor_tensor(r2, r1, pm, ALU.subtract),
                                       lambda: v.tensor_copy(pl, r2))):
                    i().then_inc(s["sel0"], 1)
                    v.wait_ge(s["sel0"], 5 * g + k + 1)
                for ic in range(5):
                    if ic < 4:
                        v.wait_ge(s["gB"], 4 * g + ic + 1)
                        v.wait_ge(s["gAs"], 4 * g + ic + 1)
                        if counted(4 * g + ic - 1):
                            v.wait_ge(s["gGl"], 4 * g + ic - 1)
                        v.tensor_tensor(swf[:, ic % 2, :], sil[:, ic % 2, :], bank(2 * (ic % 2) + 1), ALU.mult
                                        ).then_inc(s["gG"], 1)
                    if ic >= 1:
                        v.wait_ge(s["gGh"], 4 * g + ic)
                        v.tensor_tensor(swi[:, 1, ic - 1, :], swf[:, (ic - 1) % 2, :], swi[:, 0, ic - 1, :],
                                        ALU.subtract).then_inc(s["gGl"], 1)
                for e in range(E0):
                    n = g * E0 + e
                    v.wait_ge(s["pb"], n + 1)
                    if counted(2 * n):
                        v.wait_ge(s["hh"], 2 * n)
                    if e == 0:
                        v.wait_ge(s["zps"], 2 * g + 2)
                    if counted(2 * n):
                        v.wait_ge(s["hl"], 2 * n)
                    for oc in range(KC):
                        v.wait_ge(s["ups"], 2 * n + oc + 1)
                        v.tensor_tensor(u[:, oc, :], bank(oc), pb[:, e % 2, :], ALU.mult).then_inc(s["u"], 1)
                    if counted(2 * n):
                        v.wait_ge(s["x3m"], 2 * n)
                    v.tensor_scalar(mb, pb[:, e % 2, :], 0.0, None, ALU.is_ge).then_inc(s["mb"], 1)
                    for oc in range(KC):
                        v.wait_ge(s["x3ps"], 2 * n + oc + 1)
                        if not (isinstance(g, int) and g == 0 and e == 0):
                            v.wait_ge(s["x23"], 2 * n - 1 + oc)
                        v.tensor_tensor(x3[:, oc, :], bank(2 + oc), pb[:, e % 2, :], ALU.mult).then_inc(s["x3"], 1)
                        v.wait_ge(s["hh"], 2 * n + oc + 1)
                        v.tensor_tensor(h[:, 1, oc, :], u[:, oc, :], h[:, 0, oc, :], ALU.subtract
                                        ).then_inc(s["hl"], 1)
                    v.wait_ge(s["mb"], n + 1)
                    for oc in range(KC):
                        v.wait_ge(s["x3"], 2 * n + oc + 1)
                        v.scalar_tensor_tensor(x3[:, oc, :], x3[:, oc, :], b23c[:, 1, e, oc:oc + 1], mb,
                                               ALU.add, ALU.mult).then_inc(s["x3m"], 1)
                    for oc in range(KC):
                        v.wait_ge(s["x2ps"], 2 * n + oc + 1)
                        if not (isinstance(g, int) and g == 0 and e == 0):
                            v.wait_ge(s["acc"], 2 * n - 1 + oc)
                        v.wait_ge(s["x3m"], 2 * n + oc + 1)
                        v.scalar_tensor_tensor(x23[:, oc, :], bank(4 + oc), b23c[:, 0, e, oc:oc + 1], x3[:, oc, :],
                                               ALU.add, ALU.mult).then_inc(s["x23"], 1)
                    if e == E0 - 2 and next_norm is not None:
                        group_norm(next_norm, next_norm, xn4)
                v.wait_ge(s["yps0"], g + 1)
                xg = group_of(X, g)
                v.scalar_tensor_tensor(xg, ps[:, 0:2, :].rearrange("p b (t d) -> p (b t) d", t=2), tg[:, 2:3], xg,
                                       ALU.mult, ALU.add).then_inc(s["fres"], 1)
                v.wait_ge(s["fres"], g + 1)
                for k in range(GT):
                    t = g * GT + k
                    v.bn_stats(tile_of(bnraw, t), tile_of(X, t)).then_inc(s["fbn"], 1)

            v.wait_ge(L["x"], 32)
            v.bn_stats(bnraw[:, 0, :], X[:, 0, :]).then_inc(s["bn"], 1)
            with v.Fori(1, NT) as t:
                v.bn_stats(tile_of(bnraw, t), tile_of(X, t)).then_inc(s["bn"], 1)
            v.wait_ge(s["bn"], NT)
            stats(1)
            attention(0)
            v.wait_ge(s["bn"], 2 * NT)
            stats(2)
            v.wait_ge(s["statc"], 2)
            group_norm(0, 0, xn4)
            feed0(0, 1)
            with v.Fori(1, NG - 1) as g:
                feed0(g, g + 1)
            feed0(NG - 1)
            v.wait_ge(s["fbn"], NT)
            stats(3)
            attention(1)
            v.wait_ge(s["bn"], 3 * NT)
            stats(4)
            v.wait_ge(s["statc"], 4)

            def router1(g, k):
                group_lo(KC * g + KC * NG, (xT, xTb)[k], 2 * k)
                v.wait_ge(s["lgps"], g + 1)
                v.tensor_copy(span(lg, g * (GT * E1), GT * E1), ps[:, 6 + k, 0:GT * E1]).then_inc(s["lgc"], 1)

            group_norm(0, NG, xn4)
            group_norm(1, NG, xn4b)
            with v.Fori(0, NG // 2 - 1) as pair:
                for k in range(2):
                    group_norm(pair * 2 + (2 + k), pair * 2 + (NG + k + 1), (xn4, xn4b)[k])
                    router1(pair * 2 + k, k)
            router1(NG - 2, 0)
            router1(NG - 1, 1)
            v.wait_ge(s["lgc"], NG)
            lg3 = lg.rearrange("p (t e) -> p t e", t=NT)
            pr3 = R1["p"].rearrange("p (t e) -> p t e", t=NT)
            choose(R1, NT, E1, lg3, bgr.unsqueeze(1).to_broadcast([P, NT, E1]), pr3, codes[:, 1, :],
                   "rst1", "rex1", 0, 1, R1["a"].rearrange("p (t e) -> p t e", t=NT))
            v.tensor_tensor(R1["b"], R1["a"], R1["p"], ALU.mult).then_inc(s["rst1"], 1)
            group_norm(0, 2 * NG, xn4)
            v.wait_ge(s["dps"], 1)
            v.tensor_scalar(rden, ps[:, 6, 0:S], EPS_GATE, None, ALU.add).then_inc(s["tk"], 1)
            v.wait_ge(s["tk"], 1)
            v.reciprocal(rden, rden).then_inc(s["tk"], 1)
            v.wait_ge(s["tk"], 2)
            for j in range(2):
                v.scalar_tensor_tensor(route[:, j, :], route[:, j, :], float(B), rden, ALU.mult, ALU.mult
                                       ).then_inc(s["tk"], 1)
            n = 4
            for r in range(TOP // 8):
                v.wait_ge(s["tk"], n)
                for j in range(2):
                    v.max(top8[:, j, :], route[:, j, :]).then_inc(s["tk"], 1)
                n += 2
                v.wait_ge(s["tk"], n)
                for j in range(2):
                    v.match_replace(route[:, j, :], top8[:, j, :], route[:, j, :], -1.0).then_inc(s["tk"], 1)
                n += 2
            v.wait_ge(s["tk"], n)
            v.tensor_scalar(selb, route, 0.0, None, ALU.is_lt).then_inc(s["sel"], 1)

            v.wait_ge(L["late"], 32)
            v.tensor_copy(b2s[:, 0, :], b2f).then_inc(s["b2"], 1)
            v.wait_ge(s["b2"], 1)
            v.tensor_tensor(b2r[:, 0, :], b2f, b2s[:, 0, :], ALU.subtract).then_inc(s["b2"], 1)
            v.wait_ge(s["b2"], 2)
            v.tensor_copy(b2s[:, 1, :], b2r[:, 0, :]).then_inc(s["b2"], 1)
            v.wait_ge(s["b2"], 3)
            v.tensor_tensor(b2r[:, 1, :], b2r[:, 0, :], b2s[:, 1, :], ALU.subtract).then_inc(s["b2"], 1)
            v.wait_ge(s["b2"], 4)
            v.tensor_copy(b2s[:, 2, :], b2r[:, 1, :]).then_inc(s["b2"], 1)

            def feed1(g, next_norm=None):
                group_lo(KC * g + 2 * KC * NG)
                for c in range(C1):
                    m = g * C1 + c
                    v.wait_ge(s["gelu"], m + 1)
                    v.wait_ge(s["mps"], m + 1)
                    if counted(m - 1):
                        v.wait_ge(s["hml"], m - 1)
                    v.tensor_tensor(hmf[:, c % 2, :], hgf[:, c % 2, :], bank(2 + c % 2), ALU.mult
                                    ).then_inc(s["hm"], 1)
                    v.wait_ge(s["hmh"], m + 1)
                    v.tensor_tensor(hm[:, c % 2, 1, :], hmf[:, c % 2, :], hm[:, c % 2, 0, :],
                                    ALU.subtract).then_inc(s["hml"], 1)
                v.wait_ge(s["yps"], g + 1)
                v.tensor_tensor(z, xn4, ps[:, 4:8, 0:D], ALU.add).then_inc(s["z"], 1)
                v.wait_ge(s["z"], g + 1)
                for k in range(GT):
                    i = v.bn_stats(zraw[:, k, :], z[:, k, :])
                i.then_inc(s["zbn"], 1)
                v.wait_ge(s["zbn"], g + 1)
                me, qe, mo, qo = zraw[:, :, 1], zraw[:, :, 2], zraw[:, :, 4], zraw[:, :, 5]

                def link(i, k):
                    i.then_inc(s["zst"], 1)
                    v.wait_ge(s["zst"], 5 * g + k)

                link(v.tensor_tensor(zs[:, 0, :], me, mo, ALU.subtract), 1)
                link(v.tensor_tensor(zs[:, 1, :], zs[:, 0, :], zs[:, 0, :], ALU.mult), 2)
                link(v.tensor_tensor(zs[:, 2, :], qe, qo, ALU.add), 3)
                link(v.scalar_tensor_tensor(zs[:, 0, :], zs[:, 1, :], D / 4.0, zs[:, 2, :], ALU.mult, ALU.add), 4)
                v.tensor_tensor(zs[:, 1, :], me, mo, ALU.add).then_inc(s["zmn"], 1)
                link(v.tensor_scalar(zs[:, 3, :], zs[:, 0, :], 1.0 / D, EPS, ALU.mult, ALU.add), 5)
                v.wait_ge(s["zmn"], 2 * g + 1)
                v.tensor_scalar(zmean, zs[:, 1, :], 0.5, None, ALU.mult).then_inc(s["zmn"], 1)
                if next_norm is not None:
                    group_norm(next_norm, next_norm + 2 * NG, xn4)
                xg = group_of(X, g)
                v.tensor_tensor(xg, xg, rows[:, 4, :].unsqueeze(1).to_broadcast([P, GT, D]), ALU.add
                                ).then_inc(s["zo"], 1)
                v.wait_ge(s["zpow"], g + 1)
                v.wait_ge(s["zmn"], 2 * g + 2)
                for k in range(GT):
                    i = v.tensor_scalar(z[:, k, :], z[:, k, :], zmean[:, k:k + 1], zrstd[:, k:k + 1],
                                        ALU.subtract, ALU.mult)
                i.then_inc(s["zn"], 1)
                v.wait_ge(s["zn"], 2 * g + 1)
                v.tensor_tensor(z, z, rows[:, 3, :].unsqueeze(1).to_broadcast([P, GT, D]), ALU.mult
                                ).then_inc(s["zn"], 1)
                v.wait_ge(s["zn"], 2 * g + 2)
                v.tensor_tensor(xg, xg, z, ALU.add).then_inc(s["zo"], 1)

            feed1(0, 1)
            with v.Fori(1, NG - 1) as g:
                feed1(g, g + 1)
            feed1(NG - 1)

        @block.tensor
        def _(pe):
            def product(dst, terms, mid=False):
                n = 0
                for wpart, xpart in terms:
                    for i, j in PARTS:
                        r = pe.matmul(dst, wpart(i), xpart(j), start=(n == 0),
                                      stop=(not mid and n == 3 * len(terms) - 1))
                        n += 1
                return r

            def cols(w, kc, oc, width=D):
                return w[:, kc * width + oc * P:kc * width + (oc + 1) * P]

            def wa(k, i, kc, oc):
                return cols(wattn[:, k, i, :], kc, oc)

            pe.wait_ge(s["cst"], 3)
            pe.wait_ge(s["wsl"], 2)
            pe.wait_ge(s["csl"], 1)

            def kv(l):
                pe.wait_ge(s["csl"], l + 1)
                for oc in range(KC):
                    for n in range(3):
                        c = oc * 3 + n
                        lo, hi = n * KVN, min(B * SK, (n + 1) * KVN)
                        if c >= 2:
                            pe.wait_ge(s["kl"], 6 * l + c - 1)
                        product(ps[:, c % 2, 0:hi - lo],
                                [(lambda i, kc=kc: wa(1, i, kc, oc),
                                  lambda j, kc=kc: ctxT[:, j, kc, lo:hi]) for kc in range(KC)]).then_inc(s["kps"], 1)
                for b in range(B):
                    if b >= 2:
                        if l == 0:
                            pe.wait_ge(s["vf"], b - 1)
                        else:
                            pe.wait_ge(s["vl"], B * l + b - 1)
                    product(ps[0:SK, 2 + b % 2, 0:D],
                            [(lambda i, kc=kc: ctxT[:, i, kc, b * SK:(b + 1) * SK],
                              lambda j, kc=kc: wattn[:, 2, j, kc * D:(kc + 1) * D]) for kc in range(KC)]).then_inc(s["vps"], 1)

            def attention(l):
                base = NT * l

                def turn(t, k):
                    pe.wait_ge(s["xn"], t + (base + 1))
                    if counted(t + base):
                        pe.wait_ge(s["ql"], t + base)
                    for kc in range(KC):
                        i = pe.transpose(ps[:, 6, kc * P:(kc + 1) * P], xn_a[:, k % 2, kc * P:(kc + 1) * P], ident)
                    i.then_inc(s["xnTps"], 1)

                def query(t):
                    pe.wait_ge(s["xl"], t + (base + 1))
                    for oc in range(KC):
                        i = product(ps[:, 6, D + oc * P:D + (oc + 1) * P],
                                    [(lambda i, kc=kc: wa(0, i, kc, oc),
                                      lambda j, kc=kc: xnT_a[:, j, kc, :]) for kc in range(KC)])
                    i.then_inc(s["qps"], 1)

                def scores(t, k, b):
                    pe.wait_ge(s["ql"], t + (base + 1))
                    if counted(2 * t + 2 * base):
                        pe.wait_ge(s["sub"], 2 * t + 2 * base)
                    pe.wait_ge(s["kbd"], b + (B * l + 1))
                    for g in range(4):
                        c, r = g // 2, 64 * (g % 2)
                        dst = ps[:, g, 0:HG * SK]
                        i = product(dst, [(lambda i: qT[r:r + 64, i, c, :],
                                           lambda j: Kbd[(k // TB) % 2][r:r + 64, j, c, :])], mid=(l == 0))
                        if l == 0:
                            i = pe.matmul(dst, ones1[:, :],
                                          span(mrow[:, :], b * SK, SK).unsqueeze(1).to_broadcast([1, HG, SK]),
                                          start=False, stop=True)
                    i.then_inc(s["sc"], 1)

                def turn_probs(t, k, g):
                    pe.wait_ge(s["pl"], 2 * t + (2 * base + 1 + g // 2))
                    if counted(4 * t + (4 * base + g - 1)):
                        pe.wait_ge(s["pt"], 4 * t + (4 * base + g - 1))
                    if g == 1:
                        if counted(2 * t + (2 * base - 1)):
                            pe.wait_ge(s["osum"], 2 * t + (2 * base - 1))
                    dst = ps[0:SK, 4 + g % 2, :].bitcast(F16)
                    for part in range(2):
                        for j in range(4):
                            at_ = (part * 4 + j) * P
                            i = pe.transpose(dst[:, at_:at_ + P], Phl[k % 2][:, part, 4 * g + j, :], identh[:, :])
                    i.then_inc(s["ptps"], 1)

                def weigh(t, k, b):
                    if counted(t + base):
                        pe.wait_ge(s["res"], t + base)
                    pe.wait_ge(s["vc"], b + (B * l + 1))
                    pe.wait_ge(s["pt"], 4 * t + (4 * base + 4))
                    for hh in range(H):
                        o, vc = (hh % 8) * 3 * V1, Vc[(k // TB) % 2]
                        bk = 7 if hh < 8 else 5
                        pe.matmul(ps[:, bk, o:o + 3 * V1], PT[:, hh // 4, 0, hh % 4, :],
                                  vc[:, hh].rearrange("s k d -> s (k d)"), start=True, stop=False)
                        i = pe.matmul(ps[:, bk, o:o + 2 * V1], PT[:, hh // 4, 1, hh % 4, :],
                                      vc[:, hh, 0:2].rearrange("s k d -> s (k d)"), start=False, stop=True)
                    i.then_inc(s["pv"], 1)

                def turn_out(t):
                    pe.wait_ge(s["on"], t + (base + 1))
                    for kc in range(KC):
                        i = pe.transpose(ps[:, 7, kc * P:(kc + 1) * P], o_a[:, kc * P:(kc + 1) * P], ident)
                    i.then_inc(s["oTps"], 1)

                def project(t):
                    pe.wait_ge(s["ol"], t + (base + 1))
                    product(ps[:, 7, 0:D], [(lambda i, kc=kc: oT[:, i, kc, :], lambda j, kc=kc: wattn[:, 3, j, kc * D:(kc + 1) * D])
                                            for kc in range(KC)]).then_inc(s["y"], 1)

                kv(l)
                pe.wait_ge(s["vmk"], 4 if l == 0 else 7)
                pe.wait_ge(s["vp"], 2 * B * (l + 1))
                pe.wait_ge(s["vl"], B * (l + 1))
                pe.wait_ge(s["kl"], 6 * (l + 1))
                turn(0, 0)
                query(0)

                def step(t, k, b, bp, n=True, c=True, x=True, w=True):
                    if x:
                        scores(t, k, b)
                    if n:
                        turn(t + 1, k + 1)
                    if c:
                        weigh(t + (-2), (k + 2) % 4, bp)
                    if w:
                        turn_probs(t + (-1), k + 1, 0)
                    if n:
                        query(t + 1)
                    if w:
                        turn_probs(t + (-1), k + 1, 1)
                        turn_probs(t + (-1), k + 1, 2)
                    if c:
                        turn_out(t + (-2))
                    if w:
                        turn_probs(t + (-1), k + 1, 3)
                    if c:
                        project(t + (-2))

                for k in range(4):
                    step(k, k, k // TB, (k - 2) // TB, w=k >= 1, c=k >= 2)
                with pe.Fori(2, (NT - 4) // TB, 2) as b0:
                    for k in range(4):
                        step(b0 * TB + k, k, b0 + k // TB, b0 + (k - 2) // TB)
                for t in range(NT - 4, NT + 2):
                    step(t, t % 4, t // TB, (t - 2) // TB, n=t + 1 < NT, x=t < NT, w=t <= NT)

            def turn_group(n, src, first_bank):
                pe.wait_ge(s["fxn"], n + 1)
                for kc in range(KC):
                    for k in range(GT):
                        i = pe.transpose(ps[:, first_bank + kc, k * P:(k + 1) * P], src[:, k, kc * P:(kc + 1) * P], ident)
                    i.then_inc(s["fxTps"], 1)

            def logits(bk, w, E, x):
                for k in range(GT):
                    i = product(ps[:, bk, k * E:(k + 1) * E],
                                [(lambda i, kc=kc: x[:, i, kc, k * P:(k + 1) * P], lambda j, kc=kc: w[:, j, kc, :])
                                 for kc in range(KC)])
                return i

            def feed0(g, first=False):
                if counted(2 * E0 * g):
                    pe.wait_ge(s["u"], 2 * E0 * g)
                if counted(g):
                    pe.wait_ge(s["fres"], g)
                turn_group(g, xn4, 0)
                pe.wait_ge(s["fxl"], KC * g + KC)
                logits(7, gatew, E0, xT).then_inc(s["lps"], 1)
                if first:
                    pe.wait_ge(s["sl"], 2)
                for ic in range(4):
                    if ic >= 2:
                        pe.wait_ge(s["gG"], 4 * g + ic - 1)
                    elif ic == 1:
                        if counted(2 * E0 * g):
                            pe.wait_ge(s["x3"], 2 * E0 * g)
                    for half in range(2):
                        product(bank(2 * (ic % 2) + half),
                                [(lambda i, kc=kc: cols(sw12[:, half, i, :], kc, ic, I0),
                                  lambda j, kc=kc: xT[:, j, kc, :]) for kc in range(KC)]
                                ).then_inc(s["gA" if half == 0 else "gB"], 1)
                pe.wait_ge(s["sel0"], 5 * g + 5)
                if counted(E0 * g):
                    pe.wait_ge(s["pb"], E0 * g)
                pv = ps[0:3 * E0, 6, 0:GN // 2].bitcast(BF16)
                for k in range(GT):
                    i = pe.transpose(pv[:, k * P:(k + 1) * P], psp[:, k, :], identb[:, :])
                i.then_inc(s["pTps"], 1)

                def up(e):
                    n = g * E0 + e
                    if first:
                        pe.wait_ge(s["wl"], 2 * e + 2)
                    if counted(n):
                        pe.wait_ge(s["pb"], n)
                    pe.matmul(bank(6), selp[:, e, :], pT[:, :], start=True, stop=True).then_inc(s["pps"], 1)
                    if counted(2 * n):
                        pe.wait_ge(s["u"], 2 * n)
                    for oc in range(KC):
                        product(bank(oc), [(lambda i, kc=kc: cols(w0[:, e, 0, i, :], kc, oc),
                                            lambda j, kc=kc: xT[:, j, kc, :]) for kc in range(KC)]
                                ).then_inc(s["ups"], 1)

                if first:
                    pe.wait_ge(s["sl"], 4)
                pe.wait_ge(s["gGl"], 4 * g + 4)
                if counted(2 * E0 * g):
                    pe.wait_ge(s["x23"], 2 * E0 * g)
                for oc in range(KC):
                    product(bank(4 + oc), [(lambda i, ic=ic: cols(sw3[:, i, :], ic, oc),
                                            lambda j, ic=ic: swi[:, j, ic, :]) for ic in range(4)]
                            ).then_inc(s["zps"], 1)
                pe.wait_ge(s["pTc"], g + 1)
                pe.wait_ge(s["gG"], 4 * g + 4)
                up(0)
                for e in range(E0):
                    n = g * E0 + e
                    if counted(2 * n):
                        pe.wait_ge(s["x3"], 2 * n)
                    for oc in range(KC):
                        product(bank(2 + oc), [(lambda i, kc=kc: cols(w0[:, e, 2, i, :], kc, oc),
                                                lambda j, kc=kc: xT[:, j, kc, :]) for kc in range(KC)]
                                ).then_inc(s["x3ps"], 1)
                    if e + 1 < E0:
                        up(e + 1)
                    pe.wait_ge(s["hl"], 2 * n + 2)
                    if counted(2 * n):
                        pe.wait_ge(s["x23"], 2 * n)
                    if e == 0:
                        pe.wait_ge(s["zcp"], 2 * g + 2)
                    for oc in range(KC):
                        product(bank(4 + oc), [(lambda i, kc=kc: cols(w0[:, e, 1, i, :], kc, oc),
                                                lambda j, kc=kc: h[:, j, kc, :]) for kc in range(KC)]
                                ).then_inc(s["x2ps"], 1)
                pe.wait_ge(s["acc"], 2 * E0 * g + 2 * E0)
                for k in range(GT):
                    for oc in range(KC):
                        i = pe.transpose(ps[:, k // 2, (k % 2) * D + oc * P:(k % 2) * D + (oc + 1) * P],
                                         yT[:, oc, k * P:(k + 1) * P], ident)
                i.then_inc(s["yps0"], 1)

            attention(0)
            pe.wait_ge(s["rws"], 2)
            feed0(0, first=True)
            with pe.Fori(1, NG) as g:
                feed0(g)
            pe.wait_ge(s["wsl"], 3)
            pe.wait_ge(s["fres"], NG)
            attention(1)

            def router1(g, k):
                pe.wait_ge(s["fxl"], KC * g + (KC * NG - KC))
                turn_group(g + NG, (xn4, xn4b)[k], 2 * k)
                pe.wait_ge(s["fxl"], KC * g + (KC * NG + KC))
                if counted(g + (-1)):
                    pe.wait_ge(s["lgc"], g + (-1))
                logits(6 + k, wg, E1, (xT, xTb)[k]).then_inc(s["lgps"], 1)

            router1(0, 0)
            router1(1, 1)
            with pe.Fori(2, NG, 2) as g:
                router1(g, 0)
                router1(g + 1, 1)
            pe.wait_ge(s["rst1"], RSTEPS + 2)
            for k in range(NT // 4):
                if counted(k - 1):
                    pe.wait_ge(s["smc"], k - 1)
                for j in range(4):
                    t = 4 * k + j
                    i = pe.transpose(ps[0:E1, 4 + k % 2, j * P:(j + 1) * P], R1["b"][:, t * E1:(t + 1) * E1], ident)
                i.then_inc(s["smps"], 1)
            pe.wait_ge(s["rt"], 16 * B)
            for j in range(2):
                i = pe.matmul(ps[:, 6, 0:S], same_e, route[:, j, :], start=(j == 0), stop=(j == 1))
            i.then_inc(s["dps"], 1)
            pe.wait_ge(s["wl"], 2 * E0 + 4)
            pe.wait_ge(s["b2"], 5)
            pe.wait_ge(L["late"], 32)
            pe.wait_ge(s["tk"], 1)

            def feed1(g):
                turn_group(g + 2 * NG, xn4, 0)
                pe.wait_ge(s["fxl"], KC * g + (2 * KC * NG + KC))
                pe.wait_ge(s["selg"], g + 1)

                def hidden(c, m):
                    if counted(m - 1):
                        pe.wait_ge(s["gelu"], m - 1)
                    product(bank(c % 2), [(lambda i, kc=kc: cols(w1f[:, i, :], kc, c, E1 * F1),
                                           lambda j, kc=kc: xT[:, j, kc, :]) for kc in range(KC)]
                            ).then_inc(s["hps"], 1)
                    if counted(m - 1):
                        pe.wait_ge(s["hm"], m - 1)
                    pe.matmul(bank(2 + c % 2), selh[:, c, :], selg, start=True, stop=True).then_inc(s["mps"], 1)

                def down(c, m):
                    pe.wait_ge(s["hml"], m + 1)
                    if c == 0:
                        if counted(g):
                            pe.wait_ge(s["z"], g)
                    for k in range(GT):
                        for i, j in PARTS:
                            r = pe.matmul(ps[:, 4 + k, 0:D], hm[:, c % 2, i, k * P:(k + 1) * P],
                                          w2f[:, j, c * D:(c + 1) * D], start=(c == 0 and (i, j) == PARTS[0]), stop=False)
                    r.then_inc(s["hmr"], 1)

                hidden(0, g * C1)
                hidden(1, g * C1 + 1)
                for c in range(C1):
                    if c + 2 < C1:
                        hidden(c + 2, g * C1 + (c + 2))
                    down(c, g * C1 + c)
                for k in range(GT):
                    for j in range(3):
                        i = pe.matmul(ps[:, 4 + k, 0:D], selg[:, k * P:(k + 1) * P], b2s[:, j, :],
                                      start=False, stop=(j == 2))
                i.then_inc(s["yps"], 1)

            feed1(0)
            with pe.Fori(1, NG) as g:
                feed1(g)


def kernel(**inputs):
    import numpy as np
    import concourse.bacc as _bacc
    from concourse.bass_utils import run_bass_kernel_spmd as _run

    def n(k):
        return np.ascontiguousarray(inputs[k])

    def chunks(w):
        return np.ascontiguousarray(np.moveaxis(w.reshape((w.shape[0] // P, P) + w.shape[1:]), 0, 1))

    f = np.float32
    arrays = {}
    arrays["x"] = np.ascontiguousarray(n("x").reshape(NT, P, D).transpose(1, 0, 2))
    arrays["ctxT"] = chunks(n("ctx_1024").reshape(B * SK, D).T)
    mask = n("mask_BxS2_bf0")
    arrays["mrow"] = mask.reshape(1, B * SK)
    arrays["mcol"] = np.ascontiguousarray(mask.T)
    for l, ks in ((0, ("wq", "wk", "wv", "wo")), (1, ("Wq", "Wk", "Wv", "Wo"))):
        arrays[f"wattn{l}"] = np.ascontiguousarray(
            np.stack([chunks(n(f"L{l}_xattn_{k}").T).reshape(P, KC * D) for k in ks], axis=1))
    vectors = [n("L0_xattn_bv"), n("L0_xattn_bo"), n("L1_xattn_bo"), n("L1_ffn_gamma"), n("L1_ffn_beta"),
               n("L1_ffn_bg"), n("g_xattn"), n("g_ffn")]
    arrays["bc"] = np.concatenate(vectors).reshape(1, BCST)
    w0 = np.stack([chunks(n(f"L0_ffn_{k}").transpose(2, 0, 1)).transpose(0, 2, 1, 3) for k in ("w1", "w2", "w3")],
                  axis=2)
    arrays["feed0"] = w0.reshape(P, E0, 3, KC * D)
    arrays["sw12"] = np.stack([chunks(n("L0_ffn_sw1").T), chunks(n("L0_ffn_sw2").T)], axis=1).reshape(P, 2, KC * I0)
    arrays["sw3"] = chunks(n("L0_ffn_sw3").T).reshape(P, -1)
    arrays["w1f"] = chunks(n("L1_ffn_w1").transpose(1, 0, 2).reshape(D, E1 * F1)).reshape(P, -1)
    arrays["w2f"] = chunks(n("L1_ffn_w2").reshape(E1 * F1, D)).reshape(P, -1)
    arrays["b2f"] = n("L1_ffn_b2")
    r = np.arange(P)
    codes = np.zeros((P, 2, E1), f)
    codes[:, 0, :E0] = E0 - np.arange(E0)
    codes[:, 1, :] = E1 - np.arange(E1)
    bqk = np.stack([n("L0_xattn_bq").reshape(KC, P).T, n("L0_xattn_bk").reshape(KC, P).T], axis=1)
    parts = [np.eye(P, dtype=f), ((r[:, None] % (HG * HD)) // HD == np.arange(HG)).astype(f),
             (r[:, None] % E1 == r % E1).astype(f), codes, bqk,
             n("L1_ffn_b1").reshape(C1, P).T, *(n(f"L0_ffn_{k}").reshape(E0, KC, P).transpose(2, 0, 1)
                                                for k in ("b1", "b2", "b3")),
             chunks(n("L0_ffn_gate_w").T), chunks(n("L1_ffn_wg"))]
    arrays["cst"] = np.concatenate([p.reshape(P, -1) for p in parts], axis=1)
    bf = np.dtype("bfloat16")
    arrays["identh"] = np.eye(P, dtype=np.float16)
    arrays["identb"] = np.eye(P, dtype=f).astype(bf)
    arrays["selp"] = np.repeat(np.tile(np.eye(E0, dtype=f), (3, 1)), P, axis=1).astype(bf).reshape(3 * E0, E0, P)
    arrays["selh"] = np.repeat(np.eye(E1, dtype=f), F1, axis=1).astype(bf).reshape(E1, C1, P)

    nc = _bacc.Bacc("TRN2", target_bir_lowering=False, num_devices=1)
    aps = {}
    ins = {}
    for k, x in arrays.items():
        x = np.ascontiguousarray(x)
        ins[f"in_{k}"] = x
        aps[k] = nc.dram_tensor(f"in_{k}", x.shape, mybir.dt.from_np(x.dtype), kind="ExternalInput").ap()
    out = nc.dram_tensor("out_0", (P, NT, D), F32, kind="ExternalOutput").ap()
    build(nc, aps, out)
    got = _run(nc, [ins], core_ids=[0]).results[0]["out_0"]
    return np.ascontiguousarray(got.reshape(P, NT, D).transpose(1, 0, 2).reshape(B, S, D))
```

```python
from contextlib import ExitStack

import concourse.bass as bass
from concourse import mybir

ALU = mybir.AluOpType
ACT = mybir.ActivationFunctionType
F32 = mybir.dt.float32
BF16 = mybir.dt.bfloat16
F16 = mybir.dt.float16
F32R = mybir.dt.float32r
U8 = mybir.dt.uint8
AX = mybir.AxisListType

P = 128
B, S, D = 16, 256, 256
SK = 77
H, HD = 16, 16
KC = D // P
NT = B * S // P
TB = S // P
GT = 4
NG = NT // GT
GN = GT * P
HG = 4
V1 = HD + 1
E0, E1 = 8, 16
I0 = 512
F1 = 64
C1 = E1 * F1 // P
KVN = 412
TOP = S // 2
EPS = 1e-5
EPS_GATE = 1e-6
NEG = -1e30
RSTEPS = 17
CST = 2 * P + HG + 2 * E1 + 2 * KC + C1 + 3 * E0 * KC + KC * E0 + KC * E1
BCST = 5 * D + E1 + 4
PARTS = ((1, 0), (0, 1), (0, 0))


def build(nc, a, out):
    ctx = ExitStack()
    with ctx:
        def sb(name, shape, dt=F32):
            return ctx.enter_context(nc.sbuf_tensor(name, shape, dt))

        def sem(name):
            return ctx.enter_context(nc.semaphore(name))

        X = sb("X", [P, NT, D])
        cst = sb("cst", [P, CST])
        o = [0]

        def const(n):
            o[0] += n
            return cst[:, o[0] - n:o[0]]

        ident = const(P)
        headm = const(HG)
        same_e = const(P)
        codes = const(2 * E1).rearrange("p (l e) -> p l e", l=2)
        bqk = const(2 * KC).rearrange("p (w k) -> p w k", w=2)
        b1f = const(C1)
        b1c = const(E0 * KC).rearrange("p (e k) -> p e k", e=E0)
        b23c = const(2 * E0 * KC).rearrange("p (w e k) -> p w e k", w=2, e=E0)
        gates_raw = const(KC * (E0 + E1))
        bc = sb("bc", [P, BCST])
        rows = bc[:, 0:5 * D].rearrange("p (r d) -> p r d", r=5)
        bgr = bc[:, 5 * D:5 * D + E1]
        gates = bc[:, 5 * D + E1:5 * D + E1 + 4]
        tg = sb("tg", [P, 4])
        rw = sb("rw", [P, 2, KC * (E0 + E1)], F32R)
        gatew = rw[:, :, 0:KC * E0].rearrange("p l (k e) -> p l k e", k=KC)
        wg = rw[:, :, KC * E0:].rearrange("p l (k e) -> p l k e", k=KC)
        selp = sb("selp", [3 * E0, E0, P], BF16)
        identb = sb("identb", [P, P], BF16)
        identh = sb("identh", [P, P], F16)
        ones1 = sb("ones1", [1, P], BF16)
        mcol8 = sb("mcol8", [SK, B], U8)
        keep = sb("keep", [SK, B])
        epsm = sb("epsm", [P, NT])
        mhalf = sb("mhalf", [P, NT])
        one = sb("one", [P, 8])
        bnraw = sb("bnraw", [P, NT, 6])
        mean = sb("mean", [P, NT])
        rstd = sb("rstd", [P, NT])
        st = sb("st", [P, 4, NT])

        top8 = sb("top8", [P, 2, 8])
        R0 = {n: sb("r_" + n, [P, GT * E0]) for n in ("a", "b", "oh1", "oh2")}
        rm = sb("rm", [P, 5, NT])
        prob = sb("prob", [P, GT, E0])
        chosen = sb("chosen", [P, GT, E0])
        psp = sb("psp", [P, GT, 3 * E0], BF16)
        prs = sb("prs", [P, 2, GT * E0])
        pT = sb("pT", [3 * E0, GN], BF16)
        def over():
            return ExitStack()

        def tmp(stack, name, shape, dt=F32):
            return stack.enter_context(nc.sbuf_tensor(name, shape, dt))[(slice(None),) * len(shape)]

        with over() as att:
            with over() as raw:
                wattn_raw = tmp(raw, "wattn_raw", [P, 4, 2, KC * D])
                ctx_raw = tmp(raw, "ctx_raw", [P, 2, KC, B * SK])
            wattn = tmp(att, "wattn", [P, 4, 2, KC * D], F32R)
            ctxT = tmp(att, "ctxT", [P, 2, KC, B * SK], F32R)
            kT = tmp(att, "kT", [P, 2, KC, B * SK], F32R)
            Vb = tmp(att, "Vb", [SK, 3, B, H * V1], BF16)
            Vc = [tmp(att, f"Vc{k}", [SK, H, 3, V1], BF16) for k in range(2)]
            Kbd = [tmp(att, f"Kbd{k}", [P, 2, KC, HG * SK], F32R) for k in range(2)]
            Pf = tmp(att, "Pf", [P, H, SK])
            Phl = [tmp(att, f"Phl{k}", [P, 2, H, SK], F16) for k in range(2)]
            mrow8 = tmp(att, "mrow8", [1, B * SK], U8)
            mrow = tmp(att, "mrow", [1, B * SK], BF16)
            xn_a = tmp(att, "xn_a", [P, 2, D])
            xnT_a = tmp(att, "xnT_a", [P, 2, KC, P], F32R)
            qT = tmp(att, "qT", [P, 2, KC, P], F32R)
            nmx = tmp(att, "nmx", [P, H])
            o_s = tmp(att, "o_s", [P, H, V1])
            rec = tmp(att, "rec", [P, H])
            o_a = tmp(att, "o_a", [P, D])
            oT = tmp(att, "oT", [P, 2, KC, P], F32R)
            with over() as early:
                vf = tmp(early, "vf", [SK, 2, D])
                vr = tmp(early, "vr", [SK, 2, D])
            PT = tmp(att, "PT", [SK, 4, 2, 4, P], F16)

        xn4 = tmp(ctx, "xn4", [P, GT, D])
        xT = tmp(ctx, "xT", [P, 2, KC, GN], F32R)
        with over() as f0:
            with over() as raw:
                w0_raw = tmp(raw, "w0_raw", [P, E0, 3, 2, KC * D])
                sw12_raw = tmp(raw, "sw12_raw", [P, 2, 2, KC * I0])
                sw3_raw = tmp(raw, "sw3_raw", [P, 2, I0 // P * D])
            w0 = tmp(f0, "w0", [P, E0, 3, 2, KC * D], F32R)
            sw12 = tmp(f0, "sw12", [P, 2, 2, KC * I0], F32R)
            sw3 = tmp(f0, "sw3", [P, 2, I0 // P * D], F32R)
            pb = tmp(f0, "pb", [P, 2, GN])
            x23 = tmp(f0, "x23", [P, KC, GN])
            sil, swf = pb, x23
            yT = tmp(f0, "yT", [P, KC, GN])
            mb = tmp(f0, "mb", [P, GN], BF16)
            with over() as shared:
                swi = tmp(shared, "swi", [P, 2, I0 // P, GN], F32R)
            u = tmp(f0, "u", [P, KC, GN])
            h = tmp(f0, "h", [P, 2, KC, GN], F32R)
            x3 = tmp(f0, "x3", [P, KC, GN])

        with over() as f1:
            with over() as raw:
                w1f_raw = tmp(raw, "w1f_raw", [P, 2, KC * E1 * F1])
                w2f_raw = tmp(raw, "w2f_raw", [P, 2, C1 * D])
            w1f = tmp(f1, "w1f", [P, 2, KC * E1 * F1], F32R)
            w2f = tmp(f1, "w2f", [P, 2, C1 * D], F32R)
            selh = tmp(f1, "selh", [E1, C1, P], BF16)
            b2f = tmp(f1, "b2f", [E1, D])
            b2r = tmp(f1, "b2r", [E1, 2, D])
            b2s = tmp(f1, "b2s", [E1, 3, D], BF16)
            xn4b = tmp(f1, "xn4b", [P, GT, D])
            xTb = tmp(f1, "xTb", [P, 2, KC, GN], F32R)
            R1 = {n: tmp(f1, "r1_" + n, [P, NT * E1]) for n in ("a", "b", "p", "oh1", "oh2")}
            lg = tmp(f1, "lg", [P, NT * E1])
            smT = tmp(f1, "smT", [E1, NT * P])
            route = tmp(f1, "route", [P, 2, S])
            rden = tmp(f1, "rden", [P, S])
            selb = tmp(f1, "selb", [P, 2, S], BF16)
            selT = smT[:, 0:B * S // 2].bitcast(BF16).rearrange("p (b s) -> p b s", b=B)
            selg = [tmp(f1, f"selg{k}", [E1, GN], BF16) for k in range(2)]
            hgf = tmp(f1, "hgf", [P, 2, GN])
            hmf = tmp(f1, "hmf", [P, 2, GN])
            hm = tmp(f1, "hm", [P, 2, 2, GN], F32R)
            z = tmp(f1, "z", [P, GT, D])
            zs = tmp(f1, "zs", [P, 4, GT])
            zraw = tmp(f1, "zraw", [P, GT, 6])
            zmean = tmp(f1, "zmean", [P, GT])
            zrstd = tmp(f1, "zrstd", [P, GT])

        ps = ctx.enter_context(nc.psum_tensor("ps", [P, 8, 512], F32))

        L = {n: sem("ld_" + n) for n in ("const", "small", "x0", "x1", "kv", "attn0", "shared", "attn1", "ctx1",
                                         "feed1", "late")}
        Le = [sem(f"ld_expert{e}") for e in range(E0)]
        names = """prep cst tanh stc stat statc wsh wsl csh csl kps kcp kl vps vf vh vl vm vp vc vmk xn xnTps xnT xl
            qps q ql kbd sc mx sub ex ph pl ptps pt pv osum rec on oTps oT ol y res res2 bn fxn
            fxTps fxT fxl lps rst rex sel0 pTps pTc gA gAs gB gG gGh gGl zps zcp pps pb mb ups u hf
            hh hl x3ps x3 x3m x2ps x23 acc yps0 fres fbn wh wl sh sl rws b2 lgps lgc rst1 rex1 smps
            smc rt dps tk sel selT selR selg hps gelu mps hm hmh hml hmr yps z zbn zst zmn zpow zn
            zo out bsp msk""".split()
        s = {n: sem("s_" + n) for n in names}

        def counted(v):
            return not isinstance(v, int) or v > 0

        def tile_of(x, t):
            return x[:, t, :] if isinstance(t, int) else x[:, bass.ds(t, 1), :].rearrange("p a d -> p (a d)")

        def col(x, t):
            return x[:, t:t + 1] if isinstance(t, int) else x[:, bass.ds(t, 1)]

        def span(x, c, n):
            return x[..., c:c + n] if isinstance(c, int) else x[..., bass.ds(c, n)]

        def group_of(x, g):
            return x[:, g * GT:(g + 1) * GT, :] if isinstance(g, int) else x[:, bass.ds(g * GT, GT), :]

        block = ctx.enter_context(nc.Block())

        def bank(n):
            return ps[:, n, :]

        @block.sync
        def _(sp):
            def ld(key, dst, src):
                sp.dma_start(dst, src).then_inc(L[key], 16)

            ld("attn0", wattn_raw[:, :, 1, :], a["wattn0"])
            ld("kv", ctx_raw[:, 1], a["ctxT"])
            ld("const", cst[:, :], a["cst"])
            ld("const", bc[:, :], a["bc"].partition_broadcast(P))
            ld("small", mrow8, a["mrow"])
            ld("small", mcol8[:, :], a["mcol"])
            ld("small", identb[:, :], a["identb"])
            ld("small", identh[:, :], a["identh"])
            ld("small", selp[:, :, :], a["selp"])
            sp.wait_ge(s["bn"], 2 * NT)
            ld("shared", sw12_raw[:, :, 1, :], a["sw12"])
            ld("shared", sw3_raw[:, 1, :], a["sw3"])
            for e in range(E0):
                sp.dma_start(w0_raw[:, e, :, 1, :], a["feed0"][:, e]).then_inc(Le[e], 16)
            sp.wait_ge(s["fres"], NG)
            ld("attn1", wattn_raw[:, :, 1, :], a["wattn1"])
            ld("ctx1", ctx_raw[:, 1], a["ctxT"])
            sp.wait_ge(s["bn"], 3 * NT)
            ld("feed1", w1f_raw[:, 1, :], a["w1f"])
            ld("feed1", w2f_raw[:, 1, :], a["w2f"])
            ld("late", selh, a["selh"])
            ld("late", b2f, a["b2f"])
            for b in range(B):
                sp.wait_ge(s["smc"], b // 2 + 1)
                sp.dma_start(route[E1 * (b % 8):E1 * (b % 8 + 1), b // 8, :],
                             smT[:, b * S:(b + 1) * S]).then_inc(s["rt"], 16)
            sp.wait_ge(s["sel"], 1)
            for b in range(B):
                sp.dma_start(selT[:, b, :], selb[E1 * (b % 8):E1 * (b % 8 + 1), b // 8, :]
                             ).then_inc(s["selT" if b < GT // TB else "selR"], 16)
            for g in range(NG):
                sp.wait_ge(s["zo"], 2 * (g + 1))
                sp.dma_start(out[:, GT * g:GT * (g + 1), :], X[:, GT * g:GT * (g + 1), :]).then_inc(s["out"], 16)
            sp.wait_ge(s["out"], 16 * NG)

        @block.gpsimd
        def _(pool):
            pool.memset(ones1[:, :], 1.0).then_inc(s["cst"], 1)
            pool.memset(mhalf[:, :], -0.5).then_inc(s["cst"], 1)
            pool.memset(one[:, :], 1.0).then_inc(s["cst"], 1)

            def rsqrt(k):
                pool.wait_ge(s["stat"], k)
                pool.tensor_tensor(rstd[:, :], epsm[:, :], mhalf[:, :], ALU.pow).then_inc(s["statc"], 1)

            pool.wait_ge(s["cst"], 3)

            def split(key, n, hi, lo, src):
                pool.tensor_copy(hi, src).then_inc(s[key], 1)
                pool.wait_ge(s[key], n + 1)
                pool.tensor_tensor(lo, src, hi, ALU.subtract).then_inc(s[key], 1)

            def attention(l):
                base = NT * l

                for b in range(B):
                    pool.wait_ge(s["vm"], B * l + b + 1)
                    pool.tensor_tensor(Vb[:, 2, b, :].rearrange("s (h d) -> s h d", h=H)[:, :, 0:HD],
                                       vr[:, b % 2, :].rearrange("s (h d) -> s h d", h=H),
                                       Vb[:, 1, b, :].rearrange("s (h d) -> s h d", h=H)[:, :, 0:HD],
                                       ALU.subtract).then_inc(s["vp"], 1)
                if l == 0:
                    rsqrt(1)

                def halve(t, k):
                    for j in range(2):
                        hs = slice(8 * j, 8 * j + 8)
                        pool.wait_ge(s["ex"], 2 * t + (2 * base + j + 1))
                        pool.tensor_tensor(Phl[k % 2][:, 0, hs, :], Pf[:, hs, :],
                                           one[:, :].unsqueeze(2).to_broadcast([P, 8, SK]), ALU.mult
                                           ).then_inc(s["ph"], 1)
                        pool.wait_ge(s["ph"], 2 * t + (2 * base + j + 1))
                        pool.tensor_tensor(Phl[k % 2][:, 1, hs, :], Pf[:, hs, :], Phl[k % 2][:, 0, hs, :],
                                           ALU.subtract).then_inc(s["pl"], 1)

                def bias(t):
                    pool.wait_ge(s["res"], t + (base + 1))
                    pool.tensor_tensor(tile_of(X, t), tile_of(X, t), rows[:, 1 + l, :], ALU.add
                                       ).then_inc(s["res2"], 1)

                for k in range(4):
                    halve(k, k)
                    if k >= 2:
                        bias(k - 2)
                with pool.Fori(4, NT - 4, 4) as t0:
                    for k in range(4):
                        halve(t0 + k, k)
                        bias(t0 + (k - 2))
                for k in range(4):
                    halve(NT - 4 + k, k)
                    bias(NT - 6 + k)
                bias(NT - 2)
                bias(NT - 1)

            attention(0)
            rsqrt(2)

            def feed0(g, first=False):
                for e in range(E0):
                    n = g * E0 + e
                    if first and e + 2 < E0:
                        expert_lo(e + 2)
                    for hf in range(2):
                        if e == 0 and hf == 0:
                            pool.wait_ge(s["zcp"], 2 * g + 2)
                        if e > 0:
                            pool.wait_ge(s["acc"], 2 * n - 1 + hf)
                        pool.wait_ge(s["x23"], 2 * n + hf + 1)
                        pool.tensor_tensor(yT[:, hf, :], yT[:, hf, :], x23[:, hf, :], ALU.add).then_inc(s["acc"], 1)

            def feed0_weights():
                pool.wait_ge(s["sh"], 1)
                pool.tensor_tensor(sw12[:, :, 1, :], sw12_raw[:, :, 1, :], sw12[:, :, 0, :], ALU.subtract
                                   ).then_inc(s["sl"], 1)
                pool.wait_ge(s["sh"], 2)
                pool.tensor_tensor(sw3[:, 1, :], sw3_raw[:, 1, :], sw3[:, 0, :], ALU.subtract).then_inc(s["sl"], 1)

            def expert_lo(e):
                pool.wait_ge(s["wh"], e + 1)
                pool.tensor_tensor(w0[:, e, :, 1, :], w0_raw[:, e, :, 1, :], w0[:, e, :, 0, :], ALU.subtract
                                   ).then_inc(s["wl"], 1)

            feed0_weights()
            expert_lo(0)
            expert_lo(1)
            feed0(0, first=True)
            with pool.Fori(1, NG) as g:
                feed0(g)
            rsqrt(3)
            attention(1)
            rsqrt(4)
            pool.wait_ge(L["feed1"], 32)
            split("wl", E0, w1f[:, 0, :], w1f[:, 1, :], w1f_raw[:, 1, :])
            split("wl", E0 + 2, w2f[:, 0, :], w2f[:, 1, :], w2f_raw[:, 1, :])

            def feed1(g, k):
                if counted(g + (-1)):
                    pool.wait_ge(s["yps"], g + (-1))
                pool.tensor_copy(selg[k], span(selT.rearrange("e b s -> e (b s)"), g * GN, GN)).then_inc(s["selg"], 1)

            def root(g):
                pool.wait_ge(s["zst"], 5 * g + 5)
                pool.tensor_tensor(zrstd, zs[:, 3, :], mhalf[:, 0:GT], ALU.pow).then_inc(s["zpow"], 1)

            pool.wait_ge(s["selT"], 16 * (GT // TB))
            feed1(0, 0)
            pool.wait_ge(s["selR"], 16 * (B - GT // TB))
            feed1(1, 1)
            with pool.Fori(0, NG // 2 - 1) as pair:
                for k in range(2):
                    root(pair * 2 + k)
                    feed1(pair * 2 + (2 + k), k)
            root(NG - 2)
            root(NG - 1)

        @block.scalar
        def _(act):
            act.dma_start(X[:, 0:NT // 2, :], a["x"][:, 0:NT // 2, :]).then_inc(L["x0"], 16)
            act.dma_start(X[:, NT // 2:NT, :], a["x"][:, NT // 2:NT, :]).then_inc(L["x1"], 16)
            act.wait_ge(L["attn0"], 16)
            raw = wattn_raw[:, :, 1, :]
            act.mul(wattn[:, 0, 0, :], raw[:, 0], HD ** -0.5).then_inc(s["wsh"], 1)
            act.copy(wattn[:, 1:4, 0, :], raw[:, 1:4]).then_inc(s["wsh"], 1)
            act.wait_ge(L["kv"], 16)
            act.copy(ctxT[:, 0], ctx_raw[:, 1]).then_inc(s["csh"], 1)
            act.wait_ge(L["const"], 32)
            act.activation(tg[:, :], gates, ACT.Tanh).then_inc(s["tanh"], 1)

            def kv(l):
                if l == 1:
                    act.wait_ge(L["attn1"], 16)
                    act.copy(wattn[:, :, 0, :], wattn_raw[:, :, 1, :]).then_inc(s["wsh"], 1)
                    act.wait_ge(L["ctx1"], 16)
                    act.copy(ctxT[:, 0], ctx_raw[:, 1]).then_inc(s["csh"], 1)
                for oc in range(KC):
                    for n in range(3):
                        c = oc * 3 + n
                        lo, hi = n * KVN, min(B * SK, (n + 1) * KVN)
                        act.wait_ge(s["kps"], 6 * l + c + 1)
                        src = ps[:, c % 2, 0:hi - lo]
                        if l == 0:
                            act.activation(kT[:, 0, oc, lo:hi], src, ACT.Identity,
                                           bias=bqk[:, 1, oc:oc + 1]).then_inc(s["kcp"], 1)
                        else:
                            act.copy(kT[:, 0, oc, lo:hi], src).then_inc(s["kcp"], 1)
                def values_mid(b):
                    act.wait_ge(s["vl"], B * l + b + 1)
                    act.copy(Vb[:, 1, b, :].rearrange("s (h d) -> s h d", h=H)[:, :, 0:HD],
                             vr[:, b % 2, :].rearrange("s (h d) -> s h d", h=H)).then_inc(s["vm"], 1)

                for b in range(B):
                    dst = Vb[:, 0, b, :].rearrange("s (h d) -> s h d", h=H)[:, :, 0:HD]
                    if l == 0:
                        act.wait_ge(s["vf"], b + 1)
                        act.mul(dst, vf[:, b % 2, :].rearrange("s (h d) -> s h d", h=H), keep[:, b:b + 1]
                                ).then_inc(s["vh"], 1)
                    else:
                        act.wait_ge(s["vps"], B * l + b + 1)
                        act.copy(dst, ps[0:SK, 2 + b % 2, 0:D].rearrange("s (h d) -> s h d", h=H)
                                 ).then_inc(s["vh"], 1)
                    if b:
                        values_mid(b - 1)
                values_mid(B - 1)

            def xnT_copy(v):
                act.wait_ge(s["xnTps"], v + 1)
                act.copy(xnT_a[:, 0], ps[:, 6, 0:D].rearrange("p (k t) -> p k t", k=KC)).then_inc(s["xnT"], 1)

            def q_copy(l, v):
                act.wait_ge(s["qps"], v + 1)
                if l == 0:
                    for oc in range(KC):
                        i = act.activation(qT[:, 0, oc, :], ps[:, 6, D + oc * P:D + (oc + 1) * P], ACT.Identity,
                                           bias=bqk[:, 0, oc:oc + 1])
                else:
                    i = act.mul(qT[:, 0], ps[:, 6, D:2 * D].rearrange("p (k t) -> p k t", k=KC), HD ** -0.5)
                i.then_inc(s["q"], 1)

            def exp(j, v):
                act.wait_ge(s["sub"], 2 * v + (j + 1))
                act.activation(Pf[:, 8 * j:8 * j + 8, :], Pf[:, 8 * j:8 * j + 8, :], ACT.Exp).then_inc(s["ex"], 1)

            def pt_copy(g, v):
                act.wait_ge(s["ptps"], 4 * v + (g + 1))
                act.copy(PT[:, g].rearrange("s l h t -> s (l h t)"), ps[0:SK, 4 + g % 2, :].bitcast(F16)
                         ).then_inc(s["pt"], 1)

            def oT_copy(v):
                act.wait_ge(s["oTps"], v + 1)
                act.copy(oT[:, 0], ps[:, 7, 0:D].rearrange("p (k t) -> p k t", k=KC)).then_inc(s["oT"], 1)

            def attention(l):
                base = NT * l

                def values(b, kb):
                    if counted(2 * b + (base - 2) if not isinstance(b, int) or b >= 2 else base):
                        act.wait_ge(s["pv"], 2 * b + (base - 2) if not isinstance(b, int) or b >= 2 else base)
                    src = Vb[:, :, b, :] if isinstance(b, int) \
                        else Vb[:, :, bass.ds(b, 1), :].rearrange("s k a n -> s k (a n)")
                    act.copy(Vc[kb].rearrange("s h k d -> s k h d"), src.rearrange("s k (h d) -> s k h d", h=H)
                             ).then_inc(s["vc"], 1)

                def step(t, b=True, c=True, n=True, x=True, vb=None, kb=0):
                    v = t + base
                    if n:
                        xnT_copy(v + 1)
                    if b:
                        pt_copy(0, v + (-1))
                    if n:
                        q_copy(l, v + 1)
                    if b:
                        pt_copy(1, v + (-1))
                    if c:
                        oT_copy(v + (-2))
                    if x:
                        exp(0, v)
                    if b:
                        pt_copy(2, v + (-1))
                    if x:
                        exp(1, v)
                    if b:
                        pt_copy(3, v + (-1))
                    if vb is not None:
                        values(vb, kb)

                kv(l)
                act.wait_ge(s["vmk"], 4 if l == 0 else 7)
                act.wait_ge(s["vp"], B * (l + 1))
                values(0, 0)
                if l == 0:
                    act.wait_ge(s["msk"], 5)
                xnT_copy(base)
                q_copy(l, base)
                def entry(k, b0):
                    return b0 + (k // TB + 1) if k % TB == TB - 1 else None

                for k in range(4):
                    step(k, b=k >= 1, c=k >= 2, vb=entry(k, 0), kb=(k // TB + 1) % 2)
                with act.Fori(2, (NT - 4) // TB, 2) as b0:
                    for k in range(4):
                        step(b0 * TB + k, vb=entry(k, b0), kb=(k // TB + 1) % 2)
                for t in range(NT - 4, NT + 2):
                    k = t % 4
                    step(t, b=t <= NT, n=t + 1 < NT, x=t < NT, kb=(k // TB + 1) % 2,
                         vb=entry(k, B - 2) if t < NT - 1 else None)

            def xT_copy(v, dst, first_bank=0):
                for kc in range(KC):
                    act.wait_ge(s["fxTps"], KC * v + (kc + 1))
                    act.copy(dst[:, kc, :], bank(first_bank + kc)).then_inc(s["fxT"], 1)

            def expert_hi(e):
                act.wait_ge(Le[e], 16)
                act.copy(w0[:, e, :, 0, :], w0_raw[:, e, :, 1, :]).then_inc(s["wh"], 1)

            def feed0(g, first=False, last=False):
                act.wait_ge(s["rst"], RSTEPS * g + 2)
                act.activation(R0["a"][:, :], R0["a"][:, :], ACT.Exp).then_inc(s["rex"], 1)
                for ic in range(5):
                    if ic < 4:
                        if ic == 0:
                            if counted(2 * E0 * g):
                                act.wait_ge(s["x23"], 2 * E0 * g)
                        act.wait_ge(s["gA"], 4 * g + ic + 1)
                        if ic >= 2:
                            act.wait_ge(s["gG"], 4 * g + ic - 1)
                        act.activation(sil[:, ic % 2, :], bank(2 * (ic % 2)), ACT.Silu).then_inc(s["gAs"], 1)
                    if ic >= 1:
                        act.wait_ge(s["gG"], 4 * g + ic)
                        act.copy(swi[:, 0, ic - 1, :], swf[:, (ic - 1) % 2, :]).then_inc(s["gGh"], 1)
                act.wait_ge(s["pTps"], g + 1)
                act.copy(pT[:, :], ps[0:3 * E0, 6, 0:GN // 2].bitcast(BF16)).then_inc(s["pTc"], 1)
                for oc in range(KC):
                    if oc == 0:
                        if counted(g):
                            act.wait_ge(s["yps0"], g)
                    act.wait_ge(s["zps"], 2 * g + oc + 1)
                    act.copy(yT[:, oc, :], bank(4 + oc)).then_inc(s["zcp"], 1)
                for e in range(E0):
                    n = g * E0 + e
                    if first and e + 2 < E0:
                        expert_hi(e + 2)
                    if e >= 2:
                        act.wait_ge(s["x3"], 2 * n - 2)
                        act.wait_ge(s["mb"], n - 1)
                    elif e == 0:
                        act.wait_ge(s["gG"], 4 * g + 4)
                    act.wait_ge(s["pps"], n + 1)
                    act.copy(pb[:, e % 2, :], bank(6)).then_inc(s["pb"], 1)
                    if counted(2 * n):
                        act.wait_ge(s["x2ps"], 2 * n)
                    for oc in range(KC):
                        act.wait_ge(s["u"], 2 * n + oc + 1)
                        act.activation(u[:, oc, :], u[:, oc, :], ACT.Silu, bias=b1c[:, e, oc:oc + 1]
                                       ).then_inc(s["hf"], 1)
                        act.wait_ge(s["hf"], 2 * n + oc + 1)
                        act.copy(h[:, 0, oc, :], u[:, oc, :]).then_inc(s["hh"], 1)
                if not last:
                    act.wait_ge(s["x3ps"], 2 * E0 * g + 2 * E0)
                    xT_copy(g + 1, xT[:, 0], 6)

            def feed1(g, last=False):
                for c in range(C1):
                    m = g * C1 + c
                    act.wait_ge(s["hps"], m + 1)
                    if counted(m - 1):
                        act.wait_ge(s["hm"], m - 1)
                    act.activation(hgf[:, c % 2, :], bank(c % 2), ACT.Gelu, bias=b1f[:, c:c + 1]
                                   ).then_inc(s["gelu"], 1)
                    act.wait_ge(s["hm"], m + 1)
                    if counted(m - 1):
                        act.wait_ge(s["hmr"], m - 1)
                    act.copy(hm[:, c % 2, 0, :], hmf[:, c % 2, :]).then_inc(s["hmh"], 1)
                if not last:
                    xT_copy(g + (2 * NG + 1), xT[:, 0])

            attention(0)
            act.wait_ge(L["shared"], 32)
            act.copy(sw12[:, :, 0, :], sw12_raw[:, :, 1, :]).then_inc(s["sh"], 1)
            xT_copy(0, xT[:, 0], 6)
            act.copy(sw3[:, 0, :], sw3_raw[:, 1, :]).then_inc(s["sh"], 1)
            expert_hi(0)
            expert_hi(1)
            feed0(0, first=True)
            with act.Fori(1, NG - 1) as g:
                feed0(g)
            feed0(NG - 1, last=True)
            attention(1)

            def router1(g, k):
                if counted(g + (-1)):
                    act.wait_ge(s["lgps"], g + (-1))
                xT_copy(g + NG, (xT, xTb)[k][:, 0], 2 * k)

            router1(0, 0)
            router1(1, 1)
            with act.Fori(2, NG, 2) as g:
                router1(g, 0)
                router1(g + 1, 1)
            act.wait_ge(s["rst1"], 3)
            act.activation(R1["a"], R1["a"], ACT.Exp).then_inc(s["rex1"], 1)
            for k in range(NT // 4):
                act.wait_ge(s["smps"], k + 1)
                act.copy(smT[:, k * 512:(k + 1) * 512], ps[0:E1, 4 + k % 2, :]).then_inc(s["smc"], 1)
            xT_copy(2 * NG, xT[:, 0])
            feed1(0)
            with act.Fori(1, NG - 1) as g:
                feed1(g)
            feed1(NG - 1, last=True)

        @block.vector
        def _(v):
            def stats(k):
                c = 5 * (k - 1)
                me, qe, mo, qo = bnraw[:, :, 1], bnraw[:, :, 2], bnraw[:, :, 4], bnraw[:, :, 5]

                def link(i):
                    nonlocal c
                    c += 1
                    i.then_inc(s["stc"], 1)
                    v.wait_ge(s["stc"], c)

                link(v.tensor_tensor(st[:, 0, :], me, mo, ALU.subtract))
                link(v.tensor_tensor(st[:, 1, :], st[:, 0, :], st[:, 0, :], ALU.mult))
                link(v.tensor_tensor(st[:, 2, :], qe, qo, ALU.add))
                link(v.tensor_tensor(mean[:, :], me, mo, ALU.add))
                link(v.tensor_scalar(st[:, 3, :], st[:, 1, :], D / 4.0, None, ALU.mult))
                v.tensor_scalar(mean[:, :], mean[:, :], 0.5, None, ALU.mult).then_inc(s["bsp"], 1)
                v.tensor_tensor(st[:, 0, :], st[:, 3, :], st[:, 2, :], ALU.add).then_inc(s["bsp"], 1)
                v.wait_ge(s["bsp"], 2 * k)
                v.tensor_scalar(epsm[:, :], st[:, 0, :], 1.0 / D, EPS, ALU.mult, ALU.add).then_inc(s["stat"], 1)

            def context_lo(k):
                v.wait_ge(s["csh"], k)
                v.tensor_tensor(ctxT[:, 1], ctx_raw[:, 1], ctxT[:, 0], ALU.subtract).then_inc(s["csl"], 1)

            raw = wattn_raw[:, :, 1, :]
            v.wait_ge(s["wsh"], 1)
            v.scalar_tensor_tensor(wattn[:, 0, 1, :], raw[:, 0], HD ** -0.5, wattn[:, 0, 0, :],
                                   ALU.mult, ALU.subtract).then_inc(s["wsl"], 1)
            v.wait_ge(s["wsh"], 2)
            v.tensor_tensor(wattn[:, 1:4, 1, :], raw[:, 1:4], wattn[:, 1:4, 0, :], ALU.subtract
                            ).then_inc(s["wsl"], 1)
            context_lo(1)
            v.wait_ge(L["const"], 32)
            v.wait_ge(L["small"], 16 * 5)
            v.tensor_scalar(mrow[:, :], mrow8, NEG, None, ALU.mult).then_inc(s["prep"], 1)
            v.tensor_scalar(keep[:, :], mcol8[:, :], -1.0, 1.0, ALU.mult, ALU.add).then_inc(s["prep"], 1)
            v.tensor_copy(rw[:, 0, :], gates_raw).then_inc(s["rws"], 1)
            v.wait_ge(s["rws"], 1)
            v.tensor_tensor(rw[:, 1, :], gates_raw, rw[:, 0, :], ALU.subtract).then_inc(s["rws"], 1)
            v.wait_ge(s["tanh"], 1)
            for r, g in ((1, 0), (2, 1), (3, 3), (4, 3)):
                v.tensor_scalar(rows[:, r, :], rows[:, r, :], tg[:, g:g + 1], None, ALU.mult).then_inc(s["msk"], 1)
            v.tensor_scalar(bqk[:, 0, :], bqk[:, 0, :], HD ** -0.5, None, ALU.mult).then_inc(s["msk"], 1)

            def input_stats(b):
                if b in (0, B // 2):
                    v.wait_ge(L["x0" if b == 0 else "x1"], 16)
                for t in range(b * TB, (b + 1) * TB):
                    v.bn_stats(bnraw[:, t, :], X[:, t, :]).then_inc(s["bn"], 1)

            def kv(l):
                if l == 1:
                    v.wait_ge(s["wsh"], 3)
                    v.tensor_tensor(wattn[:, :, 1, :], wattn_raw[:, :, 1, :], wattn[:, :, 0, :],
                                    ALU.subtract).then_inc(s["wsl"], 1)
                    context_lo(2)
                for oc in range(KC):
                    for n in range(3):
                        c = oc * 3 + n
                        lo, hi = n * KVN, min(B * SK, (n + 1) * KVN)
                        v.wait_ge(s["kcp"], 6 * l + c + 1)
                        src = ps[:, c % 2, 0:hi - lo]
                        if l == 0:
                            v.scalar_tensor_tensor(kT[:, 1, oc, lo:hi], src, bqk[:, 1, oc:oc + 1],
                                                   kT[:, 0, oc, lo:hi], ALU.add, ALU.subtract).then_inc(s["kl"], 1)
                        else:
                            v.tensor_tensor(kT[:, 1, oc, lo:hi], src, kT[:, 0, oc, lo:hi], ALU.subtract
                                            ).then_inc(s["kl"], 1)

                for k in range(3):
                    v.memset(Vb[:, k, :, :].rearrange("s b (h d) -> s b h d", h=H)[:, :, :, HD], float(k == 0)
                             ).then_inc(s["vmk"], 1)
                if l == 0:
                    v.wait_ge(s["vmk"], 3)
                    ones = Vb[:, 0, :, :].rearrange("s b (h d) -> s b h d", h=H)[:, :, :, HD]
                    v.tensor_tensor(ones, ones, keep[:, :].unsqueeze(2).to_broadcast([SK, B, H]), ALU.mult
                                    ).then_inc(s["vmk"], 1)

                def heads(x):
                    return x.rearrange("s (h d) -> s h d", h=H)

                def values_lo(b):
                    hi, lo = heads(Vb[:, 0, b, :])[:, :, 0:HD], heads(vr[:, b % 2, :])
                    v.wait_ge(s["vh"], B * l + b + 1)
                    if b >= 2 or l == 1:
                        v.wait_ge(s["vp"], B * l + b - 1)
                    if l == 0:
                        v.scalar_tensor_tensor(lo, heads(vf[:, b % 2, :]), keep[:, b:b + 1], hi, ALU.mult, ALU.subtract
                                               ).then_inc(s["vl"], 1)
                    else:
                        v.tensor_tensor(lo, heads(ps[0:SK, 2 + b % 2, 0:D]), hi, ALU.subtract).then_inc(s["vl"], 1)

                for b in range(B):
                    if l == 0:
                        v.wait_ge(s["vps"], b + 1)
                        if counted(b - 1):
                            v.wait_ge(s["vl"], b - 1)
                        v.tensor_tensor(vf[:, b % 2, :], ps[0:SK, 2 + b % 2, 0:D], rows[0:SK, 0, :], ALU.add
                                        ).then_inc(s["vf"], 1)
                        input_stats(b)
                        if b:
                            values_lo(b - 1)
                    else:
                        values_lo(b)
                if l == 0:
                    values_lo(B - 1)

            def attention(l):
                base = NT * l

                def norm(t, k):
                    if counted(t + (base - 1)):
                        v.wait_ge(s["xnTps"], t + (base - 1))
                    v.tensor_scalar(xn_a[:, k % 2, :], tile_of(X, t), col(mean, t), col(rstd, t),
                                    ALU.subtract, ALU.mult).then_inc(s["xn"], 1)

                def keys(b, kb):
                    kd = Kbd[kb].rearrange("p l c (j s) -> p l c j s", j=HG)
                    for j in range(HG):
                        i = v.tensor_scalar(kd[:, :, :, j, :], span(kT, b * SK, SK), headm[:, j:j + 1],
                                            None, ALU.mult)
                    i.then_inc(s["kbd"], 1)

                def top(t, j):
                    v.wait_ge(s["sc"], t + (base + 1))
                    sc = ps[:, 2 * j:2 * j + 2, 0:HG * SK].rearrange("p g (h s) -> p g h s", h=HG)
                    v.tensor_reduce(nmx[:, 8 * j:8 * j + 8].rearrange("p (g h) -> p g h", g=2), sc, AX.X, ALU.max
                                    ).then_inc(s["mx"], 1)

                def less(t, j):
                    if counted(2 * t + (2 * base - 1 + j)):
                        v.wait_ge(s["pl"], 2 * t + (2 * base - 1 + j))
                    v.wait_ge(s["mx"], 2 * t + (2 * base + 1 + j))
                    sc = ps[:, 2 * j:2 * j + 2, 0:HG * SK].rearrange("p g (h s) -> p g h s", h=HG)
                    mx = nmx[:, 8 * j:8 * j + 8].rearrange("p (g h) -> p g h", g=2).unsqueeze(3)
                    v.tensor_tensor(Pf[:, 8 * j:8 * j + 8, :].rearrange("p (g h) s -> p g h s", g=2), sc,
                                    mx.to_broadcast([P, 2, HG, SK]), ALU.subtract).then_inc(s["sub"], 1)

                def out_sum(t, j):
                    v.wait_ge(s["pv"], t + (base + 1))
                    if j == 0:
                        if counted(t + base):
                            v.wait_ge(s["on"], t + base)
                    hs = slice(8, 16) if j == 0 else slice(0, 8)
                    v.tensor_reduce(o_s[:, hs, :],
                                    ps[:, 5 if j == 0 else 7, 0:24 * V1].rearrange("p (h k d) -> p h d k", h=8, k=3),
                                    AX.X, ALU.add).then_inc(s["osum"], 1)

                def out_norm(t):
                    v.wait_ge(s["osum"], 2 * t + (2 * base + 2))
                    v.reciprocal(rec, o_s[:, :, HD]).then_inc(s["rec"], 1)
                    v.wait_ge(s["rec"], t + (base + 1))
                    v.tensor_tensor(o_a.rearrange("p (h d) -> p h d", h=H), o_s[:, :, 0:HD],
                                    rec.unsqueeze(2).to_broadcast([P, H, HD]), ALU.mult).then_inc(s["on"], 1)

                def o_lo(t):
                    v.wait_ge(s["oT"], t + (base + 1))
                    v.tensor_tensor(oT[:, 1], ps[:, 7, 0:D].rearrange("p (k t) -> p k t", k=KC), oT[:, 0],
                                    ALU.subtract).then_inc(s["ol"], 1)

                def x_lo(t):
                    v.wait_ge(s["xnT"], t + (base + 1))
                    v.tensor_tensor(xnT_a[:, 1], ps[:, 6, 0:D].rearrange("p (k t) -> p k t", k=KC), xnT_a[:, 0],
                                    ALU.subtract).then_inc(s["xl"], 1)

                def q_lo(t):
                    v.wait_ge(s["q"], t + (base + 1))
                    if l == 0:
                        for oc in range(KC):
                            i = v.scalar_tensor_tensor(qT[:, 1, oc, :], ps[:, 6, D + oc * P:D + (oc + 1) * P],
                                                       bqk[:, 0, oc:oc + 1], qT[:, 0, oc, :], ALU.add, ALU.subtract)
                    else:
                        i = v.scalar_tensor_tensor(qT[:, 1].rearrange("p k t -> p (k t)"), ps[:, 6, D:2 * D],
                                                   HD ** -0.5, qT[:, 0].rearrange("p k t -> p (k t)"),
                                                   ALU.mult, ALU.subtract)
                    i.then_inc(s["ql"], 1)

                def residual(t):
                    v.wait_ge(s["y"], t + (base + 1))
                    v.scalar_tensor_tensor(tile_of(X, t), ps[:, 7, 0:D], tg[:, l:l + 1], tile_of(X, t),
                                           ALU.mult, ALU.add).then_inc(s["res"], 1)

                def moments(t):
                    v.wait_ge(s["res2"], t + (base + 1))
                    v.bn_stats(tile_of(bnraw, t), tile_of(X, t)).then_inc(s["bn"], 1)

                kv(l)
                if l == 0:
                    v.wait_ge(s["bn"], NT)
                    stats(1)
                v.wait_ge(s["kl"], 6 * (l + 1))
                keys(0, 0)
                v.wait_ge(s["statc"], 1 + 2 * l)
                norm(0, 0)
                norm(1, 1)
                x_lo(0)
                q_lo(0)

                def step(t, k, b=None, n=True, c=True, x=True, m=True, nn=True):
                    if n:
                        x_lo(t + 1)
                    if x:
                        top(t, 0)
                    if c:
                        out_sum(t + (-2), 0)
                    if x:
                        top(t, 1)
                    if c:
                        out_sum(t + (-2), 1)
                        out_norm(t + (-2))
                    if x:
                        less(t, 0)
                    if nn:
                        norm(t + 2, k)
                    if c:
                        o_lo(t + (-2))
                    if x:
                        less(t, 1)
                    if n:
                        q_lo(t + 1)
                    if c:
                        residual(t + (-2))
                    if b is not None:
                        keys(b, (k // TB + 1) % 2)
                    if m:
                        moments(t + (-3))

                for k in range(4):
                    step(k, k, b=k // TB + 1 if k % TB == 0 else None, c=k >= 2, m=k >= 3)
                with v.Fori(2, (NT - 4) // TB, 2) as b0:
                    for k in range(4):
                        step(b0 * TB + k, k, b=b0 + (k // TB + 1) if k % TB == 0 else None)
                for t in range(NT - 4, NT + 2):
                    k = t % 4
                    b = t // TB + 1
                    step(t, k, b=b if k % TB == 0 and b < B else None, n=t + 1 < NT, x=t < NT, nn=t + 2 < NT)
                moments(NT - 1)

            def group_norm(g, done, dst):
                if counted(KC * done):
                    v.wait_ge(s["fxTps"], KC * done)
                for k in range(GT):
                    t = g * GT + k
                    i = v.tensor_scalar(dst[:, k, :], tile_of(X, t), col(mean, t), col(rstd, t),
                                        ALU.subtract, ALU.mult)
                i.then_inc(s["fxn"], 1)

            def group_lo(n, dst=xT, first_bank=0):
                for kc in range(KC):
                    v.wait_ge(s["fxT"], n + (kc + 1))
                    v.tensor_tensor(dst[:, 1, kc, :], bank(first_bank + kc), dst[:, 0, kc, :], ALU.subtract
                                    ).then_inc(s["fxl"], 1)

            def choose(R, T, E, src, bias, pr, code, sem_step, sem_exp, c0, x0, out_sel,
                       between=None):
                def sh(x):
                    return x[:, 0:T * E].rearrange("p (t e) -> p t e", t=T)

                def bcast(k):
                    return rm[:, k, 0:T].unsqueeze(2).to_broadcast([P, T, E])

                ra, rb = sh(R["a"]), sh(R["b"])
                oh1, oh2 = sh(R["oh1"]), sh(R["oh2"])
                cb = code.unsqueeze(1).to_broadcast([P, T, E])
                c = 0

                def link(i):
                    nonlocal c
                    c += 1
                    i.then_inc(s[sem_step], 1)
                    v.wait_ge(s[sem_step], c0 + c)

                if bias is not None:
                    link(v.tensor_tensor(src, src, bias, ALU.add))
                link(v.tensor_reduce(rm[:, 0, 0:T], src, AX.X, ALU.max))
                link(v.tensor_tensor(ra, src, bcast(0), ALU.subtract))
                v.wait_ge(s[sem_exp], x0)
                link(v.tensor_reduce(rm[:, 1, 0:T], ra, AX.X, ALU.add))
                link(v.reciprocal(rm[:, 2, 0:T], rm[:, 1, 0:T]))
                link(v.tensor_tensor(pr, ra, bcast(2), ALU.mult))
                link(v.tensor_reduce(rm[:, 3, 0:T], pr, AX.X, ALU.max))
                link(v.tensor_tensor(rb, pr, bcast(3), ALU.is_equal))
                link(v.tensor_tensor(rb, rb, cb, ALU.mult))
                link(v.tensor_reduce(rm[:, 3, 0:T], rb, AX.X, ALU.max))
                if between is not None:
                    between()
                link(v.tensor_tensor(oh1, cb, bcast(3), ALU.is_equal))
                link(v.scalar_tensor_tensor(ra, oh1, -2.0, pr, ALU.mult, ALU.add))
                link(v.tensor_reduce(rm[:, 4, 0:T], ra, AX.X, ALU.max))
                link(v.tensor_tensor(rb, ra, bcast(4), ALU.is_equal))
                link(v.tensor_tensor(rb, rb, cb, ALU.mult))
                link(v.tensor_reduce(rm[:, 4, 0:T], rb, AX.X, ALU.max))
                link(v.tensor_tensor(oh2, cb, bcast(4), ALU.is_equal))
                link(v.tensor_tensor(out_sel, oh1, oh2, ALU.add))
                return c

            def feed0(g, next_norm=None, first=False):
                def gated(ic):
                    if ic == 0:
                        if counted(2 * E0 * g):
                            v.wait_ge(s["acc"], 2 * E0 * g)
                    v.wait_ge(s["gB"], 4 * g + ic + 1)
                    v.wait_ge(s["gAs"], 4 * g + ic + 1)
                    if counted(4 * g + ic - 1):
                        v.wait_ge(s["gGl"], 4 * g + ic - 1)
                    v.tensor_tensor(swf[:, ic % 2, :], sil[:, ic % 2, :], bank(2 * (ic % 2) + 1), ALU.mult
                                    ).then_inc(s["gG"], 1)

                v.wait_ge(s["lps"], g + 1)
                src = ps[:, 7, 0:GT * E0].rearrange("p (t e) -> p t e", t=GT)
                c = choose(R0, GT, E0, src, None, prob[:, :, :], codes[:, 0, 0:E0], "rst", "rex",
                           RSTEPS * g, g + 1, chosen[:, :, :], between=lambda: gated(0))
                assert c == RSTEPS
                v.tensor_tensor(prob[:, :, :], prob[:, :, :], chosen[:, :, :], ALU.mult).then_inc(s["rws"], 1)
                v.wait_ge(s["rws"], 2 * g + 3)
                v.scalar_tensor_tensor(prob[:, :, :], chosen[:, :, :], -1.0, prob[:, :, :], ALU.add, ALU.add
                                       ).then_inc(s["rws"], 1)
                v.wait_ge(s["rws"], 2 * g + 4)
                pf = prob[:, :, :]
                ph, pm, pl = (psp[:, :, E0 * k:E0 * k + E0] for k in range(3))
                r1 = prs[:, 0, :].rearrange("p (t e) -> p t e", t=GT)
                r2 = prs[:, 1, :].rearrange("p (t e) -> p t e", t=GT)
                for k, i in enumerate((lambda: v.tensor_copy(ph, pf), lambda: v.tensor_tensor(r1, pf, ph, ALU.subtract),
                                       lambda: v.tensor_copy(pm, r1), lambda: v.tensor_tensor(r2, r1, pm, ALU.subtract),
                                       lambda: v.tensor_copy(pl, r2))):
                    i().then_inc(s["sel0"], 1)
                    v.wait_ge(s["sel0"], 5 * g + k + 1)
                for ic in range(1, 5):
                    if ic == 3 and not first:
                        residual0(g + (-1))
                    if ic < 4:
                        gated(ic)
                    v.wait_ge(s["gGh"], 4 * g + ic)
                    v.tensor_tensor(swi[:, 1, ic - 1, :], swf[:, (ic - 1) % 2, :], swi[:, 0, ic - 1, :],
                                    ALU.subtract).then_inc(s["gGl"], 1)
                if not first:
                    group_stats(g + (-1))
                for e in range(E0):
                    n = g * E0 + e
                    v.wait_ge(s["pb"], n + 1)
                    if counted(2 * n):
                        v.wait_ge(s["hh"], 2 * n)
                    if e == 0:
                        v.wait_ge(s["zps"], 2 * g + 2)
                    if counted(2 * n):
                        v.wait_ge(s["hl"], 2 * n)
                    for oc in range(KC):
                        v.wait_ge(s["ups"], 2 * n + oc + 1)
                        v.tensor_tensor(u[:, oc, :], bank(oc), pb[:, e % 2, :], ALU.mult).then_inc(s["u"], 1)
                    if counted(2 * n):
                        v.wait_ge(s["x3m"], 2 * n)
                    v.tensor_scalar(mb, pb[:, e % 2, :], 0.0, None, ALU.is_ge).then_inc(s["mb"], 1)
                    for oc in range(KC):
                        v.wait_ge(s["x3ps"], 2 * n + oc + 1)
                        if not (isinstance(g, int) and g == 0 and e == 0):
                            v.wait_ge(s["x23"], 2 * n - 1 + oc)
                        v.tensor_tensor(x3[:, oc, :], bank(2 + oc), pb[:, e % 2, :], ALU.mult).then_inc(s["x3"], 1)
                        v.wait_ge(s["hh"], 2 * n + oc + 1)
                        v.tensor_tensor(h[:, 1, oc, :], u[:, oc, :], h[:, 0, oc, :], ALU.subtract
                                        ).then_inc(s["hl"], 1)
                    if e == E0 - 1 and next_norm is not None:
                        group_lo(KC * g + KC, xT, 6)
                    v.wait_ge(s["mb"], n + 1)
                    for oc in range(KC):
                        v.wait_ge(s["x3"], 2 * n + oc + 1)
                        v.scalar_tensor_tensor(x3[:, oc, :], x3[:, oc, :], b23c[:, 1, e, oc:oc + 1], mb,
                                               ALU.add, ALU.mult).then_inc(s["x3m"], 1)
                    for oc in range(KC):
                        v.wait_ge(s["x2ps"], 2 * n + oc + 1)
                        if not (isinstance(g, int) and g == 0 and e == 0):
                            v.wait_ge(s["acc"], 2 * n - 1 + oc)
                        v.wait_ge(s["x3m"], 2 * n + oc + 1)
                        v.scalar_tensor_tensor(x23[:, oc, :], bank(4 + oc), b23c[:, 0, e, oc:oc + 1], x3[:, oc, :],
                                               ALU.add, ALU.mult).then_inc(s["x23"], 1)
                    if e == E0 - 5 and next_norm is not None:
                        group_norm(next_norm, next_norm, xn4)

            def residual0(g):
                v.wait_ge(s["yps0"], g + 1)
                xg = group_of(X, g)
                v.scalar_tensor_tensor(xg, ps[:, 4:6, :].rearrange("p b (t d) -> p (b t) d", t=2), tg[:, 2:3], xg,
                                       ALU.mult, ALU.add).then_inc(s["fres"], 1)

            def group_stats(g):
                v.wait_ge(s["fres"], g + 1)
                for k in range(GT):
                    t = g * GT + k
                    v.bn_stats(tile_of(bnraw, t), tile_of(X, t)).then_inc(s["fbn"], 1)

            attention(0)
            v.wait_ge(s["bn"], 2 * NT)
            stats(2)
            v.wait_ge(s["statc"], 2)
            group_norm(0, 0, xn4)
            group_lo(0, xT, 6)
            feed0(0, 1, first=True)
            with v.Fori(1, NG - 1) as g:
                feed0(g, g + 1)
            feed0(NG - 1)
            residual0(NG - 1)
            group_stats(NG - 1)
            v.wait_ge(s["fbn"], NT)
            stats(3)
            attention(1)
            v.wait_ge(s["bn"], 3 * NT)
            stats(4)
            v.wait_ge(s["statc"], 4)

            def router1(g, k):
                v.wait_ge(s["lgps"], g + 1)
                v.tensor_copy(span(lg, g * (GT * E1), GT * E1), ps[:, 6 + k, 0:GT * E1]).then_inc(s["lgc"], 1)

            group_norm(0, NG, xn4)
            group_norm(1, NG, xn4b)
            group_lo(KC * NG, xT, 0)
            with v.Fori(0, NG // 2 - 1) as pair:
                for k in range(2):
                    group_norm(pair * 2 + (2 + k), pair * 2 + (NG + k + 1), (xn4, xn4b)[k])
                    group_lo(pair * (2 * KC) + (KC * NG + KC * (k + 1)), (xTb, xT)[k], 2 - 2 * k)
                    router1(pair * 2 + k, k)
            group_lo(KC * (2 * NG - 1), xTb, 2)
            router1(NG - 2, 0)
            router1(NG - 1, 1)
            v.wait_ge(s["lgc"], NG)
            lg3 = lg.rearrange("p (t e) -> p t e", t=NT)
            pr3 = R1["p"].rearrange("p (t e) -> p t e", t=NT)
            choose(R1, NT, E1, lg3, bgr.unsqueeze(1).to_broadcast([P, NT, E1]), pr3, codes[:, 1, :],
                   "rst1", "rex1", 0, 1, R1["a"].rearrange("p (t e) -> p t e", t=NT))
            v.tensor_tensor(R1["b"], R1["a"], R1["p"], ALU.mult).then_inc(s["rst1"], 1)
            group_norm(0, 2 * NG, xn4)
            group_lo(2 * KC * NG)
            v.wait_ge(s["dps"], 1)
            v.tensor_scalar(rden, ps[:, 6, 0:S], EPS_GATE, None, ALU.add).then_inc(s["tk"], 1)
            v.wait_ge(s["tk"], 1)
            v.reciprocal(rden, rden).then_inc(s["tk"], 1)
            v.wait_ge(s["tk"], 2)
            for j in range(2):
                v.scalar_tensor_tensor(route[:, j, :], route[:, j, :], float(B), rden, ALU.mult, ALU.mult
                                       ).then_inc(s["tk"], 1)
            n = 4
            for r in range(TOP // 8):
                v.wait_ge(s["tk"], n)
                for j in range(2):
                    v.max(top8[:, j, :], route[:, j, :]).then_inc(s["tk"], 1)
                n += 2
                v.wait_ge(s["tk"], n)
                for j in range(2):
                    v.match_replace(route[:, j, :], top8[:, j, :], route[:, j, :], -1.0).then_inc(s["tk"], 1)
                n += 2
            v.wait_ge(s["tk"], n)
            v.tensor_scalar(selb, route, 0.0, None, ALU.is_lt).then_inc(s["sel"], 1)

            v.wait_ge(L["late"], 32)
            v.tensor_copy(b2s[:, 0, :], b2f).then_inc(s["b2"], 1)
            v.wait_ge(s["b2"], 1)
            v.tensor_tensor(b2r[:, 0, :], b2f, b2s[:, 0, :], ALU.subtract).then_inc(s["b2"], 1)
            v.wait_ge(s["b2"], 2)
            v.tensor_copy(b2s[:, 1, :], b2r[:, 0, :]).then_inc(s["b2"], 1)
            v.wait_ge(s["b2"], 3)
            v.tensor_tensor(b2r[:, 1, :], b2r[:, 0, :], b2s[:, 1, :], ALU.subtract).then_inc(s["b2"], 1)
            v.wait_ge(s["b2"], 4)
            v.tensor_copy(b2s[:, 2, :], b2r[:, 1, :]).then_inc(s["b2"], 1)

            def finish(g, steps=range(4)):
                xg = group_of(X, g)
                if 0 in steps:
                    v.tensor_tensor(xg, xg, rows[:, 4, :].unsqueeze(1).to_broadcast([P, GT, D]), ALU.add
                                    ).then_inc(s["zo"], 1)
                if 1 in steps:
                    v.wait_ge(s["zpow"], g + 1)
                    v.wait_ge(s["zmn"], 2 * g + 2)
                    for k in range(GT):
                        i = v.tensor_scalar(z[:, k, :], z[:, k, :], zmean[:, k:k + 1], zrstd[:, k:k + 1],
                                            ALU.subtract, ALU.mult)
                    i.then_inc(s["zn"], 1)
                if 2 in steps:
                    v.wait_ge(s["zn"], 2 * g + 1)
                    v.tensor_tensor(z, z, rows[:, 3, :].unsqueeze(1).to_broadcast([P, GT, D]), ALU.mult
                                    ).then_inc(s["zn"], 1)
                if 3 in steps:
                    v.wait_ge(s["zn"], 2 * g + 2)
                    v.wait_ge(s["zo"], 2 * g + 1)
                    v.tensor_tensor(xg, xg, z, ALU.add).then_inc(s["zo"], 1)

            def feed1(g, buf, first=False, last=False):
                for c in range(C1):
                    if 1 <= c < 5 and not first:
                        finish(g + (-1), (c - 1,))
                    if c == 5 and not last:
                        group_norm(g + 1, g + (2 * NG), (xn4, xn4b)[1 - buf])
                    m = g * C1 + c
                    v.wait_ge(s["gelu"], m + 1)
                    v.wait_ge(s["mps"], m + 1)
                    if counted(m - 1):
                        v.wait_ge(s["hml"], m - 1)
                    v.tensor_tensor(hmf[:, c % 2, :], hgf[:, c % 2, :], bank(2 + c % 2), ALU.mult
                                    ).then_inc(s["hm"], 1)
                    v.wait_ge(s["hmh"], m + 1)
                    v.tensor_tensor(hm[:, c % 2, 1, :], hmf[:, c % 2, :], hm[:, c % 2, 0, :],
                                    ALU.subtract).then_inc(s["hml"], 1)
                if not last:
                    group_lo(KC * g + (2 * KC * NG + KC))
                v.wait_ge(s["yps"], g + 1)
                v.tensor_tensor(z, (xn4, xn4b)[buf], ps[:, 4:8, 0:D], ALU.add).then_inc(s["z"], 1)
                v.wait_ge(s["z"], g + 1)
                for k in range(GT):
                    i = v.bn_stats(zraw[:, k, :], z[:, k, :])
                i.then_inc(s["zbn"], 1)
                v.wait_ge(s["zbn"], g + 1)
                me, qe, mo, qo = zraw[:, :, 1], zraw[:, :, 2], zraw[:, :, 4], zraw[:, :, 5]

                def link(i, k):
                    i.then_inc(s["zst"], 1)
                    v.wait_ge(s["zst"], 5 * g + k)

                link(v.tensor_tensor(zs[:, 0, :], me, mo, ALU.subtract), 1)
                link(v.tensor_tensor(zs[:, 1, :], zs[:, 0, :], zs[:, 0, :], ALU.mult), 2)
                link(v.tensor_tensor(zs[:, 2, :], qe, qo, ALU.add), 3)
                link(v.scalar_tensor_tensor(zs[:, 0, :], zs[:, 1, :], D / 4.0, zs[:, 2, :], ALU.mult, ALU.add), 4)
                v.tensor_tensor(zs[:, 1, :], me, mo, ALU.add).then_inc(s["zmn"], 1)
                link(v.tensor_scalar(zs[:, 3, :], zs[:, 0, :], 1.0 / D, EPS, ALU.mult, ALU.add), 5)
                v.wait_ge(s["zmn"], 2 * g + 1)
                v.tensor_scalar(zmean, zs[:, 1, :], 0.5, None, ALU.mult).then_inc(s["zmn"], 1)

            feed1(0, 0, first=True)
            with v.Fori(0, NG // 2 - 1) as pair:
                for k in range(2):
                    feed1(pair * 2 + (1 + k), 1 - k)
            feed1(NG - 1, 1, last=True)
            finish(NG - 1)

        @block.tensor
        def _(pe):
            def product(dst, terms, mid=False):
                n = 0
                for wpart, xpart in terms:
                    for i, j in PARTS:
                        r = pe.matmul(dst, wpart(i), xpart(j), start=(n == 0),
                                      stop=(not mid and n == 3 * len(terms) - 1))
                        n += 1
                return r

            def cols(w, kc, oc, width=D):
                return w[:, kc * width + oc * P:kc * width + (oc + 1) * P]

            def wa(k, i, kc, oc):
                return cols(wattn[:, k, i, :], kc, oc)

            pe.wait_ge(s["cst"], 3)
            pe.wait_ge(s["wsl"], 2)
            pe.wait_ge(s["csl"], 1)

            def kv(l):
                pe.wait_ge(s["csl"], l + 1)
                for oc in range(KC):
                    for n in range(3):
                        c = oc * 3 + n
                        lo, hi = n * KVN, min(B * SK, (n + 1) * KVN)
                        if c >= 2:
                            pe.wait_ge(s["kl"], 6 * l + c - 1)
                        product(ps[:, c % 2, 0:hi - lo],
                                [(lambda i, kc=kc: wa(1, i, kc, oc),
                                  lambda j, kc=kc: ctxT[:, j, kc, lo:hi]) for kc in range(KC)]).then_inc(s["kps"], 1)
                for b in range(B):
                    if b >= 2:
                        if l == 0:
                            pe.wait_ge(s["vf"], b - 1)
                        else:
                            pe.wait_ge(s["vl"], B * l + b - 1)
                    product(ps[0:SK, 2 + b % 2, 0:D],
                            [(lambda i, kc=kc: ctxT[:, i, kc, b * SK:(b + 1) * SK],
                              lambda j, kc=kc: wattn[:, 2, j, kc * D:(kc + 1) * D]) for kc in range(KC)]
                            ).then_inc(s["vps"], 1)

            def attention(l):
                base = NT * l

                def turn(t, k):
                    pe.wait_ge(s["xn"], t + (base + 1))
                    if counted(t + base):
                        pe.wait_ge(s["ql"], t + base)
                    for kc in range(KC):
                        i = pe.transpose(ps[:, 6, kc * P:(kc + 1) * P], xn_a[:, k % 2, kc * P:(kc + 1) * P], ident)
                    i.then_inc(s["xnTps"], 1)

                def query(t):
                    pe.wait_ge(s["xl"], t + (base + 1))
                    for oc in range(KC):
                        i = product(ps[:, 6, D + oc * P:D + (oc + 1) * P],
                                    [(lambda i, kc=kc: wa(0, i, kc, oc),
                                      lambda j, kc=kc: xnT_a[:, j, kc, :]) for kc in range(KC)])
                    i.then_inc(s["qps"], 1)

                def scores(t, k, b):
                    pe.wait_ge(s["ql"], t + (base + 1))
                    if counted(2 * t + 2 * base):
                        pe.wait_ge(s["sub"], 2 * t + 2 * base)
                    pe.wait_ge(s["kbd"], b + (B * l + 1))
                    for g in range(4):
                        c, r = g // 2, 64 * (g % 2)
                        dst = ps[:, g, 0:HG * SK]
                        i = product(dst, [(lambda i: qT[r:r + 64, i, c, :],
                                           lambda j: Kbd[(k // TB) % 2][r:r + 64, j, c, :])], mid=(l == 0))
                        if l == 0:
                            i = pe.matmul(dst, ones1[:, :],
                                          span(mrow[:, :], b * SK, SK).unsqueeze(1).to_broadcast([1, HG, SK]),
                                          start=False, stop=True)
                    i.then_inc(s["sc"], 1)

                def turn_probs(t, k, g):
                    pe.wait_ge(s["pl"], 2 * t + (2 * base + 1 + g // 2))
                    if counted(4 * t + (4 * base + g - 1)):
                        pe.wait_ge(s["pt"], 4 * t + (4 * base + g - 1))
                    if g == 1:
                        if counted(2 * t + (2 * base - 1)):
                            pe.wait_ge(s["osum"], 2 * t + (2 * base - 1))
                    dst = ps[0:SK, 4 + g % 2, :].bitcast(F16)
                    for part in range(2):
                        for j in range(4):
                            at_ = (part * 4 + j) * P
                            i = pe.transpose(dst[:, at_:at_ + P], Phl[k % 2][:, part, 4 * g + j, :], identh[:, :])
                    i.then_inc(s["ptps"], 1)

                def weigh(t, k, b):
                    if counted(t + base):
                        pe.wait_ge(s["res"], t + base)
                    pe.wait_ge(s["vc"], b + (B * l + 1))
                    pe.wait_ge(s["pt"], 4 * t + (4 * base + 4))
                    for hh in range(H):
                        o, vc = (hh % 8) * 3 * V1, Vc[(k // TB) % 2]
                        bk = 7 if hh < 8 else 5
                        pe.matmul(ps[:, bk, o:o + 3 * V1], PT[:, hh // 4, 0, hh % 4, :],
                                  vc[:, hh].rearrange("s k d -> s (k d)"), start=True, stop=False)
                        i = pe.matmul(ps[:, bk, o:o + 2 * V1], PT[:, hh // 4, 1, hh % 4, :],
                                      vc[:, hh, 0:2].rearrange("s k d -> s (k d)"), start=False, stop=True)
                    i.then_inc(s["pv"], 1)

                def turn_out(t):
                    pe.wait_ge(s["on"], t + (base + 1))
                    for kc in range(KC):
                        i = pe.transpose(ps[:, 7, kc * P:(kc + 1) * P], o_a[:, kc * P:(kc + 1) * P], ident)
                    i.then_inc(s["oTps"], 1)

                def project(t):
                    pe.wait_ge(s["ol"], t + (base + 1))
                    product(ps[:, 7, 0:D], [(lambda i, kc=kc: oT[:, i, kc, :],
                                             lambda j, kc=kc: wattn[:, 3, j, kc * D:(kc + 1) * D])
                                            for kc in range(KC)]).then_inc(s["y"], 1)

                kv(l)
                pe.wait_ge(s["vmk"], 4 if l == 0 else 7)
                pe.wait_ge(s["vp"], B * (l + 1))
                pe.wait_ge(s["vl"], B * (l + 1))
                pe.wait_ge(s["kl"], 6 * (l + 1))
                turn(0, 0)
                query(0)

                def step(t, k, b, bp, n=True, c=True, x=True, w=True):
                    if n:
                        turn(t + 1, k + 1)
                    if x:
                        scores(t, k, b)
                    if c:
                        weigh(t + (-2), (k + 2) % 4, bp)
                    if w:
                        turn_probs(t + (-1), k + 1, 0)
                    if n:
                        query(t + 1)
                    if w:
                        turn_probs(t + (-1), k + 1, 1)
                        turn_probs(t + (-1), k + 1, 2)
                    if c:
                        turn_out(t + (-2))
                    if w:
                        turn_probs(t + (-1), k + 1, 3)
                    if c:
                        project(t + (-2))

                for k in range(4):
                    step(k, k, k // TB, (k - 2) // TB, w=k >= 1, c=k >= 2)
                with pe.Fori(2, (NT - 4) // TB, 2) as b0:
                    for k in range(4):
                        step(b0 * TB + k, k, b0 + k // TB, b0 + (k - 2) // TB)
                for t in range(NT - 4, NT + 2):
                    step(t, t % 4, t // TB, (t - 2) // TB, n=t + 1 < NT, x=t < NT, w=t <= NT)

            def turn_group(n, src, first_bank):
                pe.wait_ge(s["fxn"], n + 1)
                for kc in range(KC):
                    for k in range(GT):
                        i = pe.transpose(ps[:, first_bank + kc, k * P:(k + 1) * P],
                                         src[:, k, kc * P:(kc + 1) * P], ident)
                    i.then_inc(s["fxTps"], 1)

            def logits(bk, w, E, x):
                for k in range(GT):
                    i = product(ps[:, bk, k * E:(k + 1) * E],
                                [(lambda i, kc=kc: x[:, i, kc, k * P:(k + 1) * P], lambda j, kc=kc: w[:, j, kc, :])
                                 for kc in range(KC)])
                return i

            def sum_back(g):
                pe.wait_ge(s["acc"], 2 * E0 * g + 2 * E0)
                pe.wait_ge(s["x23"], 2 * E0 * g + 2 * E0)
                for k in range(GT):
                    for oc in range(KC):
                        i = pe.transpose(ps[:, 4 + k // 2, (k % 2) * D + oc * P:(k % 2) * D + (oc + 1) * P],
                                         yT[:, oc, k * P:(k + 1) * P], ident)
                i.then_inc(s["yps0"], 1)

            def feed0(g, first=False, last=False):
                if counted(2 * E0 * g):
                    pe.wait_ge(s["u"], 2 * E0 * g)
                pe.wait_ge(s["fxl"], KC * g + KC)
                logits(7, gatew, E0, xT).then_inc(s["lps"], 1)
                if first:
                    pe.wait_ge(s["sl"], 1)
                for ic in range(4):
                    if ic == 2 and not first:
                        sum_back(g + (-1))
                    if ic >= 2:
                        pe.wait_ge(s["gG"], 4 * g + ic - 1)
                    elif ic == 1:
                        if counted(2 * E0 * g):
                            pe.wait_ge(s["x3"], 2 * E0 * g)
                    for half in range(2):
                        product(bank(2 * (ic % 2) + half),
                                [(lambda i, kc=kc: cols(sw12[:, half, i, :], kc, ic, I0),
                                  lambda j, kc=kc: xT[:, j, kc, :]) for kc in range(KC)]
                                ).then_inc(s["gA" if half == 0 else "gB"], 1)
                pe.wait_ge(s["sel0"], 5 * g + 5)
                if counted(E0 * g):
                    pe.wait_ge(s["pb"], E0 * g)
                pv = ps[0:3 * E0, 6, 0:GN // 2].bitcast(BF16)
                for k in range(GT):
                    i = pe.transpose(pv[:, k * P:(k + 1) * P], psp[:, k, :], identb[:, :])
                i.then_inc(s["pTps"], 1)

                def up(e):
                    n = g * E0 + e
                    if first:
                        pe.wait_ge(s["wl"], e + 1)
                    if counted(n):
                        pe.wait_ge(s["pb"], n)
                    pe.matmul(bank(6), selp[:, e, :], pT[:, :], start=True, stop=True).then_inc(s["pps"], 1)
                    if counted(2 * n):
                        pe.wait_ge(s["u"], 2 * n)
                    for oc in range(KC):
                        product(bank(oc), [(lambda i, kc=kc: cols(w0[:, e, 0, i, :], kc, oc),
                                            lambda j, kc=kc: xT[:, j, kc, :]) for kc in range(KC)]
                                ).then_inc(s["ups"], 1)

                if first:
                    pe.wait_ge(s["sl"], 2)
                if counted(g):
                    pe.wait_ge(s["fres"], g)
                for ic in range(4):
                    pe.wait_ge(s["gGl"], 4 * g + ic + 1)
                    for oc in range(KC):
                        for i, j in PARTS:
                            r = pe.matmul(bank(4 + oc), cols(sw3[:, i, :], ic, oc), swi[:, j, ic, :],
                                          start=(ic == 0 and (i, j) == PARTS[0]),
                                          stop=(ic == 3 and (i, j) == PARTS[-1]))
                        if ic == 3:
                            r.then_inc(s["zps"], 1)
                pe.wait_ge(s["pTc"], g + 1)
                pe.wait_ge(s["gG"], 4 * g + 4)
                up(0)
                for e in range(E0):
                    n = g * E0 + e
                    if counted(2 * n):
                        pe.wait_ge(s["x3"], 2 * n)
                    for oc in range(KC):
                        product(bank(2 + oc), [(lambda i, kc=kc: cols(w0[:, e, 2, i, :], kc, oc),
                                                lambda j, kc=kc: xT[:, j, kc, :]) for kc in range(KC)]
                                ).then_inc(s["x3ps"], 1)
                    if e + 1 < E0:
                        up(e + 1)
                    elif not last:
                        pe.wait_ge(s["pb"], n + 1)
                        turn_group(g + 1, xn4, 6)
                    pe.wait_ge(s["hl"], 2 * n + 2)
                    if counted(2 * n):
                        pe.wait_ge(s["x23"], 2 * n)
                    if e == 0:
                        pe.wait_ge(s["zcp"], 2 * g + 2)
                    for oc in range(KC):
                        product(bank(4 + oc), [(lambda i, kc=kc: cols(w0[:, e, 1, i, :], kc, oc),
                                                lambda j, kc=kc: h[:, j, kc, :]) for kc in range(KC)]
                                ).then_inc(s["x2ps"], 1)

            attention(0)
            pe.wait_ge(s["rws"], 2)
            turn_group(0, xn4, 6)
            feed0(0, first=True)
            with pe.Fori(1, NG - 1) as g:
                feed0(g)
            feed0(NG - 1, last=True)
            sum_back(NG - 1)
            pe.wait_ge(s["wsl"], 3)
            pe.wait_ge(s["fres"], NG)
            attention(1)

            def turn1(g, k):
                pe.wait_ge(s["fxl"], KC * g + (KC * NG - KC))
                turn_group(g + NG, (xn4, xn4b)[k], 2 * k)

            def logits1(g, k):
                pe.wait_ge(s["fxl"], KC * g + (KC * NG + KC))
                if counted(g + (-1)):
                    pe.wait_ge(s["lgc"], g + (-1))
                logits(6 + k, wg, E1, (xT, xTb)[k]).then_inc(s["lgps"], 1)

            turn1(0, 0)
            turn1(1, 1)
            logits1(0, 0)
            with pe.Fori(0, NG // 2 - 1) as pair:
                for k in range(2):
                    turn1(pair * 2 + (2 + k), k)
                    logits1(pair * 2 + (1 + k), 1 - k)
            logits1(NG - 1, 1)
            pe.wait_ge(s["rst1"], RSTEPS + 2)
            for k in range(NT // 4):
                if counted(k - 1):
                    pe.wait_ge(s["smc"], k - 1)
                for j in range(4):
                    t = 4 * k + j
                    i = pe.transpose(ps[0:E1, 4 + k % 2, j * P:(j + 1) * P], R1["b"][:, t * E1:(t + 1) * E1], ident)
                i.then_inc(s["smps"], 1)
            pe.wait_ge(s["rt"], 16 * B)
            for j in range(2):
                i = pe.matmul(ps[:, 6, 0:S], same_e, route[:, j, :], start=(j == 0), stop=(j == 1))
            i.then_inc(s["dps"], 1)
            turn_group(2 * NG, xn4, 0)
            pe.wait_ge(s["wl"], E0 + 4)
            pe.wait_ge(s["b2"], 5)
            pe.wait_ge(L["late"], 32)
            pe.wait_ge(s["tk"], 1)

            def feed1(g, buf, last=False):
                pe.wait_ge(s["fxl"], KC * g + (2 * KC * NG + KC))
                pe.wait_ge(s["selg"], g + 1)

                def hidden(c, m):
                    if counted(m - 1):
                        pe.wait_ge(s["gelu"], m - 1)
                    product(bank(c % 2), [(lambda i, kc=kc: cols(w1f[:, i, :], kc, c, E1 * F1),
                                           lambda j, kc=kc: xT[:, j, kc, :]) for kc in range(KC)]
                            ).then_inc(s["hps"], 1)
                    if counted(m - 1):
                        pe.wait_ge(s["hm"], m - 1)
                    pe.matmul(bank(2 + c % 2), selh[:, c, :], selg[buf], start=True, stop=True).then_inc(s["mps"], 1)

                def down(c, m):
                    pe.wait_ge(s["hml"], m + 1)
                    if c == 0:
                        if counted(g):
                            pe.wait_ge(s["z"], g)
                    for k in range(GT):
                        for i, j in PARTS:
                            r = pe.matmul(ps[:, 4 + k, 0:D], hm[:, c % 2, i, k * P:(k + 1) * P],
                                          w2f[:, j, c * D:(c + 1) * D], start=(c == 0 and (i, j) == PARTS[0]),
                                          stop=False)
                    r.then_inc(s["hmr"], 1)

                hidden(0, g * C1)
                hidden(1, g * C1 + 1)
                for c in range(C1):
                    if c + 2 < C1:
                        hidden(c + 2, g * C1 + (c + 2))
                    if c == C1 - 2 and not last:
                        pe.wait_ge(s["gelu"], g * C1 + C1)
                        turn_group(g + (2 * NG + 1), (xn4, xn4b)[1 - buf], 0)
                    down(c, g * C1 + c)
                for k in range(GT):
                    for j in range(3):
                        i = pe.matmul(ps[:, 4 + k, 0:D], selg[buf][:, k * P:(k + 1) * P], b2s[:, j, :],
                                      start=False, stop=(j == 2))
                i.then_inc(s["yps"], 1)

            feed1(0, 0)
            with pe.Fori(0, NG // 2 - 1) as pair:
                for k in range(2):
                    feed1(pair * 2 + (1 + k), 1 - k)
            feed1(NG - 1, 1, last=True)


def kernel(**inputs):
    import numpy as np
    import concourse.bacc as _bacc
    from concourse.bass_utils import run_bass_kernel_spmd as _run

    def n(k):
        return np.ascontiguousarray(inputs[k])

    def chunks(w):
        return np.ascontiguousarray(np.moveaxis(w.reshape((w.shape[0] // P, P) + w.shape[1:]), 0, 1))

    f = np.float32
    arrays = {}
    arrays["x"] = np.ascontiguousarray(n("x").reshape(NT, P, D).transpose(1, 0, 2))
    arrays["ctxT"] = chunks(n("ctx_1024").reshape(B * SK, D).T)
    mask = n("mask_BxS2_bf0")
    arrays["mrow"] = mask.reshape(1, B * SK)
    arrays["mcol"] = np.ascontiguousarray(mask.T)
    for l, ks in ((0, ("wq", "wk", "wv", "wo")), (1, ("Wq", "Wk", "Wv", "Wo"))):
        arrays[f"wattn{l}"] = np.ascontiguousarray(
            np.stack([chunks(n(f"L{l}_xattn_{k}").T).reshape(P, KC * D) for k in ks], axis=1))
    vectors = [n("L0_xattn_bv"), n("L0_xattn_bo"), n("L1_xattn_bo"), n("L1_ffn_gamma"), n("L1_ffn_beta"),
               n("L1_ffn_bg"), n("g_xattn"), n("g_ffn")]
    arrays["bc"] = np.concatenate(vectors).reshape(1, BCST)
    w0 = np.stack([chunks(n(f"L0_ffn_{k}").transpose(2, 0, 1)).transpose(0, 2, 1, 3) for k in ("w1", "w2", "w3")],
                  axis=2)
    arrays["feed0"] = w0.reshape(P, E0, 3, KC * D)
    arrays["sw12"] = np.stack([chunks(n("L0_ffn_sw1").T), chunks(n("L0_ffn_sw2").T)], axis=1).reshape(P, 2, KC * I0)
    arrays["sw3"] = chunks(n("L0_ffn_sw3").T).reshape(P, -1)
    arrays["w1f"] = chunks(n("L1_ffn_w1").transpose(1, 0, 2).reshape(D, E1 * F1)).reshape(P, -1)
    arrays["w2f"] = chunks(n("L1_ffn_w2").reshape(E1 * F1, D)).reshape(P, -1)
    arrays["b2f"] = n("L1_ffn_b2")
    r = np.arange(P)
    codes = np.zeros((P, 2, E1), f)
    codes[:, 0, :E0] = E0 - np.arange(E0)
    codes[:, 1, :] = E1 - np.arange(E1)
    bqk = np.stack([n("L0_xattn_bq").reshape(KC, P).T, n("L0_xattn_bk").reshape(KC, P).T], axis=1)
    parts = [np.eye(P, dtype=f), ((r[:, None] % (HG * HD)) // HD == np.arange(HG)).astype(f),
             (r[:, None] % E1 == r % E1).astype(f), codes, bqk,
             n("L1_ffn_b1").reshape(C1, P).T, *(n(f"L0_ffn_{k}").reshape(E0, KC, P).transpose(2, 0, 1)
                                                for k in ("b1", "b2", "b3")),
             chunks(n("L0_ffn_gate_w").T), chunks(n("L1_ffn_wg"))]
    arrays["cst"] = np.concatenate([p.reshape(P, -1) for p in parts], axis=1)
    bf = np.dtype("bfloat16")
    arrays["identh"] = np.eye(P, dtype=np.float16)
    arrays["identb"] = np.eye(P, dtype=f).astype(bf)
    arrays["selp"] = np.repeat(np.tile(np.eye(E0, dtype=f), (3, 1)), P, axis=1).astype(bf).reshape(3 * E0, E0, P)
    arrays["selh"] = np.repeat(np.eye(E1, dtype=f), F1, axis=1).astype(bf).reshape(E1, C1, P)

    nc = _bacc.Bacc("TRN2", target_bir_lowering=False, num_devices=1)
    aps = {}
    ins = {}
    for k, x in arrays.items():
        x = np.ascontiguousarray(x)
        ins[f"in_{k}"] = x
        aps[k] = nc.dram_tensor(f"in_{k}", x.shape, mybir.dt.from_np(x.dtype), kind="ExternalInput").ap()
    out = nc.dram_tensor("out_0", (P, NT, D), F32, kind="ExternalOutput").ap()
    build(nc, aps, out)
    got = _run(nc, [ins], core_ids=[0]).results[0]["out_0"]
    return np.ascontiguousarray(got.reshape(P, NT, D).transpose(1, 0, 2).reshape(B, S, D))
```
